# Optimizing a Trainium2 kernel written in Bass

```python
import numpy as np
import jax
import jax.numpy as jnp

def _softmax(x, axis=-1):
    return jax.nn.softmax(x, axis=axis)

def _gelu(x):
    return jax.nn.gelu(x, approximate=True)

def _silu(x):
    return jax.nn.silu(x)

def _sigmoid(x):
    return jax.nn.sigmoid(x)

def _layernorm(x, axis=-1, eps=1e-05):
    m = jnp.mean(x, axis=axis, keepdims=True)
    v = jnp.var(x, axis=axis, keepdims=True)
    return (x - m) / jnp.sqrt(v + eps)

def _scatter_add(tgt, idx, src, axis=0):
    return tgt.at[idx].add(src)

def _segment_sum(src, seg, n):
    return jax.ops.segment_sum(src, seg, n)
kernel_name = 'mk_early_fusion_d1_tok_img768_r4_6fa731'

def setup_inputs(seed: int=0):
    np.random.seed(seed)
    _w = jnp.asarray

    def _rec_inputs():
        import jax
        import jax.numpy as jnp
        _rk = jax.random.key(seed)
        x = 7.57192e-06 + 1.00007 * jax.random.normal(jax.random.fold_in(_rk, 1), (16, 224, 224, 3), jnp.float32)
        txt = -0.0429142 + 10 * jax.random.normal(jax.random.fold_in(_rk, 2), (16, 128, 192), jnp.float32)
        return (x, txt)
    x, txt = _rec_inputs()

    def _L0_tok_setup():
        import jax, jax.numpy as jnp
        import numpy as np
        PATCH = 16
        DIM = 192
        EPS = 0.001

        def _shifts(x):
            zw = jnp.zeros_like(x[:, :, :1, :])
            right = jnp.concatenate([zw, x[:, :, :-1, :]], axis=2)
            left = jnp.concatenate([x[:, :, 1:, :], zw], axis=2)
            zh = jnp.zeros_like(x[:, :1, :, :])
            down = jnp.concatenate([zh, x[:, :-1, :, :]], axis=1)
            up = jnp.concatenate([x[:, 1:, :, :], zh], axis=1)
            return [right, left, down, up]

        def _patchify(x, p):
            b, H, W, C = x.shape
            hh, ww = (H // p, W // p)
            x = x.reshape(b, hh, p, ww, p, C)
            x = x.transpose(0, 1, 3, 2, 4, 5)
            return x.reshape(b, hh * ww, p * p * C)
        key = jax.random.key(seed)
        k1, k2 = jax.random.split(key)
        b, H, Wd, C = (64, 224, 224, 3)
        F = PATCH * PATCH * 5 * C
        x = jax.random.normal(k1, (b, H, Wd, C), dtype=jnp.float32)
        gamma = jnp.ones((F,), dtype=jnp.float32)
        beta = jnp.zeros((F,), dtype=jnp.float32)
        W = jax.random.normal(k2, (F, DIM), dtype=jnp.float32)
        bb = jnp.zeros((DIM,), dtype=jnp.float32)
        return {'x': x, 'gamma': gamma, 'beta': beta, 'W': W, 'b': bb}
    _L0_tok_all = _L0_tok_setup()
    _L0_tok_in = {k: v for k, v in _L0_tok_all.items() if k in ('gamma', 'beta', 'W', 'b')}
    del _L0_tok_all

    def _L0_attn_setup():
        import jax, jax.numpy as jnp
        import numpy as np
        import math
        LATENT_RANK = 64
        NUM_HEADS = 12
        HEAD_DIM = 64
        key = jax.random.key(seed)
        k1, k2, k3, k4, k5 = jax.random.split(key, 5)
        b, n, h = (8, 256, 192)
        r, nh = (LATENT_RANK, NUM_HEADS)
        std = 0.02
        return {'hidden_states': jax.random.normal(k1, (b, n, h), dtype=jnp.float32), 'basis_w': jax.random.normal(k2, (r, h), dtype=jnp.float32) * std, 'core': jax.random.normal(k3, (r, r), dtype=jnp.float32) * std, 'head_residual': jax.random.normal(k4, (nh, r, r), dtype=jnp.float32) * (std / 10.0), 'value_w': jax.random.normal(k5, (h, h), dtype=jnp.float32) * std, 'value_b': jnp.zeros((h,), dtype=jnp.float32)}
    _L0_attn_all = _L0_attn_setup()
    _L0_attn_in = {k: v for k, v in _L0_attn_all.items() if k in ('basis_w', 'core', 'head_residual', 'value_w', 'value_b')}
    del _L0_attn_all

    def _L0_ffn_setup():
        import jax, jax.numpy as jnp
        import numpy as np
        DECAY = 0.9
        EPS = 0.01
        TOP_K = 2
        key = jax.random.key(seed)
        k1, k2, k3, k4 = jax.random.split(key, 4)
        B, S, H, I, E = (4, 512, 192, 512, 8)
        return {'hidden_states': jax.random.normal(k1, (B, S, H), jnp.float32), 'router_w': jax.random.normal(k2, (E, H), jnp.float32) * 0.02, 'w1': jax.random.normal(k3, (E, I, H), jnp.float32) * 0.02, 'w2': jax.random.normal(k4, (E, H, I), jnp.float32) * 0.02}
    _L0_ffn_all = _L0_ffn_setup()
    _L0_ffn_in = {k: v for k, v in _L0_ffn_all.items() if k in ('router_w', 'w1', 'w2')}
    del _L0_ffn_all
    return {'x': x, 'txt': txt, 'L0_tok_gamma': _L0_tok_in['gamma'], 'L0_tok_beta': _L0_tok_in['beta'], 'L0_tok_W': _L0_tok_in['W'], 'L0_tok_b': _L0_tok_in['b'], 'L0_attn_basis_w': _L0_attn_in['basis_w'], 'L0_attn_core': _L0_attn_in['core'], 'L0_attn_head_residual': _L0_attn_in['head_residual'], 'L0_attn_value_w': _L0_attn_in['value_w'], 'L0_attn_value_b': _L0_attn_in['value_b'], 'L0_ffn_router_w': _L0_ffn_in['router_w'], 'L0_ffn_w1': _L0_ffn_in['w1'], 'L0_ffn_w2': _L0_ffn_in['w2']}

def reference(x, txt, L0_tok_gamma, L0_tok_beta, L0_tok_W, L0_tok_b, L0_attn_basis_w, L0_attn_core, L0_attn_head_residual, L0_attn_value_w, L0_attn_value_b, L0_ffn_router_w, L0_ffn_w1, L0_ffn_w2):
    import jax
    import jax.numpy as jnp

    def _L0_tok_ref(x, gamma, beta, W, b):
        import jax, jax.numpy as jnp
        import numpy as np
        PATCH = 16
        DIM = 192
        EPS = 0.001

        def _shifts(x):
            zw = jnp.zeros_like(x[:, :, :1, :])
            right = jnp.concatenate([zw, x[:, :, :-1, :]], axis=2)
            left = jnp.concatenate([x[:, :, 1:, :], zw], axis=2)
            zh = jnp.zeros_like(x[:, :1, :, :])
            down = jnp.concatenate([zh, x[:, :-1, :, :]], axis=1)
            up = jnp.concatenate([x[:, 1:, :, :], zh], axis=1)
            return [right, left, down, up]

        def _patchify(x, p):
            b, H, W, C = x.shape
            hh, ww = (H // p, W // p)
            x = x.reshape(b, hh, p, ww, p, C)
            x = x.transpose(0, 1, 3, 2, 4, 5)
            return x.reshape(b, hh * ww, p * p * C)
        x5 = jnp.concatenate([x] + _shifts(x), axis=-1)
        tokens = _patchify(x5, PATCH)
        mu = jnp.mean(tokens, axis=-1, keepdims=True)
        var = jnp.mean(jnp.square(tokens - mu), axis=-1, keepdims=True)
        ln = (tokens - mu) * jax.lax.rsqrt(var + EPS) * gamma + beta
        return jnp.einsum('bnf,fd->bnd', ln, W) + b

    def _L0_attn_ref(hidden_states, basis_w, core, head_residual, value_w, value_b):
        import jax, jax.numpy as jnp
        import numpy as np
        import math
        LATENT_RANK = 64
        NUM_HEADS = 12
        HEAD_DIM = 64
        b, n, hidden = hidden_states.shape
        nh, r = (head_residual.shape[0], core.shape[0])
        hd = hidden // nh
        latent = jnp.einsum('bnh,rh->bnr', hidden_states, basis_w)
        centered = head_residual - jnp.mean(head_residual, axis=0, keepdims=True)
        head_mats = core[None, :, :] / float(nh) + centered
        scores = jnp.einsum('bnr,hrs,bms->bhnm', latent, head_mats, latent)
        scores = scores / math.sqrt(float(r))
        probs = jax.nn.softmax(scores, axis=-1)
        v = jnp.einsum('bnh,oh->bno', hidden_states, value_w) + value_b
        v = v.reshape(b, n, nh, hd).transpose(0, 2, 1, 3)
        ctx = jnp.einsum('bhnm,bhmd->bhnd', probs, v)
        ctx = ctx.transpose(0, 2, 1, 3).reshape(b, n, hidden)
        return ctx

    def _L0_ffn_ref(hidden_states, router_w, w1, w2):
        import jax, jax.numpy as jnp
        import numpy as np
        DECAY = 0.9
        EPS = 0.01
        TOP_K = 2
        B, S, H = hidden_states.shape
        E = router_w.shape[0]
        flat = hidden_states.reshape(B * S, H)
        logits = flat @ router_w.T
        probs = jax.nn.softmax(logits, axis=-1)
        topk_probs, topk_idx = jax.lax.top_k(probs, TOP_K)
        importance = jax.lax.stop_gradient(probs).sum(axis=0)
        running = jnp.ones((E,), dtype=flat.dtype)
        blended = running + (1.0 - DECAY) * (importance - running)
        running = blended + EPS
        balance = running[topk_idx]
        balanced = topk_probs / balance
        balanced = balanced / balanced.sum(axis=-1, keepdims=True)
        h = jnp.einsum('th,eih->tei', flat, w1)
        h = jax.nn.silu(h)
        outs = jnp.einsum('tei,ehi->teh', h, w2)
        sel = jnp.take_along_axis(outs, topk_idx[:, :, None], axis=1)
        combined = (sel * balanced[..., None]).sum(axis=1)
        return combined.reshape(B, S, H)
    h = _L0_tok_ref(x, L0_tok_gamma, L0_tok_beta, L0_tok_W, L0_tok_b)
    h = jnp.concatenate([h, txt], axis=1)
    h = h + _L0_attn_ref(_layernorm(h, axis=-1), L0_attn_basis_w, L0_attn_core, L0_attn_head_residual, L0_attn_value_w, L0_attn_value_b)
    h = h + _L0_ffn_ref(_layernorm(h, axis=-1), L0_ffn_router_w, L0_ffn_w1, L0_ffn_w2)
    return h

_drawn_inputs = setup_inputs


def setup_inputs(seed=0):
    import zlib

    import numpy as np

    out = dict(_drawn_inputs(seed))
    spreads = {'L0_tok_gamma': (1.0, 0.2),
     'L0_tok_beta': (0.0, 0.1),
     'L0_tok_b': (0.0, 2.0),
     'L0_attn_value_b': (0.0, 2.0)}
    factors = {'L0_attn_basis_w': 64.0,
     'L0_attn_core': 64.0,
     'L0_attn_head_residual': 64.0,
     'L0_attn_value_w': 61.31,
     'L0_ffn_router_w': 8.0,
     'L0_ffn_w1': 8.0,
     'L0_ffn_w2': 8.0}
    for name, (base, spread) in spreads.items():
        noise = np.random.default_rng([zlib.crc32(name.encode()), seed]).standard_normal(out[name].shape)
        drawn = base * np.exp(spread * noise) if base else spread * noise
        out[name] = jnp.asarray(drawn.astype(out[name].dtype))
    for name, factor in factors.items():
        out[name] = (out[name] * factor).astype(out[name].dtype)
    return out
```

```python
from contextlib import ExitStack

import concourse.bass as bass
from concourse import mybir

F32 = mybir.dt.float32
F32R = mybir.dt.float32r
I32 = mybir.dt.int32
BF16 = mybir.dt.bfloat16
ALU = mybir.AluOpType
ACT = mybir.ActivationFunctionType
AX = mybir.AxisListType.X

IMAGES, SIDE, CH = 16, 224, 3
TEXT, DIM = 128, 192
PATCH = 16
GRID = SIDE // PATCH
SHIFTS = 5
FEATURES = PATCH * PATCH * SHIFTS * CH
TOK_EPS = 0.001

HALO = PATCH + 2
WIN = HALO * CH
BATCH_IMAGES = 8
BATCHES = IMAGES // BATCH_IMAGES
ROWP = BATCH_IMAGES * GRID
LINE = SIDE * CH
PADLINE = LINE + 2 * CH
CHUNK = 2 * WIN
CHUNKS = HALO // 2
TGROUP = 3
WROWS = FEATURES // 128

TILE_COLS = GRID // 2
PTILE = TILE_COLS * GRID
N = GRID * GRID + TEXT
SLOTS = 2
STEPS = BATCHES * GRID


def tokenize(nc, x, gamma, beta, W, b, gw_dram, h_dram):
    with ExitStack() as ctx:
        def sb(name, shape, dt=F32):
            return ctx.enter_context(nc.sbuf_tensor(name, shape, dt))

        def psum(name, shape, dt=F32):
            return ctx.enter_context(nc.psum_tensor(name, shape, dt))

        def sem(name):
            return ctx.enter_context(nc.semaphore(name))

        lines = sb("lines", [ROWP, BATCHES, HALO, PADLINE])
        w_shift = lines[0:CHUNK, BATCHES - 1, :, :].rearrange("p r l -> p (r l)")[:, 0:SHIFTS * CHUNKS * DIM] \
            .rearrange("p (s t d) -> p s t d", s=SHIFTS, t=CHUNKS)
        w_raw = sb("w_raw", [128, WROWS, DIM])
        w_scaled = sb("w_scaled", [128, WROWS, DIM])
        gamma_sb = sb("gamma_sb", [128, WROWS])
        beta_sb = sb("beta_sb", [128, WROWS])
        b_row = sb("b_row", [ROWP, DIM])
        bias = sb("bias", [ROWP, DIM])
        w_sum = w_raw[0:CHUNK, 0:CHUNKS, :]
        w_hi = sb("w_hi", [CHUNK, CHUNKS, DIM], F32R)
        w_lo = sb("w_lo", [CHUNK, CHUNKS, DIM], F32R)
        count = sb("count", [ROWP, HALO, CH, HALO])
        count_flat = count[:, :, :, :].rearrange("p r c q -> p (r c q)")
        ident = sb("ident0", [128, 128])
        eps = sb("eps0", [128, 1])
        win = sb("win", [ROWP, SLOTS, HALO * WIN])
        norm = sb("norm", [ROWP, SLOTS, HALO * WIN])
        square = sb("square", [ROWP, HALO * WIN])
        negmean = sb("negmean", [ROWP, SLOTS])
        var = sb("var", [ROWP, SLOTS])
        logvar = sb("logvar", [ROWP, SLOTS])
        rstd = sb("rstd", [ROWP, SLOTS])
        shift = sb("shift", [ROWP, SLOTS])
        winT_hi = sb("winT_hi", [CHUNK, SLOTS, CHUNKS, ROWP], F32R)
        winT_lo = sb("winT_lo", [CHUNK, SLOTS, CHUNKS, ROWP], F32R)
        tok = sb("tok", [ROWP, SLOTS, DIM])
        psT = psum("psT", [CHUNK, SLOTS, CHUNKS // TGROUP, 512])
        psO = psum("psO", [ROWP, SLOTS, 512])

        lines_clear = sem("lines_clear")
        shift_clear = sem("shift_clear")
        consts = sem("consts")
        const_step = sem("const_step")
        lines_in = [sem(f"lines_in{i}") for i in range(BATCHES)]
        w_in = sem("w_in")
        g_in = sem("g_in")
        gw_ready = sem("gw_ready")
        gw_out = sem("gw_out")
        shift_in = sem("shift_in")
        w_summed = sem("w_summed")
        w_hi_ready = sem("w_hi_ready")
        w_lo_ready = sem("w_lo_ready")
        bias_mm = sem("bias_mm")
        bias_ready = sem("bias_ready")
        win_ready = sem("win_ready")
        mean_ready = sem("mean_ready")
        square_ready = sem("square_ready")
        var_ready = sem("var_ready")
        act_step = sem("act_step")
        norm_ready = sem("norm_ready")
        turned = sem("turned")
        hi_ready = sem("hi_ready")
        lo_ready = sem("lo_ready")
        projected = sem("projected")
        tok_ready = sem("tok_ready")
        tok_out = [sem(f"tok_out{i}") for i in range(SLOTS)]

        def done(step):
            return step + SLOTS + 1

        def free(step):
            return step + 1

        block = ctx.enter_context(nc.Block())

        def load_lines(q, bi):
            i0 = bi * BATCH_IMAGES
            own = x[i0:i0 + BATCH_IMAGES].rearrange("i (g r) w c -> (i g) r (w c)", r=PATCH)
            for r0 in range(0, PATCH, 4):
                q.dma_start(lines[:, bi, 1 + r0:5 + r0, CH:CH + LINE], own[:, r0:r0 + 4, :]) \
                    .then_inc(lines_in[bi], 16)
            for i in range(BATCH_IMAGES):
                rows = x[i0 + i].rearrange("(g r) w c -> g r (w c)", r=PATCH)
                p = i * GRID
                q.dma_start(lines[p + 1:p + GRID, bi, 0, CH:CH + LINE], rows[0:GRID - 1, PATCH - 1, :]) \
                    .then_inc(lines_in[bi], 16)
                q.dma_start(lines[p:p + GRID - 1, bi, HALO - 1, CH:CH + LINE], rows[1:GRID, 0, :]) \
                    .then_inc(lines_in[bi], 16)

        LINES_LANDED = 16 * (4 + 2 * BATCH_IMAGES)
        CLEARS = 3

        SOURCE = [(1, 1), (1, 0), (1, 2), (0, 1), (2, 1)]
        gw5 = gw_dram.rearrange("(h w s c) d -> h w s c d", h=PATCH, w=PATCH, s=SHIFTS)

        def load_shifted(q, shifts):
            for s in shifts:
                dr, dc = SOURCE[s]
                for odd in range(2):
                    t0 = (dr - odd + 1) // 2
                    h0 = 2 * t0 + odd - dr
                    for c in range(CH):
                        p = (odd * CH + c) * HALO + dc
                        q.dma_start(w_shift[p:p + PATCH, s, t0:t0 + PATCH // 2, :],
                                    gw5[h0:PATCH:2, :, s, c, :].rearrange("t w d -> w t d")) \
                            .then_inc(shift_in, 16)

        SHIFTED_LANDED = 16 * SHIFTS * 2 * CH

        @block.sync
        def _(sp):
            for u in range(SLOTS):
                sp.nop(nofuse=True).then_inc(tok_out[u], 16)
            sp.dma_start(w_raw[:, :, :], W.rearrange("(p j) d -> p j d", j=WROWS)).then_inc(w_in, 16)
            sp.wait_ge(lines_clear, CLEARS)
            load_lines(sp, 0)
            sp.wait_ge(gw_ready, 1)
            sp.dma_start(gw_dram.rearrange("(p j) d -> p j d", j=WROWS), w_scaled[:, :, :]).then_inc(gw_out, 16)
            sp.wait_ge(gw_out, 16)
            sp.wait_ge(shift_clear, 1)
            load_shifted(sp, range(0, SHIFTS, 2))
            sp.wait_ge(lines_clear, 2 * CLEARS)
            load_lines(sp, 1)
            for bi in range(BATCHES):
                with sp.Fori(0, GRID // SLOTS) as i:
                    for u in range(SLOTS):
                        column = i * SLOTS + u
                        out = h_dram[bi * BATCH_IMAGES:(bi + 1) * BATCH_IMAGES, bass.ds(column * GRID, GRID), :]
                        sp.wait_ge(tok_ready, done(bi * GRID + column))
                        sp.dma_start(out, tok[:, u, :]).then_inc(tok_out[u], 16)
            for u in range(SLOTS):
                sp.wait_ge(tok_out[u], 16 * (STEPS // SLOTS) + 16)

        @block.gpsimd
        def _(pool):
            def clear(bi):
                pool.memset(lines[:, bi, 0:HALO:HALO - 1, :], 0.0).then_inc(lines_clear, 1)
                pool.memset(lines[:, bi, 1:HALO - 1, 0:CH], 0.0).then_inc(lines_clear, 1)
                pool.memset(lines[:, bi, 1:HALO - 1, PADLINE - CH:PADLINE], 0.0).then_inc(lines_clear, 1)

            clear(0)
            pool.memset(eps[:, :], TOK_EPS).then_inc(consts, 1)
            pool.memset(ident[:, :], 0.0).then_inc(const_step, 1)
            pool.wait_ge(const_step, 1)
            pool.affine_select(out=ident[:, :], in_=ident[:, :], compare_op=ALU.not_equal, fill=1.0,
                               base=0, pattern=[[-1, 128]], channel_multiplier=1).then_inc(consts, 1)
            end = PATCH + 1
            regions = [((0, HALO), (0, HALO), 0.0), ((1, end), (0, HALO), 1.0), ((0, HALO), (1, end), 1.0),
                       ((1, end), (1, end), 4.0), ((2, end - 1), (2, end - 1), 5.0),
                       ((1, 2), (1, 2), 3.0), ((1, 2), (end - 1, end), 3.0),
                       ((end - 1, end), (1, 2), 3.0), ((end - 1, end), (end - 1, end), 3.0)]
            for n, (r, q, v) in enumerate(regions):
                pool.wait_ge(const_step, 1 + n)
                last = n == len(regions) - 1
                pool.memset(count[:, r[0]:r[1], :, q[0]:q[1]], v).then_inc(consts if last else const_step, 1)

            def windows(bi):
                pool.wait_ge(lines_in[bi], LINES_LANDED)
                with pool.Fori(0, GRID // SLOTS) as i:
                    for u in range(SLOTS):
                        column = i * SLOTS + u
                        pool.wait_ge(norm_ready, free(bi * GRID + column))
                        pool.nop(nofuse=True)
                        src = lines[:, bi, :, bass.ds(column * (PATCH * CH), WIN)]
                        pool.tensor_copy(win[:, u, :].rearrange("p (r c q) -> p r c q", r=HALO, c=CH),
                                         src.rearrange("p r (q c) -> p r c q", c=CH)).then_inc(win_ready, 1)

            pool.wait_ge(w_summed, SHIFTS - 1)
            clear(1)
            windows(0)
            windows(1)

        @block.scalar
        def _(act):
            act.preload_act_table_set("natural_log_exp_and_others")
            act.nop(nofuse=True).then_inc(norm_ready, SLOTS)
            act.dma_start(gamma_sb[:, :], gamma.rearrange("(p j) -> p j", j=WROWS)).then_inc(g_in, 16)
            act.dma_start(beta_sb[:, :], beta.rearrange("(p j) -> p j", j=WROWS)).then_inc(g_in, 16)
            act.dma_start(b_row[:, :], b.rearrange("(a d) -> a d", a=1).to_broadcast([ROWP, DIM])).then_inc(g_in, 16)
            act.wait_ge(gw_out, 16)
            act.wait_ge(shift_clear, 1)
            load_shifted(act, range(1, SHIFTS, 2))
            act.wait_ge(w_summed, SHIFTS - 1)
            act.activation(w_hi[:, :, :], w_sum, ACT.Copy).then_inc(w_hi_ready, 1)
            act.wait_ge(consts, 3)

            def normalise(s, u):
                act.wait_ge(mean_ready, s + 1)
                act.activation(square[:, :], win[:, u, :], ACT.Square, bias=negmean[:, u:u + 1]).then_inc(square_ready, 1)
                act.wait_ge(var_ready, s + 1)
                act.activation(logvar[:, u:u + 1], var[:, u:u + 1], ACT.Ln, bias=eps[0:ROWP, :]).then_inc(act_step, 1)
                act.wait_ge(act_step, s * 3 + 1)
                act.activation(rstd[:, u:u + 1], logvar[:, u:u + 1], ACT.Exp, scale=-0.5).then_inc(act_step, 1)
                act.wait_ge(act_step, s * 3 + 2)
                act.activation(shift[:, u:u + 1], negmean[:, u:u + 1], ACT.Copy, scale=rstd[:, u:u + 1]).then_inc(act_step, 1)
                act.wait_ge(act_step, s * 3 + 3)
                act.activation(norm[:, u, :], win[:, u, :], ACT.Identity, bias=shift[:, u:u + 1],
                               scale=rstd[:, u:u + 1]).then_inc(norm_ready, 1)

            def split_hi(s, u):
                act.wait_ge(projected, free(s))
                act.wait_ge(turned, done(s))
                act.activation(winT_hi[:, u, :, :].rearrange("k (g t) p -> k g (t p)", t=TGROUP),
                               psT[:, u, :, 0:TGROUP * ROWP], ACT.Copy).then_inc(hi_ready, 1)

            normalise(0, 0)
            with act.Fori(0, STEPS // SLOTS - 1) as i:
                for u in range(SLOTS):
                    s = i * SLOTS + u
                    normalise(s + 1, (u + 1) % SLOTS)
                    split_hi(s, u)
            normalise(STEPS - 1, 1)
            split_hi(STEPS - 2, 0)
            split_hi(STEPS - 1, 1)

        @block.vector
        def _(dve):
            dve.memset(w_shift, 0.0).then_inc(shift_clear, 1)
            dve.nop(nofuse=True).then_inc(lo_ready, SLOTS)
            dve.nop(nofuse=True).then_inc(tok_ready, SLOTS)
            dve.wait_ge(w_in, 16)
            dve.wait_ge(g_in, 48)
            dve.tensor_tensor(w_scaled[:, :, :], w_raw[:, :, :],
                              gamma_sb[:, :].rearrange("p (j a) -> p j a", a=1).to_broadcast([128, WROWS, DIM]),
                              ALU.mult).then_inc(gw_ready, 1)
            dve.wait_ge(bias_mm, 1)
            dve.tensor_tensor(bias[:, :], psO[:, 0, 0:DIM], b_row[:, :], ALU.add).then_inc(bias_ready, 1)
            dve.wait_ge(shift_in, SHIFTED_LANDED)
            for s in range(1, SHIFTS):
                first = w_shift[:, 0, :, :] if s == 1 else w_sum
                if s > 1:
                    dve.wait_ge(w_summed, s - 1)
                dve.tensor_tensor(w_sum, first, w_shift[:, s, :, :], ALU.add).then_inc(w_summed, 1)
            dve.wait_ge(w_hi_ready, 1)
            dve.tensor_tensor(w_lo[:, :, :], w_sum, w_hi[:, :, :].bitcast(F32), ALU.subtract).then_inc(w_lo_ready, 1)
            dve.wait_ge(consts, 3)

            def statistics(s, u):
                dve.wait_ge(win_ready, s + 1)
                dve.wait_ge(turned, free(s))
                dve.tensor_tensor_reduce(norm[:, u, :], win[:, u, :], count_flat, -1.0 / FEATURES, 0.0,
                                         ALU.mult, ALU.add, negmean[:, u:u + 1]).then_inc(mean_ready, 1)
                dve.wait_ge(square_ready, s + 1)
                dve.tensor_tensor_reduce(square[:, :], square[:, :], count_flat, 1.0 / FEATURES, 0.0,
                                         ALU.mult, ALU.add, var[:, u:u + 1]).then_inc(var_ready, 1)

            def split_lo(s, u):
                dve.wait_ge(hi_ready, s + 1)
                dve.tensor_tensor(winT_lo[:, u, :, :].rearrange("k (g t) p -> k g (t p)", t=TGROUP),
                                  psT[:, u, :, 0:TGROUP * ROWP],
                                  winT_hi[:, u, :, :].rearrange("k (g t) p -> k g (t p)", t=TGROUP).bitcast(F32),
                                  ALU.subtract).then_inc(lo_ready, 1)

            def add_bias(s, u):
                dve.wait_ge(tok_out[u], (s // SLOTS) * 16 + 16 if isinstance(s, int) else (s - u) * (16 // SLOTS) + 16)
                dve.wait_ge(projected, done(s))
                dve.tensor_tensor(tok[:, u, :], psO[:, u, 0:DIM], bias[:, :], ALU.add).then_inc(tok_ready, 1)

            dve.wait_ge(bias_ready, 1)
            statistics(0, 0)
            statistics(1, 1)
            split_lo(0, 0)
            with dve.Fori(0, STEPS // SLOTS - 1) as i:
                for u in range(SLOTS):
                    s = i * SLOTS + u
                    statistics(s + 2, u)
                    split_lo(s + 1, (u + 1) % SLOTS)
                    add_bias(s, u)
            split_lo(STEPS - 1, 1)
            add_bias(STEPS - 2, 0)
            add_bias(STEPS - 1, 1)

        @block.tensor
        def _(pe):
            pe.nop(nofuse=True).then_inc(turned, SLOTS)
            pe.nop(nofuse=True).then_inc(projected, SLOTS)
            pe.wait_ge(w_in, 16)
            pe.wait_ge(g_in, 48)
            for j in range(WROWS):
                mm = pe.matmul(psO[:, 0, 0:DIM], beta_sb[:, j:j + 1].to_broadcast([128, ROWP]), w_raw[:, j, :],
                               start=(j == 0), stop=(j == WROWS - 1))
            mm.then_inc(bias_mm, 1)
            pe.wait_ge(consts, 3)

            def turn(s, u):
                pe.wait_ge(lo_ready, free(s))
                pe.wait_ge(norm_ready, done(s))
                for t in range(CHUNKS):
                    g, k = t // TGROUP, t % TGROUP
                    mm = pe.transpose(psT[:, u, g, k * ROWP:(k + 1) * ROWP],
                                      norm[:, u, t * CHUNK:(t + 1) * CHUNK], ident[0:ROWP, 0:ROWP])
                mm.then_inc(turned, 1)

            def project(s, u):
                pe.wait_ge(tok_ready, free(s))
                pe.wait_ge(lo_ready, done(s))
                for t in range(CHUNKS):
                    hi, lo = winT_hi[:, u, t, :], winT_lo[:, u, t, :]
                    pe.matmul(psO[:, u, 0:DIM], lo, w_hi[:, t, :], start=(t == 0), stop=False)
                    pe.matmul(psO[:, u, 0:DIM], hi, w_lo[:, t, :], start=False, stop=False)
                    mm = pe.matmul(psO[:, u, 0:DIM], hi, w_hi[:, t, :], start=False, stop=(t == CHUNKS - 1))
                mm.then_inc(projected, 1)

            turn(0, 0)
            pe.wait_ge(w_lo_ready, 1)
            pe.wait_ge(bias_ready, 1)
            with pe.Fori(0, STEPS // SLOTS - 1) as i:
                for u in range(SLOTS):
                    s = i * SLOTS + u
                    turn(s + 1, (u + 1) % SLOTS)
                    project(s, u)
            turn(STEPS - 1, 1)
            project(STEPS - 2, 0)
            project(STEPS - 1, 1)


HEADS, RANK = 12, 64
HEAD_DIM = DIM // HEADS
LN_EPS = 1e-5
HALF = DIM // 2
NTILES = 3
TILE_ROWS = [PTILE, PTILE, TEXT]
TILE_AT = [0, PTILE, 2 * PTILE]
KEYS = N // 3
GROUP = 4
GROUPS = HEADS // GROUP
SCORE_SCALE = RANK ** -0.5
BANK = 512
LN_AT, TURN_AT = 5, 6
POST_SCALE, POST_TURN, POST_ROUTE, POST_RANK = 0, 2, 5, 8
POST_PARTS = (4, 6, 9)
EXPERTS, HIDDEN, TOPK = 8, 512, 2
TOKENS = IMAGES * N
ROW = DIM + 1
SPACE = -(-(TOKENS + 127) // 128) * 128
BLOCKS = (TOPK * TOKENS + EXPERTS * 127) // 128
SPARE = BLOCKS - -(-TOPK * TOKENS // 128)
MASKED = -3e38
PIECES = [(c, max(a, c * N), min(a + BANK, (c + 1) * N))
          for a in (0, BANK) for c in range(3) if max(a, c * N) < min(a + BANK, (c + 1) * N)]


def attention(nc, txt, basis_w, core, head_residual, value_w, value_b, router_w, h_dram, h2_dram, rows_dram, kept):
    picks, pick_probs, places, importance = kept
    with ExitStack() as ctx:
        def sb(name, shape, dt=F32):
            return ctx.enter_context(nc.sbuf_tensor(name, shape, dt))

        def psum(name, shape, dt=F32):
            return ctx.enter_context(nc.psum_tensor(name, shape, dt))

        def sem(name):
            return ctx.enter_context(nc.semaphore(name))

        ident = sb("identA", [128, 128])
        eps = sb("epsA", [128, 1])
        basis_raw = sb("basis_raw", [RANK, DIM])
        basisT = sb("basisT", [HALF, 2, 2, RANK])
        value_raw = sb("value_raw", [HALF, 2, DIM])
        valueT = sb("valueT", [HALF, 2, DIM])
        value_bias = sb("value_bias", [KEYS, DIM])
        residual = sb("residual", [128, HEADS, RANK])
        core_sb = sb("core_sb", [128, RANK])
        mean_mat = sb("mean_mat", [128, RANK])
        mats_hi = sb("mats_hi", [128, HEADS, 2, RANK], F32R)
        mats_lo = sb("mats_lo", [128, HEADS, 2, RANK], F32R)

        h_front = sb("h_front", [128, 2, NTILES, DIM])
        h_back = sb("h_back", [128, 2, NTILES, DIM])
        stats = sb("stats", [128, NTILES, 6])
        moments = sb("moments", [128, NTILES, 2])
        logvar = sb("logvarA", [128, NTILES])
        rstd = sb("rstdA", [128, NTILES])
        newton = sb("newton", [128, 3, NTILES])
        xn = sb("xn", [128, NTILES, DIM])
        xT = sb("xT", [HALF, 2, N])
        lat = sb("lat", [128, 2, N], F32R)
        lat_one = sb("lat_one", [RANK + 1, 2, N], F32R)
        values = sb("values", [KEYS, 2, 3, HEADS, 32])
        q_hi = sb("q_hi", [128, 2, HEADS, N], F32R)
        q_lo = sb("q_lo", [RANK + 1, 2, HEADS, N], F32R)
        row_max = sb("row_max", [KEYS, 2, 3, HEADS])
        max_rows = sb("max_rows", [HEADS, N], F32R)
        probs = sb("probs", [KEYS, 2 * GROUP, 3 * N])
        ctx_sb = sb("ctx_sb", [128, N])
        recip = sb("recip", [128, NTILES, GROUP, 1])
        scaled = sb("scaled", [128, NTILES, GROUP, HEAD_DIM])

        router_raw = sb("router_raw", [EXPERTS, DIM])
        routerT = sb("routerT", [HALF, 2, EXPERTS])
        before = sb("before", [128, 128], BF16)
        all_ones = sb("all_ones", [128, 128], BF16)
        valid = sb("valid", [128, NTILES])
        order_int = sb("order_int", [128, EXPERTS + TOPK * NTILES], I32)
        order = sb("order", [128, EXPERTS])
        goal = sb("goal", [128, TOPK, NTILES, 1])
        newton2 = sb("newton2", [128, 3, NTILES])
        stats2 = sb("stats2", [128, NTILES, 6])
        moments2 = sb("moments2", [128, NTILES, 2])
        logvar2 = sb("logvar2", [128, NTILES])
        rstd2 = sb("rstd2", [128, NTILES])
        routed = sb("routed", [128, TOPK, NTILES, ROW])
        x2T = sb("x2T", [HALF, 2, N])
        logits = sb("logits", [128, NTILES, EXPERTS])
        rest = sb("rest", [128, NTILES, EXPERTS])
        key = sb("key", [128, NTILES, EXPERTS])
        top = sb("top", [128, NTILES])
        expo = sb("expo", [128, NTILES, EXPERTS])
        total = sb("total", [128, NTILES])
        pick = sb("pick", [128, NTILES, TOPK, EXPERTS])
        picked = sb("picked", [128, NTILES, EXPERTS], BF16)
        of_pick = sb("of_pick", [128, NTILES, TOPK, EXPERTS])
        place = sb("place", [128, NTILES, TOPK])
        place_int = sb("place_int", [128, NTILES, TOPK], I32)

        ps_s = psum("ps_s", [128, 2 * BANK])
        ps_t = psum("ps_t", [128, 2 * BANK])
        ps_q = psum("ps_q", [128, BANK])
        ps_v = psum("ps_v", [128, BANK])
        ps_m = psum("ps_m", [128, 2, BANK])

        one_row = sem("one_row")
        w_in, txt_const, const_step, consts = sem("w_inA"), sem("txt_const"), sem("const_stepA"), sem("constsA")
        w_turned, w_ready, mat_step = sem("w_turned"), sem("w_readyA"), sem("mat_step")
        front_in = [sem(f"front_in{i}") for i in range(2)]
        back_in = [sem(f"back_in{i}") for i in range(2)]
        max_in = [sem(f"max_in{i}") for i in range(2)]
        h2_out = [sem(f"h2_out{i}") for i in range(2)]
        dve_ln = sem("dve_ln")
        act_ln = sem("act_ln")
        refined = sem("refined")
        xn_ready = sem("xn_ready")
        x_turned = sem("x_turned")
        xT_ready = sem("xT_ready")
        lat_mm = sem("lat_mm")
        lat_hi = sem("lat_hi")
        lat_lo = sem("lat_lo")
        lat_one_ready = sem("lat_one_ready")
        v_mm = sem("v_mm")
        v_ready = sem("v_ready")
        q_mm = sem("q_mm")
        q_hi_ready = sem("q_hi_ready")
        q_lo_ready = sem("q_lo_ready")
        s_mm = sem("s_mm")
        max_ready = sem("max_ready")
        max_turned = sem("max_turned")
        max_rows_ready = sem("max_rows_ready")
        t_mm = sem("t_mm")
        probs_ready = sem("probs_ready")
        pv_mm = sem("pv_mm")
        ctx_ready = sem("ctx_ready")
        ctx_turned = sem("ctx_turned")
        recip_ready = sem("recip_ready")
        scaled_ready = sem("scaled_ready")
        h2_ready = sem("h2_ready")

        dve_ln2 = sem("dve_ln2")
        act_ln2 = sem("act_ln2")
        refined2 = sem("refined2")
        x2_ready = sem("x2_ready")
        x2_copied = sem("x2_copied")
        x2_turned = sem("x2_turned")
        x2T_ready = sem("x2T_ready")
        logit_mm = sem("logit_mm")
        route = sem("route")
        expo_ready = sem("expo_ready")
        rank_mm = sem("rank_mm")
        scattered = sem("scattered")
        order_in = sem("order_in")
        order_ready = sem("order_ready")

        block = ctx.enter_context(nc.Block())

        PARTS = [(0, 2, PTILE), (2, 3, TEXT)]

        def run(engine, prologue, body, epilogue):
            prologue()
            body(0, 0, True, True, False)
            body(1, 1, True, True, True)
            with engine.Fori(1, (IMAGES - 2) // 2) as it:
                for p in range(2):
                    body(it * 2 + p, p, True, True, True)
            body(IMAGES - 2, 0, True, False, True)
            body(IMAGES - 1, 1, False, False, True)
            epilogue()

        LOGITS_READ, MAX_TAKEN, PICKED, RANKED, ROUTE_STEPS = 1, 3, 15, 25, 28

        def of_pair(i, p, each):
            return (i // 2 + 1) * each if isinstance(i, int) else (i - p) * (each // 2) + each

        @block.sync
        def _(sp):
            sp.dma_start(basis_raw[:, :], basis_w).then_inc(w_in, 16)
            for d in range(2):
                sp.dma_start(residual[d * RANK:(d + 1) * RANK, :, :], head_residual.rearrange("h r s -> r h s")).then_inc(w_in, 16)
                sp.dma_start(core_sb[d * RANK:(d + 1) * RANK, :], core).then_inc(w_in, 16)
            sp.dma_start(value_raw[:, :, :], value_w.rearrange("(k p) h -> p k h", k=2)).then_inc(w_in, 16)
            sp.dma_start(value_bias[:, :], value_b.rearrange("(a d) -> a d", a=1).to_broadcast([KEYS, DIM])).then_inc(w_in, 16)
            sp.dma_start(router_raw[:, :], router_w).then_inc(w_in, 16)
            sp.wait_ge(consts, 5)

            def load(dst, i, p, landed):
                sp.dma_start(dst[0:PTILE, p, 0:2, :],
                             h_dram[bass.ds(i, 1), 0:2 * PTILE, :].rearrange("a (t p) d -> p (a t) d", t=2)).then_inc(landed[p], 16)
                sp.dma_start(dst[:, p, 2, :], txt[bass.ds(i, 1), :, :].rearrange("a p d -> (a p) d")).then_inc(landed[p], 16)

            def prologue():
                for i in range(2):
                    load(h_front, i, i, front_in)
                    load(h_back, i, i, back_in)

            def body(i, p, front, prep, post):
                if post and front:
                    sp.wait_ge(x2_ready, 3 * i)
                    sp.wait_ge(h2_out[1 - p], of_pair(i - 1, 1 - p, 32))
                    load(h_back, i + 1, 1 - p, back_in)
                if prep:
                    sp.wait_ge(xn_ready, 3 * (i + 1))
                    load(h_front, i + 2, p, front_in)
                if front:
                    sp.wait_ge(max_rows_ready, i + 2)
                    sp.dma_start(q_lo[RANK:RANK + 1, 1 - p, :, :].bitcast(F32), max_rows[:, :].bitcast(F32)).then_inc(max_in[1 - p], 16)
                sp.wait_ge(h2_ready, 2 * GROUPS * (i + 1))
                sp.dma_start(h2_dram[bass.ds(i, 1), 0:2 * PTILE, :].rearrange("a (t p) d -> p (a t) d", t=2),
                             h_back[0:PTILE, p, 0:2, :]).then_inc(h2_out[p], 16)
                sp.dma_start(h2_dram[bass.ds(i, 1), 2 * PTILE:N, :].rearrange("a p d -> (a p) d"), h_back[:, p, 2, :]).then_inc(h2_out[p], 16)

            def first_max():
                sp.wait_ge(max_rows_ready, 1)
                sp.dma_start(q_lo[RANK:RANK + 1, 0, :, :].bitcast(F32), max_rows[:, :].bitcast(F32)).then_inc(max_in[0], 16)

            def prologue2():
                prologue()
                first_max()

            def epilogue():
                for p in range(2):
                    sp.wait_ge(h2_out[p], 32 * IMAGES // 2)

            run(sp, prologue2, body, epilogue)

        @block.gpsimd
        def _(pool):
            pool.memset(ident[:, :], 0.0).then_inc(const_step, 1)
            pool.memset(eps[:, :], LN_EPS).then_inc(consts, 1)
            pool.wait_ge(const_step, 1)
            pool.affine_select(out=ident[:, :], in_=ident[:, :], compare_op=ALU.not_equal, fill=1.0,
                               base=0, pattern=[[-1, 128]], channel_multiplier=1).then_inc(consts, 1)
            pool.memset(h_front[:, :, :, :], 0.0).then_inc(consts, 1)
            pool.memset(h_back[:, :, :, :], 0.0).then_inc(consts, 1)
            pool.memset(values[:, :, :, :, :], 0.0).then_inc(const_step, 1)
            pool.wait_ge(const_step, 2)
            pool.memset(values[:, :, :, :, HEAD_DIM:HEAD_DIM + 1], 1.0).then_inc(consts, 1)

            for k in range(TOPK):
                for t in range(NTILES):
                    at = EXPERTS + k * NTILES + t
                    pool.iota(order_int[:, at:at + 1], [[0, 1]], base=k * TOKENS + TILE_AT[t], channel_multiplier=1).then_inc(order_in, 1)
            pool.iota(order_int[:, 0:EXPERTS], [[-1, EXPERTS]], base=EXPERTS, channel_multiplier=0).then_inc(order_in, 1)
            pool.memset(all_ones[:, :], 1.0).then_inc(order_in, 1)
            pool.memset(valid[:, :], 1.0).then_inc(const_step, 1)
            pool.wait_ge(const_step, 3)
            pool.wait_ge(order_in, 8)
            pool.affine_select(out=before[:, :], in_=all_ones[:, :], compare_op=ALU.is_gt, fill=0.0, base=0,
                               pattern=[[1, 128]], channel_multiplier=-1).then_inc(order_in, 1)
            pool.affine_select(out=valid[:, 0:2], in_=valid[:, 0:2], compare_op=ALU.is_gt, fill=0.0, base=PTILE,
                               pattern=[[0, 2]], channel_multiplier=-1).then_inc(order_in, 1)

            def scatter(i):
                pool.wait_ge(x2_copied, i + 1)
                pool.wait_ge(route, ROUTE_STEPS * (i + 1))
                pool.nop(nofuse=True)
                for t, rows in enumerate(TILE_ROWS):
                    for k in range(TOPK):
                        pool.indirect_dma_start(rows_dram[:, :], bass.IndirectOffsetOnAxis(place_int[0:rows, t, k:k + 1], 0),
                                                routed[0:rows, k, t, :], None).then_inc(scattered, 16)

            def copy(i, p, ready=None):
                if not isinstance(i, int) or i >= 2:
                    pool.wait_ge(t_mm, HEADS * (i - 1))
                pool.wait_ge(lat_lo, i + 1)
                pool.nop(nofuse=True)
                pool.tensor_copy(lat_one[0:RANK, p, :], lat[0:RANK, p, :].bitcast(F32)).then_inc(lat_one_ready, 1)

            def body(i, p, front, prep, post):
                if post:
                    scatter(i - 1)
                if prep:
                    copy(i + 2, p)

            def epilogue():
                scatter(IMAGES - 1)
                pool.wait_ge(scattered, 16 * TOPK * NTILES * IMAGES)

            run(pool, lambda: (copy(0, 0), copy(1, 1)), body, epilogue)

        @block.scalar
        def _(act):
            act.preload_act_table_set("natural_log_exp_and_others")
            act.wait_ge(mat_step, 3)
            act.activation(mats_hi[:, :, :, :],
                           residual[:, :, :].rearrange("p h (a s) -> p h a s", a=1).to_broadcast([128, HEADS, 2, RANK]),
                           ACT.Copy).then_inc(mat_step, 1)
            act.wait_ge(consts, 5)

            def layernorm_scale(i):
                act.wait_ge(dve_ln, 6 * (i + 1))
                act.activation(logvar[:, :], moments[:, :, 1], ACT.Ln, bias=eps[:, :]).then_inc(act_ln, 1)
                act.wait_ge(act_ln, 2 * i + 1)
                act.activation(rstd[:, :], logvar[:, :], ACT.Exp, scale=-0.5).then_inc(act_ln, 1)

            def transposed(i):
                act.wait_ge(x_turned, i + 1)
                act.activation(xT[:, :, :], ps_m[0:HALF, :, 0:N], ACT.Copy).then_inc(xT_ready, 1)

            def latents(i, p):
                act.wait_ge(lat_mm, i + 1)
                act.activation(lat[:, p, :], ps_q[:, 0:N], ACT.Copy).then_inc(lat_hi, 1)

            def query(i, p, h):
                act.wait_ge(q_mm, HEADS * i + h + 1)
                act.activation(q_hi[:, p, h, :], ps_q[:, 0:N], ACT.Copy).then_inc(q_hi_ready, 1)

            def exponentials(i, h, slot, free):
                if free:
                    act.wait_ge(pv_mm, GROUPS * i + h // GROUP - 1)
                act.wait_ge(t_mm, HEADS * i + h + 1)
                act.activation(probs[:, slot, :], ps_t[0:KEYS, 0:3 * N], ACT.Exp, scale=SCORE_SCALE).then_inc(probs_ready, 1)

            def post_scale(i):
                act.wait_ge(dve_ln2, 6 * (i + 1))
                act.activation(logvar2[:, :], moments2[:, :, 1], ACT.Ln, bias=eps[:, :]).then_inc(act_ln2, 1)
                act.wait_ge(act_ln2, 2 * i + 1)
                act.activation(rstd2[:, :], logvar2[:, :], ACT.Exp, scale=-0.5).then_inc(act_ln2, 1)

            def post_copies(i):
                act.wait_ge(x2_ready, 3 * (i + 1))
                act.activation(routed[:, 1, :, 0:DIM], routed[:, 0, :, 0:DIM], ACT.Copy).then_inc(x2_copied, 1)
                act.wait_ge(x2_turned, i + 1)
                act.activation(x2T[:, :, :], ps_m[0:HALF, :, 0:N], ACT.Copy).then_inc(x2T_ready, 1)

            def post_exponentials(i):
                act.wait_ge(route, ROUTE_STEPS * i + MAX_TAKEN)
                act.activation(expo[:, :, :], expo[:, :, :], ACT.Exp).then_inc(expo_ready, 1)

            def prologue():
                for i in range(2):
                    layernorm_scale(i)
                    transposed(i)
                    latents(i, i)
                for h in range(HEADS):
                    query(0, 0, h)

            def body(i, p, front, prep, post):
                for h in range(HEADS):
                    if front:
                        query(i + 1, 1 - p, h)
                    group = GROUPS * p + h // GROUP
                    exponentials(i, h, (group % 2) * GROUP + h % GROUP, not isinstance(i, int) or GROUPS * i + h // GROUP >= 2)
                    if post and h == POST_SCALE:
                        post_scale(i - 1)
                    if post and h == POST_TURN:
                        post_copies(i - 1)
                    if post and h == POST_ROUTE:
                        post_exponentials(i - 1)
                    if prep and h == LN_AT:
                        layernorm_scale(i + 2)
                    if prep and h == TURN_AT:
                        transposed(i + 2)
                if prep:
                    latents(i + 2, p)

            def epilogue():
                post_scale(IMAGES - 1)
                post_copies(IMAGES - 1)
                post_exponentials(IMAGES - 1)

            run(act, prologue, body, epilogue)

        @block.vector
        def _(dve):
            dve.memset(lat_one[RANK:RANK + 1, :, :].bitcast(F32), -1.0).then_inc(one_row, 1)
            dve.wait_ge(w_in, 16 * 8)
            dve.tensor_reduce(mean_mat[:, :], residual[:, :, :].rearrange("p h s -> p s h"), AX, ALU.add).then_inc(mat_step, 1)
            dve.wait_ge(mat_step, 1)
            dve.tensor_tensor(mean_mat[:, :], core_sb[:, :], mean_mat[:, :], ALU.subtract).then_inc(mat_step, 1)
            dve.wait_ge(mat_step, 2)
            dve.scalar_tensor_tensor(out=residual[:, :, :],
                                     in0=mean_mat[:, :].rearrange("p (a s) -> p a s", a=1).to_broadcast([128, HEADS, RANK]),
                                     scalar=1.0 / HEADS, in1=residual[:, :, :], op0=ALU.mult, op1=ALU.add).then_inc(mat_step, 1)
            dve.wait_ge(mat_step, 4)
            dve.tensor_tensor(mats_lo[:, :, :, :],
                              residual[:, :, :].rearrange("p h (a s) -> p h a s", a=1).to_broadcast([128, HEADS, 2, RANK]),
                              mats_hi[:, :, :, :].bitcast(F32), ALU.subtract).then_inc(mat_step, 1)
            dve.wait_ge(w_turned, 1)
            dve.tensor_copy(basisT[:, :, :, :], ps_m[0:HALF, 0, 0:2 * RANK].rearrange("p (k a r) -> p k a r", k=2, a=1)
                            .to_broadcast([HALF, 2, 2, RANK])).then_inc(w_ready, 1)
            dve.tensor_copy(routerT[:, :, :], ps_m[0:HALF, 0, 256:256 + 2 * EXPERTS].rearrange("p (k e) -> p k e", k=2)).then_inc(w_ready, 1)
            dve.tensor_copy(valueT[:, :, :], ps_m[0:HALF, 1, 0:2 * DIM].rearrange("p (k o) -> p k o", k=2)).then_inc(w_ready, 1)
            dve.wait_ge(consts, 5)

            def layernorm_stats(i, p):
                dve.wait_ge(front_in[p], of_pair(i, p, 32))
                for t in range(NTILES):
                    dve.bn_stats(stats[:, t, :], h_front[:, p, t, :]).then_inc(dve_ln, 1)
                dve.wait_ge(dve_ln, 6 * i + 3)
                dve.nop(nofuse=True)
                for t in range(NTILES):
                    dve.bn_aggr(moments[:, t, :], stats[:, t, :]).then_inc(dve_ln, 1)

            def layernorm(i, p):
                dve.wait_ge(act_ln, 2 * (i + 1))
                if not isinstance(i, int) or i > 0:
                    dve.wait_ge(x_turned, i)
                square, half, scale = (newton[:, k, :] for k in range(3))
                dve.tensor_tensor(square, rstd[:, :], rstd[:, :], ALU.mult).then_inc(refined, 1)
                dve.wait_ge(refined, 4 * i + 1)
                dve.scalar_tensor_tensor(out=half, in0=moments[:, :, 1], scalar=LN_EPS, in1=square,
                                         op0=ALU.add, op1=ALU.mult).then_inc(refined, 1)
                dve.wait_ge(refined, 4 * i + 2)
                dve.tensor_scalar(half, half, -0.5, 1.5, ALU.mult, ALU.add).then_inc(refined, 1)
                dve.wait_ge(refined, 4 * i + 3)
                dve.tensor_tensor(scale, rstd[:, :], half, ALU.mult).then_inc(refined, 1)
                dve.wait_ge(refined, 4 * i + 4)
                for t in range(NTILES):
                    dve.tensor_scalar(xn[:, t, :], h_front[:, p, t, :], moments[:, t, 0:1], newton[:, 2, t:t + 1],
                                      ALU.subtract, ALU.mult).then_inc(xn_ready, 1)

            def latents(i, p):
                dve.wait_ge(lat_hi, i + 1)
                dve.tensor_tensor(lat[RANK:128, p, :], ps_q[RANK:128, 0:N], lat[RANK:128, p, :].bitcast(F32),
                                  ALU.subtract).then_inc(lat_lo, 1)

            def value(i, p):
                dve.wait_ge(v_mm, i + 1)
                for a, b in ((0, 2), (2, 3)):
                    src = ps_m[0:KEYS, a // 2, 0:(b - a) * DIM].rearrange("p (c h d) -> p c h d", c=b - a, h=HEADS)
                    bias = value_bias[:, :].rearrange("p (c h d) -> p c h d", c=1, h=HEADS)
                    if b - a > 1:
                        bias = bias.to_broadcast([KEYS, b - a, HEADS, HEAD_DIM])
                    dve.tensor_tensor(values[:, p, a:b, :, 0:HEAD_DIM], src, bias, ALU.add).then_inc(v_ready, 1)

            def query(i, p, h):
                dve.wait_ge(q_hi_ready, HEADS * i + h + 1)
                dve.tensor_tensor(q_lo[0:RANK, p, h, :], ps_q[0:RANK, 0:N], q_hi[0:RANK, p, h, :].bitcast(F32),
                                  ALU.subtract).then_inc(q_lo_ready, 1)

            def maximum(i, p, h):
                dve.wait_ge(s_mm, HEADS * i + h + 1)
                dve.tensor_reduce(row_max[:, p, :, h], ps_s[0:KEYS, 0:3 * N].rearrange("p (c m) -> p c m", c=3), AX,
                                  ALU.max).then_inc(max_ready, 1)

            def maximum_rows(i, p):
                dve.wait_ge(max_turned, i + 1)
                if not isinstance(i, int) or i > 0:
                    dve.wait_ge(max_in[1 - p], of_pair(i - 1, 1 - p, 16))
                dve.tensor_copy(max_rows[:, :], ps_m[0:HEADS, 1, 0:N]).then_inc(max_rows_ready, 1)

            def products(i, g):
                n = GROUPS * i + g
                dve.wait_ge(pv_mm, n + 1)
                if not isinstance(n, int) or n > 0:
                    dve.wait_ge(ctx_turned, n)
                dve.tensor_copy(ctx_sb[:, :], ps_v[:, 0:N]).then_inc(ctx_ready, 1)

            def residual_add(i, p, g):
                n = GROUPS * i + g
                dve.wait_ge(ctx_turned, n + 1)
                if g == 0:
                    dve.wait_ge(back_in[p], of_pair(i, p, 32))
                src = ps_m[:, 0, 0:NTILES * GROUP * 32].rearrange("p (t b e) -> p t b e", t=NTILES, b=GROUP)
                for a, b, rows in PARTS:
                    dve.reciprocal(recip[0:rows, a:b, :, :], src[0:rows, a:b, :, HEAD_DIM:HEAD_DIM + 1]).then_inc(recip_ready, 1)
                dve.wait_ge(recip_ready, 2 * n + 2)
                for a, b, rows in PARTS:
                    dve.tensor_tensor(scaled[0:rows, a:b, :, :], src[0:rows, a:b, :, 0:HEAD_DIM],
                                      recip[0:rows, a:b, :, :].to_broadcast([rows, b - a, GROUP, HEAD_DIM]),
                                      ALU.mult).then_inc(scaled_ready, 1)
                dve.wait_ge(scaled_ready, 2 * n + 2)
                for a, b, rows in PARTS:
                    at = h_back[0:rows, p, a:b, g * GROUP * HEAD_DIM:(g + 1) * GROUP * HEAD_DIM]
                    dve.tensor_tensor(at, at, scaled[0:rows, a:b, :, :].rearrange("p t b e -> p t (b e)"),
                                      ALU.add).then_inc(h2_ready, 1)

            def post_stats(i, p):
                dve.wait_ge(h2_ready, 2 * GROUPS * (i + 1))
                for t in range(NTILES):
                    dve.bn_stats(stats2[:, t, :], h_back[:, p, t, :]).then_inc(dve_ln2, 1)
                dve.wait_ge(dve_ln2, 6 * i + 3)
                dve.nop(nofuse=True)
                for t in range(NTILES):
                    dve.bn_aggr(moments2[:, t, :], stats2[:, t, :]).then_inc(dve_ln2, 1)

            def post_norm(i, p):
                dve.wait_ge(act_ln2, 2 * (i + 1))
                square, half, scale = (newton2[:, k, :] for k in range(3))
                dve.tensor_tensor(square, rstd2[:, :], rstd2[:, :], ALU.mult).then_inc(refined2, 1)
                dve.wait_ge(refined2, 4 * i + 1)
                dve.scalar_tensor_tensor(out=half, in0=moments2[:, :, 1], scalar=LN_EPS, in1=square,
                                         op0=ALU.add, op1=ALU.mult).then_inc(refined2, 1)
                dve.wait_ge(refined2, 4 * i + 2)
                dve.tensor_scalar(half, half, -0.5, 1.5, ALU.mult, ALU.add).then_inc(refined2, 1)
                dve.wait_ge(refined2, 4 * i + 3)
                dve.tensor_tensor(scale, rstd2[:, :], half, ALU.mult).then_inc(refined2, 1)
                dve.wait_ge(refined2, 4 * i + 4)
                if not isinstance(i, int) or i > 0:
                    dve.wait_ge(scattered, 16 * TOPK * NTILES * i)
                for t in range(NTILES):
                    dve.tensor_scalar(routed[:, 0, t, 0:DIM], h_back[:, p, t, :], moments2[:, t, 0:1], newton2[:, 2, t:t + 1],
                                      ALU.subtract, ALU.mult).then_inc(x2_ready, 1)

            def over_experts(ap):
                return ap.rearrange("p (t e) -> p t e", e=1).to_broadcast([128, NTILES, EXPERTS])

            def over_tiles(ap):
                return ap.rearrange("p (t e) -> p t e", t=1).to_broadcast([128, NTILES, EXPERTS])

            def routing(i):
                n = 0

                def step(instruction, wait=True):
                    nonlocal n
                    n += 1
                    instruction.then_inc(route, 1)
                    if wait:
                        dve.wait_ge(route, ROUTE_STEPS * i + n)

                def first_part():
                    dve.wait_ge(logit_mm, i + 1)
                    step(dve.tensor_copy(logits[:, :, :], ps_m[:, 1, 0:NTILES * EXPERTS].rearrange("p (t e) -> p t e", t=NTILES)))
                    assert n == LOGITS_READ
                    step(dve.tensor_reduce(top[:, :], logits[:, :, :], AX, ALU.max))
                    step(dve.tensor_tensor(expo[:, :, :], logits[:, :, :], over_experts(top[:, :]), ALU.subtract))
                    assert n == MAX_TAKEN
                    for k in range(TOPK):
                        of = logits if k == 0 else rest
                        if k:
                            step(dve.scalar_tensor_tensor(out=rest[:, :, :], in0=pick[:, :, 0, :], scalar=MASKED,
                                                          in1=logits[:, :, :], op0=ALU.mult, op1=ALU.add))
                            step(dve.tensor_reduce(top[:, :], rest[:, :, :], AX, ALU.max))
                        step(dve.tensor_tensor(key[:, :, :], of[:, :, :], over_experts(top[:, :]), ALU.is_equal))
                        step(dve.tensor_tensor(key[:, :, :], key[:, :, :], over_tiles(order[:, :]), ALU.mult))
                        step(dve.tensor_reduce(total[:, :], key[:, :, :], AX, ALU.max))
                        step(dve.tensor_tensor(pick[:, :, k, :], over_tiles(order[:, :]), over_experts(total[:, :]), ALU.is_equal))
                    step(dve.tensor_tensor(key[:, :, :], pick[:, :, 0, :], pick[:, :, 1, :], ALU.add))
                    step(dve.tensor_tensor(picked[:, :, :], key[:, :, :], over_experts(valid[:, :]), ALU.mult))
                    assert n == PICKED

                def second_part():
                    dve.wait_ge(expo_ready, i + 1)
                    step(dve.tensor_reduce(total[:, :], expo[:, :, :], AX, ALU.add))
                    step(dve.reciprocal(total[:, :], total[:, :]))
                    step(dve.tensor_tensor(key[:, :, :], expo[:, :, :], over_experts(total[:, :]), ALU.mult))
                    step(dve.tensor_tensor(importance[:, :, :], importance[:, :, :], key[:, :, :], ALU.add))
                    step(dve.tensor_tensor(of_pick[:, :, :, :], pick[:, :, :, :],
                                           key[:, :, :].rearrange("p t (k e) -> p t k e", k=1).to_broadcast([128, NTILES, TOPK, EXPERTS]),
                                           ALU.mult))
                    step(dve.tensor_reduce(pick_probs[:, bass.ds(i, 1), :, :].rearrange("p i t k -> p (i t) k"),
                                           of_pick[:, :, :, :], AX, ALU.add))
                    step(dve.tensor_copy(picks[:, bass.ds(i, 1), :, :, :].rearrange("p i t k e -> p (i t) k e"), pick[:, :, :, :]))

                def third_part():
                    dve.wait_ge(rank_mm, i + 1)
                    step(dve.tensor_tensor(key[:, :, :], ps_m[:, 1, 0:NTILES * EXPERTS].rearrange("p (t e) -> p t e", t=NTILES),
                                           over_tiles(places[:, :]), ALU.add))
                    step(dve.tensor_tensor(places[:, :], ps_m[:, 1, 32:32 + EXPERTS], places[:, :], ALU.add))
                    step(dve.tensor_tensor(routed[:, :, :, DIM:ROW], goal[:, :, :, :], goal[:, :, :, :], ALU.max))
                    assert n == RANKED
                    step(dve.tensor_tensor(of_pick[:, :, :, :], pick[:, :, :, :],
                                           key[:, :, :].rearrange("p t (k e) -> p t k e", k=1).to_broadcast([128, NTILES, TOPK, EXPERTS]),
                                           ALU.mult))
                    step(dve.tensor_reduce(place[:, :, :], of_pick[:, :, :, :], AX, ALU.add))
                    dve.tensor_scalar(goal[:, :, :, :], goal[:, :, :, :], float(N), None, ALU.add)
                    step(dve.tensor_copy(place_int[:, :, :], place[:, :, :]), wait=False)
                    assert n == ROUTE_STEPS

                return first_part, second_part, third_part

            def prologue():
                dve.wait_ge(order_in, 10)
                dve.tensor_copy(order[:, :], order_int[:, 0:EXPERTS]).then_inc(order_ready, 1)
                dve.tensor_copy(goal[:, :, :, 0], order_int[:, EXPERTS:].rearrange("p (k t) -> p k t", k=TOPK)).then_inc(order_ready, 1)
                dve.memset(importance[:, :, :], 0.0).then_inc(order_ready, 1)
                dve.wait_ge(order_ready, 3)
                dve.tensor_scalar(places[:, :], order[:, :], float(-SPACE), float(EXPERTS * SPACE), ALU.mult, ALU.add).then_inc(order_ready, 1)
                for i in range(2):
                    layernorm_stats(i, i)
                    layernorm(i, i)
                    latents(i, i)
                    value(i, i)
                for h in range(HEADS):
                    query(0, 0, h)
                    maximum(0, 0, h)
                maximum_rows(0, 0)

            def body(i, p, front, prep, post):
                if post:
                    parts = routing(i - 1)
                for h in range(HEADS):
                    if front:
                        query(i + 1, 1 - p, h)
                    if post and h == POST_SCALE:
                        post_stats(i - 1, 1 - p)
                    if post and h in POST_PARTS:
                        parts[POST_PARTS.index(h)]()
                    if prep and h == LN_AT:
                        layernorm_stats(i + 2, p)
                    if h % GROUP == 0 and h > 0:
                        products(i, h // GROUP - 1)
                    if front:
                        maximum(i + 1, 1 - p, h)
                    if post and h == POST_SCALE:
                        post_norm(i - 1, 1 - p)
                    if prep and h == LN_AT:
                        layernorm(i + 2, p)
                    if h % GROUP == 1 and h > 1:
                        residual_add(i, p, h // GROUP - 1)
                if front:
                    maximum_rows(i + 1, 1 - p)
                if prep:
                    latents(i + 2, p)
                products(i, GROUPS - 1)
                residual_add(i, p, GROUPS - 1)
                if prep:
                    value(i + 2, p)

            def epilogue():
                post_stats(IMAGES - 1, 1)
                post_norm(IMAGES - 1, 1)
                for part in routing(IMAGES - 1):
                    part()

            run(dve, prologue, body, epilogue)

        @block.tensor
        def _(pe):
            pe.wait_ge(w_in, 16 * 8)
            pe.wait_ge(consts, 5)
            for k in range(2):
                half = slice(k * HALF, (k + 1) * HALF)
                pe.transpose(ps_m[0:HALF, 0, k * RANK:(k + 1) * RANK], basis_raw[:, half], ident[0:RANK, 0:RANK])
                for o in range(2):
                    pe.transpose(ps_m[0:HALF, 1, k * DIM + o * HALF:k * DIM + (o + 1) * HALF], value_raw[:, o, half],
                                      ident[0:HALF, 0:HALF])
                mm = pe.transpose(ps_m[0:HALF, 0, 256 + k * EXPERTS:256 + (k + 1) * EXPERTS], router_raw[:, half],
                                  ident[0:EXPERTS, 0:EXPERTS])
            mm.then_inc(w_turned, 1)
            pe.wait_ge(w_ready, 3)
            pe.wait_ge(mat_step, 5)

            def transpose_x(i):
                pe.wait_ge(xn_ready, 3 * (i + 1))
                if not isinstance(i, int) or i > 0:
                    pe.wait_ge(xT_ready, i)
                for t, (at, rows) in enumerate(zip(TILE_AT, TILE_ROWS)):
                    for k in range(2):
                        mm = pe.transpose(ps_m[0:HALF, k, at:at + rows], xn[0:rows, t, k * HALF:(k + 1) * HALF],
                                          ident[0:rows, 0:rows])
                mm.then_inc(x_turned, 1)

            def latents(i):
                pe.wait_ge(xT_ready, i + 1)
                for k in range(2):
                    mm = pe.matmul(ps_q[:, 0:N], basisT[:, k, :, :].rearrange("p a r -> p (a r)"), xT[:, k, :],
                                   start=(k == 0), stop=(k == 1))
                mm.then_inc(lat_mm, 1)

            def value(i):
                for c in range(3):
                    for k in range(2):
                        mm = pe.matmul(ps_m[0:KEYS, c // 2, (c % 2) * DIM:(c % 2 + 1) * DIM], xT[:, k, c * KEYS:(c + 1) * KEYS],
                                       valueT[:, k, :], start=(k == 0), stop=(k == 1))
                mm.then_inc(v_mm, 1)

            def query(i, p, h):
                if h == 0:
                    pe.wait_ge(lat_lo, i + 1)
                if not isinstance(i, int) or i > 0 or h > 0:
                    pe.wait_ge(q_lo_ready, HEADS * i + h)
                pe.matmul(ps_q[:, 0:N], mats_lo[:, h, :, :].rearrange("p a s -> p (a s)"), lat[:, p, :], start=True, stop=False)
                pe.matmul(ps_q[:, 0:N], mats_hi[:, h, :, :].rearrange("p a s -> p (a s)"), lat[:, p, :], start=False,
                          stop=True).then_inc(q_mm, 1)

            def scores_by_query(i, p, h):
                pe.wait_ge(q_hi_ready, HEADS * i + h + 1)
                if not isinstance(i, int) or i > 0 or h > 0:
                    pe.wait_ge(max_ready, HEADS * i + h)
                for c, a, b in PIECES:
                    mm = pe.matmul(ps_s[0:KEYS, a:b], q_hi[:, p, h, c * KEYS:(c + 1) * KEYS], lat[:, p, a - c * N:b - c * N],
                                   start=True, stop=True)
                mm.then_inc(s_mm, 1)

            def maximum_rows(i, p):
                pe.wait_ge(max_ready, HEADS * (i + 1))
                for c in range(3):
                    mm = pe.transpose(ps_m[0:HEADS, 1, c * KEYS:(c + 1) * KEYS], row_max[:, p, c, :], ident[0:KEYS, 0:KEYS])
                mm.then_inc(max_turned, 1)

            def scores_by_key(i, p, h):
                if h == 0:
                    pe.wait_ge(one_row, 1)
                    pe.wait_ge(max_in[p], of_pair(i, p, 16))
                    pe.wait_ge(lat_one_ready, i + 1)
                    pe.wait_ge(q_lo_ready, HEADS * (i + 1))
                if not isinstance(i, int) or i > 0 or h > 0:
                    pe.wait_ge(probs_ready, HEADS * i + h)
                for c, a, b in PIECES:
                    keys = slice(c * KEYS, (c + 1) * KEYS)
                    queries = slice(a - c * N, b - c * N)
                    pe.matmul(ps_t[0:KEYS, a:b], lat_one[:, p, keys], q_lo[:, p, h, queries], start=True, stop=False)
                    mm = pe.matmul(ps_t[0:KEYS, a:b], lat[:, p, keys], q_hi[:, p, h, queries], start=False, stop=True)
                mm.then_inc(t_mm, 1)

            def products(i, p, g, slot):
                n = GROUPS * i + g
                if g == 0:
                    pe.wait_ge(v_ready, 2 * (i + 1))
                pe.wait_ge(probs_ready, HEADS * i + (g + 1) * GROUP)
                if not isinstance(n, int) or n > 0:
                    pe.wait_ge(ctx_ready, n)
                for c in range(3):
                    for b in range(GROUP):
                        mm = pe.matmul(ps_v[32 * b:32 * (b + 1), 0:N], values[:, p, c, g * GROUP + b, :],
                                       probs[:, slot * GROUP + b, c * N:(c + 1) * N], start=(c == 0), stop=(c == 2))
                mm.then_inc(pv_mm, 1)

            def turn_products(i, g):
                n = GROUPS * i + g
                pe.wait_ge(ctx_ready, n + 1)
                for t, (at, rows) in enumerate(zip(TILE_AT, TILE_ROWS)):
                    mm = pe.transpose(ps_m[0:rows, 0, t * GROUP * 32:(t + 1) * GROUP * 32], ctx_sb[:, at:at + rows], ident[:, :])
                mm.then_inc(ctx_turned, 1)

            def post_turn(i):
                pe.wait_ge(x2_ready, 3 * (i + 1))
                for t, (at, rows) in enumerate(zip(TILE_AT, TILE_ROWS)):
                    for k in range(2):
                        mm = pe.transpose(ps_m[0:HALF, k, at:at + rows], routed[0:rows, 0, t, k * HALF:(k + 1) * HALF],
                                          ident[0:rows, 0:rows])
                mm.then_inc(x2_turned, 1)

            def post_logits(i):
                pe.wait_ge(x2T_ready, i + 1)
                for t, at in enumerate(TILE_AT):
                    for k in range(2):
                        mm = pe.matmul(ps_m[:, 1, t * EXPERTS:(t + 1) * EXPERTS], x2T[:, k, at:at + 128], routerT[:, k, :],
                                       start=(k == 0), stop=(k == 1))
                mm.then_inc(logit_mm, 1)

            def post_ranks(i):
                pe.wait_ge(route, ROUTE_STEPS * i + PICKED)
                for t in range(NTILES):
                    for of in range(t + 1):
                        pe.matmul(ps_m[:, 1, t * EXPERTS:(t + 1) * EXPERTS], (before if of == t else all_ones)[:, :],
                                  picked[:, of, :], start=(of == 0), stop=(of == t))
                for t in range(NTILES):
                    mm = pe.matmul(ps_m[:, 1, 32:32 + EXPERTS], all_ones[:, :], picked[:, t, :], start=(t == 0), stop=(t == 2))
                mm.then_inc(rank_mm, 1)

            def prologue():
                for i in range(2):
                    if i:
                        pe.wait_ge(v_ready, 2 * i)
                    transpose_x(i)
                    if i:
                        pe.wait_ge(lat_lo, i)
                    latents(i)
                    value(i)
                pe.wait_ge(lat_lo, 2)
                for h in range(HEADS):
                    query(0, 0, h)
                    scores_by_query(0, 0, h)
                pe.wait_ge(v_ready, 4)
                maximum_rows(0, 0)

            def body(i, p, front, prep, post):
                for h in range(HEADS):
                    if front:
                        query(i + 1, 1 - p, h)
                    scores_by_key(i, p, h)
                    if h % GROUP == 0 and h > 0:
                        products(i, p, h // GROUP - 1, (GROUPS * p + h // GROUP - 1) % 2)
                    if front:
                        scores_by_query(i + 1, 1 - p, h)
                    if post and h == POST_TURN:
                        pe.wait_ge(v_ready, 2 * (i + 2) if front else 2 * IMAGES)
                        pe.wait_ge(max_rows_ready, i + 1)
                        pe.wait_ge(scaled_ready, 2 * GROUPS * i)
                        post_turn(i - 1)
                    if post and h == POST_TURN + 1:
                        post_logits(i - 1)
                    if post and h == POST_RANK:
                        if prep:
                            pe.wait_ge(xT_ready, i + 3)
                        post_ranks(i - 1)
                    if h % GROUP == 1 and h > 1:
                        if h // GROUP == 1:
                            pe.wait_ge(v_ready, 2 * (i + 2) if front else 2 * IMAGES)
                        elif prep:
                            pe.wait_ge(xT_ready, i + 3)
                        turn_products(i, h // GROUP - 1)
                    if prep and h == TURN_AT:
                        pe.wait_ge(scaled_ready, 2 * (GROUPS * i + 1))
                        pe.wait_ge(max_rows_ready, i + 1)
                        if post:
                            pe.wait_ge(route, ROUTE_STEPS * (i - 1) + LOGITS_READ)
                        transpose_x(i + 2)
                if front:
                    if prep:
                        pe.wait_ge(xT_ready, i + 3)
                    if post:
                        pe.wait_ge(route, ROUTE_STEPS * (i - 1) + RANKED)
                    maximum_rows(i + 1, 1 - p)
                if prep:
                    pe.wait_ge(q_lo_ready, HEADS * (i + 2))
                    latents(i + 2)
                products(i, p, GROUPS - 1, (GROUPS * p + GROUPS - 1) % 2)
                pe.wait_ge(scaled_ready, 2 * (GROUPS * i + 2))
                turn_products(i, GROUPS - 1)
                if prep:
                    pe.wait_ge(scaled_ready, 2 * (GROUPS * i + 3))
                    pe.wait_ge(max_rows_ready, i + 2)
                    value(i + 2)

            def epilogue():
                pe.wait_ge(scaled_ready, 2 * GROUPS * IMAGES)
                post_turn(IMAGES - 1)
                post_logits(IMAGES - 1)
                post_ranks(IMAGES - 1)

            run(pe, prologue, body, epilogue)


RESULTS = TOPK * TOKENS
INNER = HIDDEN // 128


def experts(nc, w1, w2, rows_dram, results_dram, places):
    with ExitStack() as ctx:
        def sb(name, shape, dt=F32):
            return ctx.enter_context(nc.sbuf_tensor(name, shape, dt))

        def psum(name, shape, dt=F32):
            return ctx.enter_context(nc.psum_tensor(name, shape, dt))

        def sem(name):
            return ctx.enter_context(nc.semaphore(name))

        ident = sb("identB", [128, 128])
        w1_hi = sb("w1_hi", [HALF, 2, EXPERTS, HIDDEN], F32R)
        w1_lo = sb("w1_lo", [HALF, 2, EXPERTS, HIDDEN], F32R)
        w2_hi = sb("w2_hi", [128, EXPERTS, INNER, DIM], F32R)
        w2_lo = sb("w2_lo", [128, EXPERTS, INNER, DIM], F32R)
        w1_raw = sb("w1_raw", [128, EXPERTS * INNER, DIM])
        w2_raw = sb("w2_raw", [HALF, 2, EXPERTS, HIDDEN])

        int_consts = sb("int_consts", [128, EXPERTS + 1], I32)
        step_int = sb("step_int", [128, BLOCKS], I32)
        row_no = sb("row_no", [128, 1])
        first_row = sb("first_row", [128, EXPERTS])
        step_no = sb("step_no", [128, BLOCKS])
        empty = sb("empty", [128, ROW])
        pad_place = sb("pad_place", [128, EXPERTS])
        pad_int = sb("pad_int", [128, EXPERTS], I32)
        tiles_int = sb("tiles_int", [128, EXPERTS], I32)
        tiles = sb("tiles", [128, EXPERTS])
        ends = sb("ends", [128, 2, EXPERTS])
        jump = sb("jump", [128, EXPERTS])
        past = sb("past", [128, BLOCKS, EXPERTS])
        table = sb("table", [128, 2, BLOCKS])
        table_int = sb("table_int", [128, 2, BLOCKS], I32)

        rows = sb("rows", [128, 2, ROW])
        goal_int = sb("goal_int", [128, 2, 1], I32)
        x_hi = sb("x_hi", [HALF, 2, 2, 128], F32R)
        x_lo = sb("x_lo", [HALF, 2, 2, 128], F32R)
        hidden = sb("hidden", [128, 2, HIDDEN])
        hT_hi = sb("hT_hi", [128, 2, HIDDEN], F32R)
        hT_lo = sb("hT_lo", [128, 2, HIDDEN], F32R)
        result = sb("result", [128, 2, DIM])

        ps_x = psum("ps_x", [HALF, 2, BANK])
        ps_h = psum("ps_h", [128, 2, BANK])
        ps_t = psum("ps_tB", [128, 2, BANK])
        ps_y = psum("ps_y", [128, 2, BANK])

        consts, const_step = sem("constsB"), sem("const_stepB")
        w1_in, w2_in = sem("w1_in"), sem("w2_in")
        w_turned = sem("w_turnedB")
        w_hi_ready = sem("w_hi_readyB")
        w_lo_ready = sem("w_lo_readyB")
        table_step = sem("table_step")
        pads_ready = sem("pads_ready")
        table_ready = sem("table_ready")
        padded = sem("padded")
        spare_in = sem("spare_in")
        rows_in = [sem(f"rows_in{i}") for i in range(2)]
        goal_ready = sem("goal_ready")
        x_turned = sem("x_turnedB")
        x_hi_ready = sem("x_hi_readyB")
        x_lo_ready = sem("x_lo_readyB")
        h_mm = sem("h_mm")
        h_ready = sem("h_ready")
        h_turned = sem("h_turned")
        hT_hi_ready = sem("hT_hi_ready")
        hT_lo_ready = sem("hT_lo_ready")
        y_mm = sem("y_mm")
        y_ready = sem("y_ready")
        stored = [sem(f"stored{i}") for i in range(2)]

        block = ctx.enter_context(nc.Block())

        GROUPS_W = 4 * EXPERTS

        def group_of(n):
            return n < 2 * EXPERTS, (n % (2 * EXPERTS)) // 2, n % 2

        @block.sync
        def _(sp):
            sp.dma_start(w1_raw[:, :, :], w1.rearrange("e (c p) h -> p (e c) h", p=128)).then_inc(w1_in, 16)
            sp.dma_start(w2_raw[:, 0, :, :], w2[:, 0:HALF, :].rearrange("e p i -> p e i")).then_inc(w2_in, 16)
            sp.dma_start(w2_raw[:, 1, :, :], w2[:, HALF:DIM, :].rearrange("e p i -> p e i")).then_inc(w2_in, 16)
            sp.wait_ge(consts, 4)
            for k in range(SPARE):
                at = EXPERTS * SPACE + k * 128
                sp.dma_start(rows_dram[at:at + 128, :], empty[:, :]).then_inc(spare_in, 16)
            sp.wait_ge(table_ready, 1)
            sp.wait_ge(spare_in, 16 * SPARE)
            sp.wait_ge(padded, 16 * EXPERTS)

            def load(j, u):
                row = sp.value_load(table_int[0:1, 1, bass.ds(j, 1)], min_val=0, max_val=EXPERTS * SPACE + (SPARE - 1) * 128)
                sp.dma_start(rows[:, u, :], rows_dram[bass.ds(row, 128), :]).then_inc(rows_in[u], 16)

            load(0, 0)
            load(1, 1)
            with sp.Fori(0, BLOCKS // 2 - 1) as it:
                for u in range(2):
                    j = it * 2 + u
                    sp.wait_ge(x_turned, j + 1)
                    sp.wait_ge(goal_ready, j + 1)
                    load(j + 2, u)

        @block.gpsimd
        def _(pool):
            pool.memset(ident[:, :], 0.0).then_inc(const_step, 1)
            pool.memset(empty[:, 0:DIM], 0.0).then_inc(consts, 1)
            pool.iota(int_consts[:, 0:EXPERTS], [[SPACE // 128, EXPERTS]], base=0, channel_multiplier=0).then_inc(consts, 1)
            pool.iota(int_consts[:, EXPERTS:EXPERTS + 1], [[0, 1]], base=0, channel_multiplier=1).then_inc(consts, 1)
            pool.iota(step_int[:, :], [[1, BLOCKS]], base=0, channel_multiplier=0).then_inc(const_step, 1)
            pool.wait_ge(const_step, 2)
            pool.affine_select(out=ident[:, :], in_=ident[:, :], compare_op=ALU.not_equal, fill=1.0,
                               base=0, pattern=[[-1, 128]], channel_multiplier=1).then_inc(const_step, 1)
            pool.wait_ge(pads_ready, 1)
            for e in range(EXPERTS):
                pool.indirect_dma_start(rows_dram[:, :], bass.IndirectOffsetOnAxis(pad_int[:, e:e + 1], 0),
                                        empty[:, :], None).then_inc(padded, 16)

            def store(j, u):
                pool.wait_ge(goal_ready, j + 1)
                pool.wait_ge(y_ready, j + 1)
                pool.nop(nofuse=True)
                pool.indirect_dma_start(results_dram[:, :], bass.IndirectOffsetOnAxis(goal_int[:, u, :], 0),
                                        result[:, u, :], None, bounds_check=RESULTS - 1,
                                        oob_is_err=False).then_inc(stored[u], 16)

            with pool.Fori(0, BLOCKS // 2) as it:
                for u in range(2):
                    store(it * 2 + u, u)
            for u in range(2):
                pool.wait_ge(stored[u], 16 * (BLOCKS // 2))

        def split(n):
            is_w1, e, half = group_of(n)
            if is_w1:
                return (w1_hi[:, half, e, :], w1_lo[:, half, e, :], ps_x[:, n % 2, 0:HIDDEN])
            chunks = slice(half * 2, half * 2 + 2)
            return tuple(w[:, e, chunks, :].rearrange("p c d -> p (c d)") for w in (w2_hi, w2_lo)) + (ps_h[:, n % 2, 0:2 * DIM],)

        def pipeline(engine, first, middle, last):
            first()
            with engine.Fori(0, BLOCKS // 2 - 1) as it:
                for u in (1, 0):
                    middle(it * 2 + 2 - u, u)
            last(BLOCKS - 1, (BLOCKS - 1) % 2)

        @block.scalar
        def _(act):
            act.preload_act_table(ACT.Silu)
            for n in range(GROUPS_W):
                hi, _, src = split(n)
                act.wait_ge(w_turned, n + 1)
                act.activation(hi, src, ACT.Copy).then_inc(w_hi_ready, 1)

            def x_half(j, u):
                act.wait_ge(x_turned, j + 1)
                act.activation(x_hi[:, u, :, :], ps_x[:, u, 0:256].rearrange("p (k t) -> p k t", k=2), ACT.Copy).then_inc(x_hi_ready, 1)

            def silu(j, u):
                act.wait_ge(h_mm, j + 1)
                act.activation(hidden[:, u, :], ps_h[:, u, :], ACT.Silu).then_inc(h_ready, 1)

            def h_half(j, u):
                act.wait_ge(h_turned, j + 1)
                act.activation(hT_hi[:, u, :], ps_t[:, u, :], ACT.Copy).then_inc(hT_hi_ready, 1)

            def first():
                x_half(0, 0)
                silu(0, 0)
                x_half(1, 1)

            def middle(j, u):
                h_half(j - 1, 1 - u)
                silu(j, u)
                x_half(j + 1, 1 - u)

            def last(j, u):
                h_half(j - 1, 1 - u)
                silu(j, u)
                h_half(j, u)

            pipeline(act, first, middle, last)

        @block.vector
        def _(dve):
            dve.wait_ge(consts, 3)
            dve.wait_ge(const_step, 2)
            n = 0

            def step(instruction):
                nonlocal n
                n += 1
                instruction.then_inc(table_step, 1)
                dve.wait_ge(table_step, n)

            dve.tensor_scalar(first_row[:, :], int_consts[:, 0:EXPERTS], 128.0, None, ALU.mult).then_inc(table_step, 1)
            dve.tensor_copy(step_no[:, :], step_int[:, :]).then_inc(table_step, 1)
            n = 2
            step(dve.tensor_copy(row_no[:, :], int_consts[:, EXPERTS:EXPERTS + 1]))
            dve.tensor_scalar(empty[:, DIM:ROW], row_no[:, :], float(RESULTS), None, ALU.add).then_inc(consts, 1)
            step(dve.tensor_scalar(pad_place[:, :], places[:, :], row_no[:, 0:1], None, ALU.add))
            dve.tensor_copy(pad_int[:, :], pad_place[:, :]).then_inc(pads_ready, 1)
            step(dve.tensor_tensor(tiles[:, :], places[:, :], first_row[:, :], ALU.subtract))
            step(dve.tensor_scalar(tiles[:, :], tiles[:, :], 127.0, None, ALU.add))
            step(dve.tensor_copy(tiles_int[:, :], tiles[:, :]))
            step(dve.tensor_single_scalar(tiles_int[:, :], tiles_int[:, :], 7, ALU.arith_shift_right))
            step(dve.tensor_copy(tiles[:, :], tiles_int[:, :]))
            step(dve.tensor_copy(ends[:, 0, :], tiles[:, :]))
            for k, by in enumerate((1, 2, 4)):
                a, b = k % 2, 1 - k % 2
                step(dve.tensor_copy(ends[:, b, 0:by], ends[:, a, 0:by]))
                step(dve.tensor_tensor(ends[:, b, by:EXPERTS], ends[:, a, by:EXPERTS], ends[:, a, 0:EXPERTS - by], ALU.add))
            step(dve.tensor_scalar(jump[:, :], tiles[:, :], -128.0, float(SPACE), ALU.mult, ALU.add))
            step(dve.tensor_tensor(past[:, :, :], step_no[:, :].rearrange("p (j e) -> p j e", e=1).to_broadcast([128, BLOCKS, EXPERTS]),
                                   ends[:, 1, :].rearrange("p (j e) -> p j e", j=1).to_broadcast([128, BLOCKS, EXPERTS]), ALU.is_ge))
            step(dve.tensor_reduce(table[:, 0, :], past[:, :, :], AX, ALU.add))
            step(dve.tensor_scalar(table[:, 0, :], table[:, 0, :], float(EXPERTS - 1), None, ALU.min))
            step(dve.tensor_tensor(past[:, :, :], past[:, :, :],
                                   jump[:, :].rearrange("p (j e) -> p j e", j=1).to_broadcast([128, BLOCKS, EXPERTS]), ALU.mult))
            step(dve.tensor_reduce(table[:, 1, :], past[:, :, :], AX, ALU.add))
            step(dve.scalar_tensor_tensor(out=table[:, 1, :], in0=step_no[:, :], scalar=128.0, in1=table[:, 1, :],
                                          op0=ALU.mult, op1=ALU.add))
            dve.tensor_copy(table_int[:, :, :], table[:, :, :]).then_inc(table_ready, 1)

            for g in range(GROUPS_W):
                hi, lo, src = split(g)
                dve.wait_ge(w_hi_ready, g + 1)
                dve.tensor_tensor(lo, src, hi.bitcast(F32), ALU.subtract).then_inc(w_lo_ready, 1)

            def x_half(j, u):
                dve.wait_ge(x_hi_ready, j + 1)
                dve.tensor_tensor(x_lo[:, u, :, :], ps_x[:, u, 0:256].rearrange("p (k t) -> p k t", k=2),
                                  x_hi[:, u, :, :].bitcast(F32), ALU.subtract).then_inc(x_lo_ready, 1)

            def goal(j, u, wait):
                if wait:
                    dve.wait_ge(stored[u], 8 * (j - u) if u == 0 else 8 * (j - 1))
                dve.wait_ge(rows_in[u], 8 * (j - u) + 16)
                dve.tensor_copy(goal_int[:, u, :], rows[:, u, DIM:ROW]).then_inc(goal_ready, 1)

            def h_half(j, u):
                dve.wait_ge(hT_hi_ready, j + 1)
                dve.tensor_tensor(hT_lo[:, u, :], ps_t[:, u, :], hT_hi[:, u, :].bitcast(F32), ALU.subtract).then_inc(hT_lo_ready, 1)

            def finish(j, u):
                dve.wait_ge(y_mm, j + 1)
                dve.tensor_copy(result[:, u, :], ps_y[:, u, 0:DIM]).then_inc(y_ready, 1)

            def first():
                goal(0, 0, False)
                x_half(0, 0)
                goal(1, 1, False)
                x_half(1, 1)

            def middle(j, u, wait=True):
                h_half(j - 1, 1 - u)
                finish(j - 1, 1 - u)
                goal(j + 1, 1 - u, wait)
                x_half(j + 1, 1 - u)

            def last(j, u):
                h_half(j - 1, 1 - u)
                finish(j - 1, 1 - u)
                h_half(j, u)
                finish(j, u)

            pipeline(dve, first, middle, last)

        @block.tensor
        def _(pe):
            pe.wait_ge(const_step, 3)
            pe.wait_ge(w1_in, 16)
            pe.wait_ge(w2_in, 32)
            for n in range(GROUPS_W):
                is_w1, e, half = group_of(n)
                if n >= 2:
                    pe.wait_ge(w_lo_ready, n - 1)
                dst = split(n)[2]
                for c in range(INNER):
                    if is_w1:
                        mm = pe.transpose(dst[:, c * 128:(c + 1) * 128], w1_raw[:, e * INNER + c, half * HALF:(half + 1) * HALF], ident[:, :])
                    else:
                        chunk = half * 2 + c // 2
                        mm = pe.transpose(dst[:, c * HALF:(c + 1) * HALF], w2_raw[:, c % 2, e, chunk * 128:(chunk + 1) * 128],
                                          ident[0:HALF, 0:HALF])
                mm.then_inc(w_turned, 1)
            pe.wait_ge(w_lo_ready, GROUPS_W)
            pe.wait_ge(table_ready, 1)

            def turn_x(j, u, rounds):
                if rounds:
                    pe.wait_ge(x_lo_ready, j - 1)
                pe.wait_ge(rows_in[u], 8 * (j - u) + 16)
                for k in range(2):
                    mm = pe.transpose(ps_x[:, u, k * 128:(k + 1) * 128], rows[:, u, k * HALF:(k + 1) * HALF], ident[:, :])
                mm.then_inc(x_turned, 1)

            def expert_of(j):
                return pe.value_load(table_int[0:1, 0, bass.ds(j, 1)], min_val=0, max_val=EXPERTS - 1)

            def first_layer(j, u, rounds):
                e = expert_of(j)
                if rounds:
                    pe.wait_ge(h_ready, j - 1)
                pe.wait_ge(x_lo_ready, j + 1)
                mm = None
                for k in range(2):
                    hi, lo = (w[:, k, bass.ds(e, 1), :].rearrange("p e i -> p (e i)") for w in (w1_hi, w1_lo))
                    pe.matmul(ps_h[:, u, :], x_lo[:, u, k, :], hi, start=(k == 0), stop=False)
                    pe.matmul(ps_h[:, u, :], x_hi[:, u, k, :], lo, start=False, stop=False)
                    mm = pe.matmul(ps_h[:, u, :], x_hi[:, u, k, :], hi, start=False, stop=(k == 1))
                mm.then_inc(h_mm, 1)

            def turn_h(j, u, rounds):
                if rounds:
                    pe.wait_ge(hT_lo_ready, j - 1)
                pe.wait_ge(h_ready, j + 1)
                for c in range(INNER):
                    mm = pe.transpose(ps_t[:, u, c * 128:(c + 1) * 128], hidden[:, u, c * 128:(c + 1) * 128], ident[:, :])
                mm.then_inc(h_turned, 1)

            def second_layer(j, u, rounds):
                e = expert_of(j)
                if rounds:
                    pe.wait_ge(y_ready, j - 1)
                pe.wait_ge(hT_lo_ready, j + 1)
                for c in range(INNER):
                    hi, lo = (w[:, bass.ds(e, 1), c, :].rearrange("p e d -> p (e d)") for w in (w2_hi, w2_lo))
                    at = slice(c * 128, (c + 1) * 128)
                    pe.matmul(ps_y[:, u, 0:DIM], hT_lo[:, u, at], hi, start=(c == 0), stop=False)
                    pe.matmul(ps_y[:, u, 0:DIM], hT_hi[:, u, at], lo, start=False, stop=False)
                    mm = pe.matmul(ps_y[:, u, 0:DIM], hT_hi[:, u, at], hi, start=False, stop=(c == INNER - 1))
                mm.then_inc(y_mm, 1)

            def tile(j, u, more, rounds):
                turn_h(j - 1, 1 - u, rounds)
                first_layer(j, u, rounds)
                if more:
                    turn_x(j + 1, 1 - u, rounds)
                second_layer(j - 1, 1 - u, rounds)

            turn_x(0, 0, False)
            first_layer(0, 0, False)
            turn_x(1, 1, False)
            tile(1, 1, True, False)
            tile(2, 0, True, False)
            with pe.Fori(0, (BLOCKS - 4) // 2) as it:
                for u in (1, 0):
                    tile(it * 2 + 4 - u, u, True, True)
            tile(BLOCKS - 1, 1, False, True)
            turn_h(BLOCKS - 1, 1, True)
            second_layer(BLOCKS - 1, 1, True)


def combine(nc, h2_dram, results_dram, picks, pick_probs, importance, out):
    with ExitStack() as ctx:
        def sb(name, shape, dt=F32):
            return ctx.enter_context(nc.sbuf_tensor(name, shape, dt))

        def sem(name):
            return ctx.enter_context(nc.semaphore(name))

        ones = sb("onesC", [128, 128])
        running = sb("running", [128, EXPERTS])
        TILES = IMAGES * NTILES * TOPK
        of_pick = sb("of_pickC", [128, TILES, EXPERTS])
        balance = sb("balance", [128, TILES])
        share = sb("share", [128, TILES // TOPK, TOPK])
        whole = sb("whole", [128, TILES // TOPK, 1])
        weight = sb("weight", [128, IMAGES, NTILES, TOPK])
        now = sb("now", [128, 2, NTILES, TOPK])
        base = sb("base", [128, 2, NTILES, DIM])
        part = sb("part", [128, 2, TOPK, NTILES, DIM])
        ps = ctx.enter_context(nc.psum_tensor("ps_c", [128, BANK], F32))

        ones_ready, summed, step = sem("ones_ready"), sem("summedC"), sem("stepC")
        loaded = [sem(f"loaded{i}") for i in range(2)]
        now_ready = sem("now_ready")
        added = sem("added")
        out_stored = [sem(f"out_stored{i}") for i in range(2)]
        PARTS = [(0, 2, PTILE), (2, 3, TEXT)]

        block = ctx.enter_context(nc.Block())

        @block.tensor
        def _(pe):
            pe.wait_ge(ones_ready, 1)
            for t, rows in enumerate(TILE_ROWS):
                mm = pe.matmul(ps[:, 0:EXPERTS], ones[0:rows, :], importance[0:rows, t, :], start=(t == 0), stop=(t == 2))
            mm.then_inc(summed, 1)

        def patch_rows(dram, i, at):
            return dram[bass.ds(at, 2 * PTILE), :].rearrange("(t p) d -> p t d", t=2)

        @block.sync
        def _(sp):
            def load(i, u):
                for dst, dram, at in [(base[:, u], h2_dram, 0), (part[:, u, 0], results_dram, 0), (part[:, u, 1], results_dram, TOKENS)]:
                    sp.dma_start(dst[0:PTILE, 0:2, :], patch_rows(dram, i, at + i * N)).then_inc(loaded[u], 16)
                    sp.dma_start(dst[:, 2, :], dram[bass.ds(at + i * N + 2 * PTILE, TEXT), :]).then_inc(loaded[u], 16)

            load(0, 0)
            load(1, 1)
            with sp.Fori(0, IMAGES // 2 - 1) as it:
                for u in range(2):
                    i = it * 2 + u
                    sp.wait_ge(out_stored[u], 48 * (it + 1))
                    sp.nop(nofuse=True)
                    load(i + 2, u)

        @block.scalar
        def _(act):
            def store(i, u):
                act.wait_ge(added, 4 * (i + 1))
                patches = out[bass.ds(i, 1), 0:2 * PTILE, :].rearrange("a (g w) d -> w (a g) d", w=GRID)
                for t in range(2):
                    act.dma_start(patches[t * TILE_COLS:(t + 1) * TILE_COLS, :, :], base[0:PTILE, u, t, :]).then_inc(out_stored[u], 16)
                act.dma_start(out[bass.ds(i, 1), 2 * PTILE:N, :].rearrange("a p d -> (a p) d"), base[:, u, 2, :]).then_inc(out_stored[u], 16)

            with act.Fori(0, IMAGES // 2) as it:
                for u in range(2):
                    store(it * 2 + u, u)
            for u in range(2):
                act.wait_ge(out_stored[u], 48 * IMAGES // 2)

        @block.vector
        def _(dve):
            n = 0

            def chained(instruction):
                nonlocal n
                n += 1
                instruction.then_inc(step, 1)
                dve.wait_ge(step, n)

            dve.memset(ones[:, :], 1.0).then_inc(ones_ready, 1)
            dve.wait_ge(summed, 1)
            chained(dve.tensor_scalar(running[:, :], ps[:, 0:EXPERTS], 1.0, 1.0 - 0.9, ALU.subtract, ALU.mult))
            chained(dve.tensor_scalar(running[:, :], running[:, :], 1.0, 0.01, ALU.add, ALU.add))
            chained(dve.tensor_tensor(of_pick[:, :, :], picks[:, :, :, :, :].rearrange("p i t k e -> p (i t k) e"),
                                      running[:, :].rearrange("p (t e) -> p t e", t=1).to_broadcast([128, TILES, EXPERTS]), ALU.mult))
            chained(dve.tensor_reduce(balance[:, :], of_pick[:, :, :], AX, ALU.add))
            chained(dve.reciprocal(balance[:, :], balance[:, :]))
            flat = share[:, :, :].rearrange("p n k -> p (n k)")
            chained(dve.tensor_tensor(flat, pick_probs[:, :, :, :].rearrange("p i t k -> p (i t k)"), balance[:, :], ALU.mult))
            chained(dve.tensor_reduce(whole[:, :, 0], share[:, :, :], AX, ALU.add))
            chained(dve.reciprocal(whole[:, :, :], whole[:, :, :]))
            chained(dve.tensor_tensor(weight[:, :, :, :].rearrange("p i t k -> p (i t) k"), share[:, :, :],
                                      whole[:, :, :].to_broadcast([128, TILES // TOPK, TOPK]), ALU.mult))

            def add(i, u, it):
                dve.tensor_copy(now[:, u, :, :], weight[:, bass.ds(i, 1), :, :].rearrange("p i t k -> p (i t) k")).then_inc(now_ready, 1)
                dve.wait_ge(loaded[u], 96 * (it + 1))
                dve.nop(nofuse=True)
                dve.wait_ge(now_ready, i + 1)
                dve.nop(nofuse=True)
                for k in range(TOPK):
                    if k:
                        dve.wait_ge(added, 4 * i + 2)
                    for a, b, rows in PARTS:
                        for t in range(a, b):
                            mm = dve.scalar_tensor_tensor(out=base[0:rows, u, t, :], in0=part[0:rows, u, k, t, :],
                                                          scalar=now[0:rows, u, t, k:k + 1], in1=base[0:rows, u, t, :],
                                                          op0=ALU.mult, op1=ALU.add)
                        mm.then_inc(added, 1)

            with dve.Fori(0, IMAGES // 2) as it:
                for u in range(2):
                    add(it * 2 + u, u, it)


def program(nc, x, txt, gamma, beta, W, b, basis_w, core, head_residual, value_w, value_b, router_w, w1, w2, out):
    gw_dram = nc.dram_tensor("gamma_w", (FEATURES, DIM), F32, kind="Internal").ap()
    h_dram = nc.dram_tensor("h", (IMAGES, N, DIM), F32, kind="Internal").ap()
    h2_dram = nc.dram_tensor("h2", (TOKENS, DIM), F32, kind="Internal").ap()
    rows_dram = nc.dram_tensor("rows_by_expert", (EXPERTS * SPACE + SPARE * 128, ROW), F32, kind="Internal").ap()
    results_dram = nc.dram_tensor("results", (RESULTS, DIM), F32, kind="Internal").ap()
    with ExitStack() as ctx:
        def sb(name, shape):
            return ctx.enter_context(nc.sbuf_tensor(name, shape, F32))

        picks = sb("picks", [128, IMAGES, NTILES, TOPK, EXPERTS])
        pick_probs = sb("pick_probs", [128, IMAGES, NTILES, TOPK])
        places = sb("places", [128, EXPERTS])
        importance = sb("importance", [128, NTILES, EXPERTS])
        tokenize(nc, x, gamma, beta, W, b, gw_dram, h_dram)
        attention(nc, txt, basis_w, core, head_residual, value_w, value_b, router_w, h_dram,
                  h2_dram.rearrange("(i n) d -> i n d", i=IMAGES), rows_dram, (picks, pick_probs, places, importance))
        experts(nc, w1, w2, rows_dram, results_dram, places)
        combine(nc, h2_dram, results_dram, picks, pick_probs, importance, out)


_INS = ["x", "txt", "L0_tok_gamma", "L0_tok_beta", "L0_tok_W", "L0_tok_b", "L0_attn_basis_w", "L0_attn_core",
        "L0_attn_head_residual", "L0_attn_value_w", "L0_attn_value_b", "L0_ffn_router_w", "L0_ffn_w1", "L0_ffn_w2"]


def kernel(**inputs):
    import numpy as _np
    import concourse.bacc as _bacc
    from concourse import mybir as _mybir
    from concourse.bass_utils import run_bass_kernel_spmd as _run

    nc = _bacc.Bacc("TRN2", target_bir_lowering=False, num_devices=1)
    arrays, args = {}, []
    for name in _INS:
        a = _np.ascontiguousarray(inputs[name])
        arrays[f"in_{name}"] = a
        args.append(nc.dram_tensor(f"in_{name}", a.shape, _mybir.dt.from_np(a.dtype), kind="ExternalInput").ap())
    out = nc.dram_tensor("out_dram", (IMAGES, N, DIM), _mybir.dt.float32, kind="ExternalOutput").ap()
    program(nc, *args, out)
    r = _run(nc, [arrays], core_ids=[0])
    return r.results[0]["out_dram"]
```

```python
from contextlib import ExitStack

import concourse.bass as bass
from concourse import mybir

F32 = mybir.dt.float32
F32R = mybir.dt.float32r
I32 = mybir.dt.int32
BF16 = mybir.dt.bfloat16
ALU = mybir.AluOpType
ACT = mybir.ActivationFunctionType
AX = mybir.AxisListType.X

IMAGES, SIDE, CH = 16, 224, 3
TEXT, DIM = 128, 192
PATCH = 16
GRID = SIDE // PATCH
SHIFTS = 5
FEATURES = PATCH * PATCH * SHIFTS * CH
TOK_EPS = 0.001

HALO = PATCH + 2
WIN = HALO * CH
BATCH_IMAGES = 8
BATCHES = IMAGES // BATCH_IMAGES
ROWP = BATCH_IMAGES * GRID
LINE = SIDE * CH
PADLINE = LINE + 2 * CH
CHUNK = 2 * WIN
CHUNKS = HALO // 2
TGROUP = 3

TILE_COLS = GRID // 2
PTILE = TILE_COLS * GRID
N = GRID * GRID + TEXT
SLOTS = 2
STEPS = BATCHES * GRID


def tokenize(nc, x, gamma, beta, W, b, h_dram):
    with ExitStack() as ctx:
        def sb(name, shape, dt=F32):
            return ctx.enter_context(nc.sbuf_tensor(name, shape, dt))

        def psum(name, shape, dt=F32):
            return ctx.enter_context(nc.psum_tensor(name, shape, dt))

        def sem(name):
            return ctx.enter_context(nc.semaphore(name))

        lines = sb("lines", [ROWP, BATCHES, HALO, PADLINE])
        w_shift = lines[0:CHUNK, BATCHES - 1, :, :].rearrange("p r l -> p (r l)")[:, 0:SHIFTS * CHUNKS * DIM] \
            .rearrange("p (s t d) -> p s t d", s=SHIFTS, t=CHUNKS)
        factors_raw = sb("factors_raw", [2 * PATCH, 2, FEATURES // PATCH])
        of_half = sb("of_half", [2 * PATCH, 2])
        spread = sb("spread", [2 * PATCH, 2, SHIFTS, 2, HALO, CH])
        pick_row = sb("pick_row", [2 * PATCH, 3, CHUNKS])
        pick_half = sb("pick_half", [2 * PATCH, 3, CHUNKS])
        factors = sb("factors", [CHUNK, 2, SHIFTS, CHUNKS])
        b_row = sb("b_row", [ROWP, DIM])
        bias = sb("bias", [ROWP, DIM])
        w_sum = sb("w_sum", [CHUNK, CHUNKS, DIM])
        w_hi = sb("w_hi", [CHUNK, CHUNKS, DIM], F32R)
        w_lo = sb("w_lo", [CHUNK, CHUNKS, DIM], F32R)
        count = sb("count", [ROWP, HALO, HALO, CH])
        count_rows = count[:, :, :, :].rearrange("p r q c -> p r (q c)")
        zeros = sb("zeros", [BATCH_IMAGES, LINE])
        ident = sb("ident0", [128, 128])
        eps = sb("eps0", [128, 1])
        win = sb("win", [ROWP, SLOTS, HALO, WIN])
        centred = sb("centred", [ROWP, SLOTS, HALO, WIN])
        square = sb("square", [ROWP, SLOTS, HALO, WIN])
        negmean = sb("negmean", [ROWP, SLOTS])
        var = sb("var", [ROWP, SLOTS])
        logvar = sb("logvar", [ROWP, SLOTS])
        rstd = sb("rstd", [ROWP, SLOTS])
        newton = sb("newton0", [ROWP, SLOTS, 2])
        winT_hi = sb("winT_hi", [CHUNK, SLOTS, CHUNKS, ROWP], F32R)
        winT_lo = sb("winT_lo", [CHUNK, SLOTS, CHUNKS, ROWP], F32R)
        tok = sb("tok", [ROWP, SLOTS, DIM])
        psT = psum("psT", [CHUNK, SLOTS, CHUNKS // TGROUP, 512])
        psO = psum("psO", [ROWP, SLOTS, 512])

        lines_clear = sem("lines_clear")
        zeros_ready = sem("zeros_ready")
        shift_clear = sem("shift_clear")
        consts = sem("consts")
        const_step = sem("const_step")
        pick_ready = sem("pick_ready")
        picked = sem("picked0")
        lines_in = [sem(f"lines_in{i}") for i in range(BATCHES)]
        edges_in = sem("edges_in")
        f_in = sem("f_in")
        b_in = sem("b_in")
        spread_ready = sem("spread_ready")
        factors_mm = sem("factors_mm")
        factors_ready = sem("factors_ready")
        shift_in = [sem(f"shift_in{i}") for i in range(SHIFTS)]
        w_summed = sem("w_summed")
        w_hi_ready = sem("w_hi_ready")
        w_lo_ready = sem("w_lo_ready")
        bias_mm = sem("bias_mm")
        bias_ready = sem("bias_ready")
        win_ready = sem("win_ready")
        mean_ready = sem("mean_ready")
        centred_ready = sem("centred_ready")
        square_ready = sem("square_ready")
        var_ready = sem("var_ready")
        log_ready = sem("log_ready")
        rstd_ready = sem("rstd_ready")
        refined = sem("refined0")
        turned = sem("turned")
        hi_ready = sem("hi_ready")
        lo_ready = sem("lo_ready")
        projected = sem("projected")
        tok_ready = sem("tok_ready")
        tok_out = [sem(f"tok_out{i}") for i in range(SLOTS)]

        block = ctx.enter_context(nc.Block())

        def late(step, by):
            return not isinstance(step, int) or step >= by

        def of_slot(step, u, each):
            return (step // SLOTS) * each if isinstance(step, int) else (step - u) * (each // SLOTS)

        def run(engine, body):
            for k in range(-2, 2):
                body(k, k % SLOTS, 0, k + 2)
            with engine.Fori(0, (GRID - 4) // SLOTS) as it:
                for u in range(SLOTS):
                    body(it * SLOTS + u + 2, u, 0, it * SLOTS + u + 4)
            with engine.Fori(0, GRID // SLOTS) as it:
                for u in range(SLOTS):
                    body(it * SLOTS + u + GRID - 2, u, 1, it * SLOTS + u)
            for k in range(STEPS - 2, STEPS + 1):
                body(k, k % SLOTS, None, None)

        def valid(step):
            return not isinstance(step, int) or 0 <= step < STEPS

        def load_lines(q, bi, rows=range(0, PATCH, 4)):
            i0 = bi * BATCH_IMAGES
            own = x[i0:i0 + BATCH_IMAGES].rearrange("i (g r) w c -> (i g) r (w c)", r=PATCH)
            for r0 in rows:
                q.dma_start(lines[:, bi, 1 + r0:5 + r0, CH:CH + LINE], own[:, r0:r0 + 4, :]) \
                    .then_inc(lines_in[bi], 16)

        def load_neighbours(q, bi):
            i0 = bi * BATCH_IMAGES
            own = x[i0:i0 + BATCH_IMAGES].rearrange("i (g r) w c -> (i g) r (w c)", r=PATCH)
            q.dma_start(lines[1:ROWP, bi, 0, CH:CH + LINE], own[0:ROWP - 1, PATCH - 1, :]).then_inc(edges_in, 16)
            q.dma_start(lines[0:ROWP - 1, bi, HALO - 1, CH:CH + LINE], own[1:ROWP, 0, :]).then_inc(edges_in, 16)
            q.wait_ge(edges_in, 32 * (bi + 1))
            q.dma_start(lines[0:ROWP:GRID, bi, 0, CH:CH + LINE], zeros[:, :]).then_inc(lines_in[bi], 16)
            q.dma_start(lines[GRID - 1:ROWP:GRID, bi, HALO - 1, CH:CH + LINE], zeros[:, :]).then_inc(lines_in[bi], 16)

        LINES_LANDED = 16 * (4 + 2)

        SOURCE = [(1, 1), (1, 0), (1, 2), (0, 1), (2, 1)]
        w5 = W.rearrange("(h w s c) d -> h w s c d", h=PATCH, w=PATCH, s=SHIFTS)

        def load_shifted(q, s):
            dr, dc = SOURCE[s]
            for odd in range(2):
                t0 = (dr - odd + 1) // 2
                h0 = 2 * t0 + odd - dr
                for c in range(CH):
                    p = (odd * HALO + dc) * CH + c
                    q.dma_start(w_shift[p:p + (PATCH - 1) * CH + 1:CH, s, t0:t0 + PATCH // 2, :],
                                w5[h0:PATCH:2, :, s, c, :].rearrange("t w d -> w t d")) \
                        .then_inc(shift_in[s], 16)

        SHIFTED_LANDED = 16 * 2 * CH

        @block.sync
        def _(sp):
            sp.dma_start(factors_raw[0:PATCH, 0, :], gamma.rearrange("(h f) -> h f", h=PATCH)).then_inc(f_in, 16)
            sp.dma_start(factors_raw[PATCH:2 * PATCH, 0, :], gamma.rearrange("(h f) -> h f", h=PATCH)).then_inc(f_in, 16)
            load_lines(sp, 0)
            for s in range(0, SHIFTS, 2):
                sp.wait_ge(shift_clear, s + 1)
                load_shifted(sp, s)
            sp.wait_ge(w_summed, SHIFTS)
            sp.wait_ge(bias_mm, 1)
            load_lines(sp, 1)
            sp.wait_ge(lines_clear, 4)
            load_neighbours(sp, 1)
            for bi in range(BATCHES):
                with sp.Fori(0, GRID // SLOTS) as i:
                    for u in range(SLOTS):
                        column = i * SLOTS + u
                        out = h_dram[bi * BATCH_IMAGES:(bi + 1) * BATCH_IMAGES, bass.ds(column * GRID, GRID), :]
                        sp.wait_ge(tok_ready, bi * GRID + column + 1)
                        sp.dma_start(out, tok[:, u, :]).then_inc(tok_out[u], 16)
            for u in range(SLOTS):
                sp.wait_ge(tok_out[u], 16 * (STEPS // SLOTS))

        @block.gpsimd
        def _(pool):
            def clear(bi):
                pool.memset(lines[:, bi, 0:HALO:HALO - 1, :], 0.0).then_inc(lines_clear, 1)
                pool.memset(lines[:, bi, 1:HALO - 1, 0:CH], 0.0).then_inc(lines_clear, 1)
                pool.memset(lines[:, bi, 1:HALO - 1, PADLINE - CH:PADLINE], 0.0).then_inc(lines_clear, 1)

            pool.memset(lines[:, 0, 0:HALO:HALO - 1, :], 0.0).then_inc(lines_clear, 1)
            pool.memset(pick_row[:, :, :], 0.0).then_inc(pick_ready, 1)
            pool.memset(pick_half[:, :, :], 0.0).then_inc(pick_ready, 1)
            pool.memset(of_half[:, :], 0.0).then_inc(pick_ready, 1)
            pool.wait_ge(pick_ready, 3)
            for rows, base in ((pick_row, 0), (pick_half, PATCH + 1)):
                pool.affine_select(out=rows[:, :, :], in_=rows[:, :, :], compare_op=ALU.not_equal, fill=1.0,
                                   base=base, pattern=[[-1, 3], [2, CHUNKS]], channel_multiplier=-1).then_inc(pick_ready, 1)
            pool.affine_select(out=of_half[:, 0:1], in_=of_half[:, 0:1], compare_op=ALU.is_ge, fill=1.0,
                               base=-PATCH, pattern=[[0, 1]], channel_multiplier=1).then_inc(pick_ready, 1)
            pool.affine_select(out=of_half[:, 1:2], in_=of_half[:, 1:2], compare_op=ALU.is_ge, fill=1.0,
                               base=PATCH - 1, pattern=[[0, 1]], channel_multiplier=-1).then_inc(pick_ready, 1)
            pool.memset(lines[:, 0, 1:HALO - 1, 0:CH], 0.0).then_inc(consts, 1)
            pool.memset(lines[:, 0, 1:HALO - 1, PADLINE - CH:PADLINE], 0.0).then_inc(consts, 1)
            pool.memset(eps[:, :], TOK_EPS).then_inc(consts, 1)
            pool.memset(ident[:, :], 0.0).then_inc(const_step, 1)
            pool.wait_ge(const_step, 1)
            pool.affine_select(out=ident[:, :], in_=ident[:, :], compare_op=ALU.not_equal, fill=1.0,
                               base=0, pattern=[[-1, 128]], channel_multiplier=1).then_inc(consts, 1)
            end = PATCH + 1
            regions = [((0, HALO), (0, HALO), 0.0), ((1, end), (0, HALO), 1.0), ((0, HALO), (1, end), 1.0),
                       ((1, end), (1, end), 4.0), ((2, end - 1), (2, end - 1), 5.0),
                       ((1, 2), (1, 2), 3.0), ((1, 2), (end - 1, end), 3.0),
                       ((end - 1, end), (1, 2), 3.0), ((end - 1, end), (end - 1, end), 3.0)]
            for n, (r, q, v) in enumerate(regions):
                pool.wait_ge(const_step, 1 + n)
                last = n == len(regions) - 1
                pool.memset(count[:, r[0]:r[1], q[0]:q[1], :], v).then_inc(consts if last else const_step, 1)

            def window(s, u, bi, column):
                if late(s, SLOTS):
                    pool.wait_ge(mean_ready, s - 1)
                pool.nop(nofuse=True)
                pool.tensor_copy(win[:, u, :, :], lines[:, bi, :, bass.ds(column * (PATCH * CH), WIN)]).then_inc(win_ready, 1)

            pool.wait_ge(lines_in[0], LINES_LANDED)
            for s in range(SLOTS):
                window(s, s, 0, s)
            pool.wait_ge(w_summed, SHIFTS)
            pool.wait_ge(bias_mm, 1)
            clear(1)
            with pool.Fori(1, GRID // SLOTS) as it:
                for u in range(SLOTS):
                    window(it * SLOTS + u, u, 0, it * SLOTS + u)
            pool.wait_ge(lines_in[1], LINES_LANDED)
            with pool.Fori(0, GRID // SLOTS) as it:
                for u in range(SLOTS):
                    window(it * SLOTS + u + GRID, u, 1, it * SLOTS + u)

        CONSTS = 5

        @block.scalar
        def _(act):
            act.dma_start(factors_raw[0:PATCH, 1, :], beta.rearrange("(h f) -> h f", h=PATCH)).then_inc(f_in, 16)
            act.dma_start(factors_raw[PATCH:2 * PATCH, 1, :], beta.rearrange("(h f) -> h f", h=PATCH)).then_inc(f_in, 16)
            act.preload_act_table_set("natural_log_exp_and_others")
            act.dma_start(b_row[:, :], b.rearrange("(a d) -> a d", a=1).to_broadcast([ROWP, DIM])).then_inc(b_in, 16)
            act.wait_ge(lines_clear, 1)
            act.wait_ge(zeros_ready, 1)
            load_neighbours(act, 0)
            for s in range(1, SHIFTS, 2):
                act.wait_ge(shift_clear, s + 1)
                load_shifted(act, s)
            act.wait_ge(consts, CONSTS)

            def centre(s, u, bi, column):
                act.wait_ge(mean_ready, s + 1)
                if late(s, SLOTS):
                    act.wait_ge(turned, s - 1)
                act.nop(nofuse=True)
                window = lines[:, bi, :, bass.ds(column * (PATCH * CH), WIN)]
                act.activation(centred[:, u, :, :], window, ACT.Identity, bias=negmean[:, u:u + 1]).then_inc(centred_ready, 1)
                act.wait_ge(centred_ready, s + 1)
                act.activation(square[:, u, :, :], centred[:, u, :, :], ACT.Square).then_inc(square_ready, 1)

            def split_hi(s, u):
                act.wait_ge(turned, s + 1)
                if late(s, SLOTS):
                    act.wait_ge(projected, s - 1)
                act.activation(winT_hi[:, u, :, :].rearrange("k (g t) p -> k g (t p)", t=TGROUP),
                               psT[:, u, :, 0:TGROUP * ROWP], ACT.Copy).then_inc(hi_ready, 1)

            def scale(s, u):
                act.wait_ge(var_ready, s + 1)
                act.activation(logvar[:, u:u + 1], var[:, u:u + 1], ACT.Ln, bias=eps[0:ROWP, :]).then_inc(log_ready, 1)
                if late(s, SLOTS):
                    act.wait_ge(refined, 4 * (s - 1))
                act.wait_ge(log_ready, s + 1)
                act.activation(rstd[:, u:u + 1], logvar[:, u:u + 1], ACT.Exp, scale=-0.5).then_inc(rstd_ready, 1)

            def body(k, u, bi, column):
                if isinstance(k, int) and k == 0:
                    act.wait_ge(w_summed, SHIFTS)
                    act.activation(w_hi[:, :, :], w_sum[:, :, :], ACT.Copy).then_inc(w_hi_ready, 1)
                if valid(k):
                    split_hi(k, u)
                if bi is not None:
                    centre(k + 2, u, bi, column)
                if valid(k):
                    scale(k, u)

            run(act, body)

        @block.vector
        def _(dve):
            dve.memset(w_shift[:, 0, :, :], 0.0).then_inc(shift_clear, 1)
            dve.memset(zeros[:, :], 0.0).then_inc(zeros_ready, 1)
            dve.memset(w_shift[:, 1, :, :], 0.0).then_inc(shift_clear, 1)
            dve.memset(spread[:, :, :, :, :, :], 0.0).then_inc(picked, 1)
            for s in range(2, SHIFTS):
                dve.memset(w_shift[:, s, :, :], 0.0).then_inc(shift_clear, 1)
            dve.wait_ge(f_in, 64)
            dve.wait_ge(pick_ready, 7)
            dve.wait_ge(picked, 1)
            for s, (_, dc) in enumerate(SOURCE):
                for half in range(2):
                    for k in range(2):
                        dve.tensor_scalar(spread[:, k, s, half, dc:dc + PATCH, :],
                                          factors_raw[:, k, :].rearrange("h (w s c) -> h w s c", w=PATCH, s=SHIFTS)[:, :, s, :],
                                          of_half[:, half:half + 1], None, ALU.mult)
            dve.tensor_scalar(pick_row[:, :, :], pick_row[:, :, :], of_half[:, 0:1], None, ALU.mult).then_inc(picked, 1)
            dve.wait_ge(picked, 2)
            dve.scalar_tensor_tensor(out=pick_row[:, :, :], in0=pick_half[:, :, :], scalar=of_half[:, 1:2], in1=pick_row[:, :, :],
                                     op0=ALU.mult, op1=ALU.add).then_inc(spread_ready, 1)
            dve.wait_ge(factors_mm, 1)
            dve.tensor_copy(factors[:, :, :, :].rearrange("p k s t -> p (k s t)"), psO[0:CHUNK, 1, 0:2 * SHIFTS * CHUNKS]).then_inc(factors_ready, 1)
            dve.wait_ge(factors_ready, 1)
            for s in range(SHIFTS):
                dve.wait_ge(shift_in[s], SHIFTED_LANDED)
                if s:
                    dve.wait_ge(w_summed, s)
                for t in range(CHUNKS):
                    if s == 0:
                        mm = dve.tensor_scalar(w_sum[:, t, :], w_shift[:, s, t, :], factors[:, 0, s, t:t + 1], None, ALU.mult)
                    else:
                        mm = dve.scalar_tensor_tensor(out=w_sum[:, t, :], in0=w_shift[:, s, t, :], scalar=factors[:, 0, s, t:t + 1],
                                                      in1=w_sum[:, t, :], op0=ALU.mult, op1=ALU.add)
                mm.then_inc(w_summed, 1)
            dve.wait_ge(consts, CONSTS)

            def mean(s, u):
                if late(s, SLOTS):
                    dve.wait_ge(var_ready, s - 1)
                    dve.wait_ge(square_ready, s - 1)
                dve.wait_ge(win_ready, s + 1)
                dve.tensor_tensor_reduce(square[:, u, :, :], win[:, u, :, :], count_rows, -1.0 / FEATURES, 0.0,
                                         ALU.mult, ALU.add, negmean[:, u:u + 1]).then_inc(mean_ready, 1)

            def split_lo(s, u):
                dve.wait_ge(hi_ready, s + 1)
                dve.tensor_tensor(winT_lo[:, u, :, :].rearrange("k (g t) p -> k g (t p)", t=TGROUP),
                                  psT[:, u, :, 0:TGROUP * ROWP],
                                  winT_hi[:, u, :, :].rearrange("k (g t) p -> k g (t p)", t=TGROUP).bitcast(F32),
                                  ALU.subtract).then_inc(lo_ready, 1)

            def variance(s, u):
                dve.wait_ge(square_ready, s + 1)
                dve.tensor_tensor_reduce(square[:, u, :, :], square[:, u, :, :], count_rows, 1.0 / FEATURES, 0.0,
                                         ALU.mult, ALU.add, var[:, u:u + 1]).then_inc(var_ready, 1)

            def refine(s, u, part):
                y, a, scale = rstd[:, u:u + 1], newton[:, u, 0:1], newton[:, u, 1:2]
                if part == 0:
                    dve.wait_ge(rstd_ready, s + 1)
                    step = dve.tensor_tensor(a, y, y, ALU.mult)
                else:
                    dve.wait_ge(refined, 4 * s + part)
                if part == 1:
                    step = dve.scalar_tensor_tensor(out=a, in0=var[:, u:u + 1], scalar=TOK_EPS, in1=a, op0=ALU.add, op1=ALU.mult)
                if part == 2:
                    step = dve.tensor_scalar(a, a, -0.5, 1.5, ALU.mult, ALU.add)
                if part == 3:
                    step = dve.tensor_tensor(scale, y, a, ALU.mult)
                step.then_inc(refined, 1)

            def finish(s, u):
                if late(s, SLOTS):
                    dve.wait_ge(tok_out[u], of_slot(s, u, 16))
                dve.wait_ge(refined, 4 * s + 4)
                dve.wait_ge(projected, s + 1)
                dve.scalar_tensor_tensor(out=tok[:, u, :], in0=psO[:, u, 0:DIM], scalar=newton[:, u, 1:2], in1=bias[:, :],
                                         op0=ALU.mult, op1=ALU.add).then_inc(tok_ready, 1)

            def body(k, u, bi, column):
                if isinstance(k, int) and k == 0:
                    dve.wait_ge(w_hi_ready, 1)
                    dve.tensor_tensor(w_lo[:, :, :], w_sum[:, :, :], w_hi[:, :, :].bitcast(F32), ALU.subtract).then_inc(w_lo_ready, 1)
                    dve.wait_ge(bias_mm, 1)
                    dve.wait_ge(b_in, 16)
                    dve.tensor_tensor(bias[:, :], psO[:, 0, 0:DIM], b_row[:, :], ALU.add).then_inc(bias_ready, 1)
                last = valid(k - 1)
                if bi is not None:
                    mean(k + 2, u)
                if last:
                    refine(k - 1, 1 - u, 0)
                if valid(k):
                    split_lo(k, u)
                if last:
                    refine(k - 1, 1 - u, 1)
                    refine(k - 1, 1 - u, 2)
                if valid(k + 1):
                    variance(k + 1, 1 - u)
                if last:
                    refine(k - 1, 1 - u, 3)
                    finish(k - 1, 1 - u)

            run(dve, body)

        @block.tensor
        def _(pe):
            pe.wait_ge(spread_ready, 1)
            for k in range(2):
                for s, (dr, _) in enumerate(SOURCE):
                    at = (k * SHIFTS + s) * CHUNKS
                    mm = pe.matmul(psO[0:CHUNK, 1, at:at + CHUNKS], spread[:, k, s, :, :, :].rearrange("h a q c -> h (a q c)"),
                                   pick_row[:, dr, :], start=True, stop=True)
            mm.then_inc(factors_mm, 1)
            pe.wait_ge(factors_ready, 1)
            for s in range(SHIFTS):
                pe.wait_ge(shift_in[s], SHIFTED_LANDED)
                for t in range(CHUNKS):
                    mm = pe.matmul(psO[:, 0, 0:DIM], factors[:, 1, s, t:t + 1].to_broadcast([CHUNK, ROWP]), w_shift[:, s, t, :],
                                   start=(s == 0 and t == 0), stop=(s == SHIFTS - 1 and t == CHUNKS - 1))
            mm.then_inc(bias_mm, 1)
            pe.wait_ge(consts, CONSTS)

            def turn(s, u):
                if late(s, SLOTS):
                    pe.wait_ge(lo_ready, s - 1)
                pe.wait_ge(centred_ready, s + 1)
                flat = centred[:, u, :, :].rearrange("p r w -> p (r w)")
                for t in range(CHUNKS):
                    g, k = t // TGROUP, t % TGROUP
                    mm = pe.transpose(psT[:, u, g, k * ROWP:(k + 1) * ROWP], flat[:, t * CHUNK:(t + 1) * CHUNK], ident[0:ROWP, 0:ROWP])
                mm.then_inc(turned, 1)

            def project(s, u):
                if late(s, SLOTS):
                    pe.wait_ge(tok_ready, s - 1)
                pe.wait_ge(lo_ready, s + 1)
                for t in range(CHUNKS):
                    hi, lo = winT_hi[:, u, t, :], winT_lo[:, u, t, :]
                    pe.matmul(psO[:, u, 0:DIM], lo, w_hi[:, t, :], start=(t == 0), stop=False)
                    pe.matmul(psO[:, u, 0:DIM], hi, w_lo[:, t, :], start=False, stop=False)
                    mm = pe.matmul(psO[:, u, 0:DIM], hi, w_hi[:, t, :], start=False, stop=(t == CHUNKS - 1))
                mm.then_inc(projected, 1)

            def body(k, u, bi, column):
                if valid(k + 1):
                    turn(k + 1, 1 - u)
                if isinstance(k, int) and k == 0:
                    pe.wait_ge(w_lo_ready, 1)
                    pe.wait_ge(bias_ready, 1)
                if valid(k):
                    project(k, u)

            run(pe, body)


HEADS, RANK = 12, 64
HEAD_DIM = DIM // HEADS
LN_EPS = 1e-5
HALF = DIM // 2
NTILES = 3
TILE_ROWS = [PTILE, PTILE, TEXT]
TILE_AT = [0, PTILE, 2 * PTILE]
KEYS = N // 3
GROUP = 4
GROUPS = HEADS // GROUP
SCORE_SCALE = RANK ** -0.5
BANK = 512
LN_AT, TURN_AT = 5, 6
POST_SCALE, POST_TURN, POST_ROUTE, POST_RANK = 0, 2, 5, 8
POST_PARTS = (4, 6, 9)
EXPERTS, HIDDEN, TOPK = 8, 512, 2
TOKENS = IMAGES * N
ROW = DIM + 1
SPACE = -(-(TOKENS + 127) // 128) * 128
BLOCKS = (TOPK * TOKENS + EXPERTS * 127) // 128
SPARE = BLOCKS - -(-TOPK * TOKENS // 128)
MASKED = -3e38
PIECES = [(c, max(a, c * N), min(a + BANK, (c + 1) * N))
          for a in (0, BANK) for c in range(3) if max(a, c * N) < min(a + BANK, (c + 1) * N)]


def attention(nc, txt, basis_w, core, head_residual, value_w, value_b, router_w, h_dram, h2_dram, rows_dram, kept):
    picks, pick_probs, places, importance = kept
    with ExitStack() as ctx:
        def sb(name, shape, dt=F32):
            return ctx.enter_context(nc.sbuf_tensor(name, shape, dt))

        def psum(name, shape, dt=F32):
            return ctx.enter_context(nc.psum_tensor(name, shape, dt))

        def sem(name):
            return ctx.enter_context(nc.semaphore(name))

        ident = sb("identA", [128, 128])
        eps = sb("epsA", [128, 1])
        basis_raw = sb("basis_raw", [RANK, DIM])
        basisT = sb("basisT", [HALF, 2, 2, RANK])
        value_raw = sb("value_raw", [HALF, 2, DIM])
        valueT = sb("valueT", [HALF, 2, DIM])
        value_bias = sb("value_bias", [KEYS, DIM])
        residual = sb("residual", [128, HEADS, RANK])
        core_sb = sb("core_sb", [128, RANK])
        mean_mat = sb("mean_mat", [128, RANK])
        mats_hi = sb("mats_hi", [128, HEADS, 2, RANK], F32R)
        mats_lo = sb("mats_lo", [128, HEADS, 2, RANK], F32R)

        h_front = sb("h_front", [128, 2, NTILES, DIM])
        h_back = sb("h_back", [128, 2, NTILES, DIM])
        stats = sb("stats", [128, NTILES, 6])
        moments = sb("moments", [128, NTILES, 2])
        logvar = sb("logvarA", [128, NTILES])
        rstd = sb("rstdA", [128, NTILES])
        newton = sb("newton", [128, 3, NTILES])
        xn = sb("xn", [128, NTILES, DIM])
        xT = sb("xT", [HALF, 2, N])
        lat = sb("lat", [128, 2, N], F32R)
        lat_one = sb("lat_one", [RANK + 1, 2, N], F32R)
        values = sb("values", [KEYS, 2, 3, HEADS, 32])
        q_hi = sb("q_hi", [128, 2, HEADS, N], F32R)
        q_lo = sb("q_lo", [RANK + 1, 2, HEADS, N], F32R)
        row_max = sb("row_max", [KEYS, 2, 3, HEADS])
        max_rows = sb("max_rows", [HEADS, N], F32R)
        probs = sb("probs", [KEYS, 2 * GROUP, 3 * N])
        ctx_sb = sb("ctx_sb", [128, N])
        recip = sb("recip", [128, NTILES, GROUP, 1])
        scaled = sb("scaled", [128, NTILES, GROUP, HEAD_DIM])

        router_raw = sb("router_raw", [EXPERTS, DIM])
        routerT = sb("routerT", [HALF, 2, EXPERTS])
        before = sb("before", [128, 128], BF16)
        all_ones = sb("all_ones", [128, 128], BF16)
        valid = sb("valid", [128, NTILES])
        order_int = sb("order_int", [128, EXPERTS + TOPK * NTILES], I32)
        order = sb("order", [128, EXPERTS])
        goal = sb("goal", [128, TOPK, NTILES, 1])
        newton2 = sb("newton2", [128, 3, NTILES])
        stats2 = sb("stats2", [128, NTILES, 6])
        moments2 = sb("moments2", [128, NTILES, 2])
        logvar2 = sb("logvar2", [128, NTILES])
        rstd2 = sb("rstd2", [128, NTILES])
        routed = sb("routed", [128, TOPK, NTILES, ROW])
        x2T = sb("x2T", [HALF, 2, N])
        logits = sb("logits", [128, NTILES, EXPERTS])
        rest = sb("rest", [128, NTILES, EXPERTS])
        key = sb("key", [128, NTILES, EXPERTS])
        top = sb("top", [128, NTILES])
        expo = sb("expo", [128, NTILES, EXPERTS])
        total = sb("total", [128, NTILES])
        pick = sb("pick", [128, NTILES, TOPK, EXPERTS])
        picked = sb("picked", [128, NTILES, EXPERTS], BF16)
        of_pick = sb("of_pick", [128, NTILES, TOPK, EXPERTS])
        place = sb("place", [128, NTILES, TOPK])
        place_int = sb("place_int", [128, NTILES, TOPK], I32)

        ps_s = psum("ps_s", [128, 2 * BANK])
        ps_t = psum("ps_t", [128, 2 * BANK])
        ps_q = psum("ps_q", [128, BANK])
        ps_v = psum("ps_v", [128, BANK])
        ps_m = psum("ps_m", [128, 2, BANK])

        one_row = sem("one_row")
        w_in, txt_const, const_step, consts = sem("w_inA"), sem("txt_const"), sem("const_stepA"), sem("constsA")
        w_turned, w_ready, mat_step = sem("w_turned"), sem("w_readyA"), sem("mat_step")
        front_in = [sem(f"front_in{i}") for i in range(2)]
        back_in = [sem(f"back_in{i}") for i in range(2)]
        max_in = [sem(f"max_in{i}") for i in range(2)]
        h2_out = [sem(f"h2_out{i}") for i in range(2)]
        dve_ln = sem("dve_ln")
        act_ln = sem("act_ln")
        refined = sem("refined")
        xn_ready = sem("xn_ready")
        x_turned = sem("x_turned")
        xT_ready = sem("xT_ready")
        lat_mm = sem("lat_mm")
        lat_hi = sem("lat_hi")
        lat_lo = sem("lat_lo")
        lat_one_ready = sem("lat_one_ready")
        v_mm = sem("v_mm")
        v_ready = sem("v_ready")
        q_mm = sem("q_mm")
        q_hi_ready = sem("q_hi_ready")
        q_lo_ready = sem("q_lo_ready")
        s_mm = sem("s_mm")
        max_ready = sem("max_ready")
        max_turned = sem("max_turned")
        max_rows_ready = sem("max_rows_ready")
        t_mm = sem("t_mm")
        probs_ready = sem("probs_ready")
        pv_mm = sem("pv_mm")
        ctx_ready = sem("ctx_ready")
        ctx_turned = sem("ctx_turned")
        recip_ready = sem("recip_ready")
        scaled_ready = sem("scaled_ready")
        h2_ready = sem("h2_ready")

        dve_ln2 = sem("dve_ln2")
        act_ln2 = sem("act_ln2")
        refined2 = sem("refined2")
        x2_ready = sem("x2_ready")
        x2_copied = sem("x2_copied")
        x2_turned = sem("x2_turned")
        x2T_ready = sem("x2T_ready")
        logit_mm = sem("logit_mm")
        route = sem("route")
        expo_ready = sem("expo_ready")
        rank_mm = sem("rank_mm")
        scattered = sem("scattered")
        order_in = sem("order_in")
        order_ready = sem("order_ready")

        block = ctx.enter_context(nc.Block())

        PARTS = [(0, 2, PTILE), (2, 3, TEXT)]

        def run(engine, prologue, body, epilogue):
            prologue()
            body(0, 0, True, True, False)
            body(1, 1, True, True, True)
            with engine.Fori(1, (IMAGES - 2) // 2) as it:
                for p in range(2):
                    body(it * 2 + p, p, True, True, True)
            body(IMAGES - 2, 0, True, False, True)
            body(IMAGES - 1, 1, False, False, True)
            epilogue()

        LOGITS_READ, MAX_TAKEN, PICKED, RANKED, ROUTE_STEPS = 1, 3, 15, 25, 28

        def of_pair(i, p, each):
            return (i // 2 + 1) * each if isinstance(i, int) else (i - p) * (each // 2) + each

        @block.sync
        def _(sp):
            sp.dma_start(basis_raw[:, :], basis_w).then_inc(w_in, 16)
            for d in range(2):
                sp.dma_start(residual[d * RANK:(d + 1) * RANK, :, :], head_residual.rearrange("h r s -> r h s")).then_inc(w_in, 16)
                sp.dma_start(core_sb[d * RANK:(d + 1) * RANK, :], core).then_inc(w_in, 16)
            sp.dma_start(value_raw[:, :, :], value_w.rearrange("(k p) h -> p k h", k=2)).then_inc(w_in, 16)
            sp.dma_start(value_bias[:, :], value_b.rearrange("(a d) -> a d", a=1).to_broadcast([KEYS, DIM])).then_inc(w_in, 16)
            sp.dma_start(router_raw[:, :], router_w).then_inc(w_in, 16)
            sp.wait_ge(consts, 5)

            def load(dst, i, p, landed):
                sp.dma_start(dst[0:PTILE, p, 0:2, :],
                             h_dram[bass.ds(i, 1), 0:2 * PTILE, :].rearrange("a (t p) d -> p (a t) d", t=2)).then_inc(landed[p], 16)
                sp.dma_start(dst[:, p, 2, :], txt[bass.ds(i, 1), :, :].rearrange("a p d -> (a p) d")).then_inc(landed[p], 16)

            def prologue():
                for i in range(2):
                    load(h_front, i, i, front_in)
                    load(h_back, i, i, back_in)

            def body(i, p, front, prep, post):
                if post and front:
                    sp.wait_ge(x2_ready, 3 * i)
                    sp.wait_ge(h2_out[1 - p], of_pair(i - 1, 1 - p, 32))
                    load(h_back, i + 1, 1 - p, back_in)
                if prep:
                    sp.wait_ge(xn_ready, 3 * (i + 1))
                    load(h_front, i + 2, p, front_in)
                if front:
                    sp.wait_ge(max_rows_ready, i + 2)
                    sp.dma_start(q_lo[RANK:RANK + 1, 1 - p, :, :].bitcast(F32), max_rows[:, :].bitcast(F32)).then_inc(max_in[1 - p], 16)
                sp.wait_ge(h2_ready, 2 * GROUPS * (i + 1))
                sp.dma_start(h2_dram[bass.ds(i, 1), 0:2 * PTILE, :].rearrange("a (t p) d -> p (a t) d", t=2),
                             h_back[0:PTILE, p, 0:2, :]).then_inc(h2_out[p], 16)
                sp.dma_start(h2_dram[bass.ds(i, 1), 2 * PTILE:N, :].rearrange("a p d -> (a p) d"), h_back[:, p, 2, :]).then_inc(h2_out[p], 16)

            def first_max():
                sp.wait_ge(max_rows_ready, 1)
                sp.dma_start(q_lo[RANK:RANK + 1, 0, :, :].bitcast(F32), max_rows[:, :].bitcast(F32)).then_inc(max_in[0], 16)

            def prologue2():
                prologue()
                first_max()

            def epilogue():
                for p in range(2):
                    sp.wait_ge(h2_out[p], 32 * IMAGES // 2)

            run(sp, prologue2, body, epilogue)

        @block.gpsimd
        def _(pool):
            pool.memset(ident[:, :], 0.0).then_inc(const_step, 1)
            pool.memset(eps[:, :], LN_EPS).then_inc(consts, 1)
            pool.wait_ge(const_step, 1)
            pool.affine_select(out=ident[:, :], in_=ident[:, :], compare_op=ALU.not_equal, fill=1.0,
                               base=0, pattern=[[-1, 128]], channel_multiplier=1).then_inc(consts, 1)
            pool.memset(h_front[:, :, :, :], 0.0).then_inc(consts, 1)
            pool.memset(h_back[:, :, :, :], 0.0).then_inc(consts, 1)
            pool.memset(values[:, :, :, :, :], 0.0).then_inc(const_step, 1)
            pool.wait_ge(const_step, 2)
            pool.memset(values[:, :, :, :, HEAD_DIM:HEAD_DIM + 1], 1.0).then_inc(consts, 1)

            for k in range(TOPK):
                for t in range(NTILES):
                    at = EXPERTS + k * NTILES + t
                    pool.iota(order_int[:, at:at + 1], [[0, 1]], base=k * TOKENS + TILE_AT[t], channel_multiplier=1).then_inc(order_in, 1)
            pool.iota(order_int[:, 0:EXPERTS], [[-1, EXPERTS]], base=EXPERTS, channel_multiplier=0).then_inc(order_in, 1)
            pool.memset(all_ones[:, :], 1.0).then_inc(order_in, 1)
            pool.memset(valid[:, :], 1.0).then_inc(const_step, 1)
            pool.wait_ge(const_step, 3)
            pool.wait_ge(order_in, 8)
            pool.affine_select(out=before[:, :], in_=all_ones[:, :], compare_op=ALU.is_gt, fill=0.0, base=0,
                               pattern=[[1, 128]], channel_multiplier=-1).then_inc(order_in, 1)
            pool.affine_select(out=valid[:, 0:2], in_=valid[:, 0:2], compare_op=ALU.is_gt, fill=0.0, base=PTILE,
                               pattern=[[0, 2]], channel_multiplier=-1).then_inc(order_in, 1)

            def scatter(i):
                pool.wait_ge(x2_copied, i + 1)
                pool.wait_ge(route, ROUTE_STEPS * (i + 1))
                pool.nop(nofuse=True)
                for t, rows in enumerate(TILE_ROWS):
                    for k in range(TOPK):
                        pool.indirect_dma_start(rows_dram[:, :], bass.IndirectOffsetOnAxis(place_int[0:rows, t, k:k + 1], 0),
                                                routed[0:rows, k, t, :], None).then_inc(scattered, 16)

            def copy(i, p, ready=None):
                if not isinstance(i, int) or i >= 2:
                    pool.wait_ge(t_mm, HEADS * (i - 1))
                pool.wait_ge(lat_lo, i + 1)
                pool.nop(nofuse=True)
                pool.tensor_copy(lat_one[0:RANK, p, :], lat[0:RANK, p, :].bitcast(F32)).then_inc(lat_one_ready, 1)

            def body(i, p, front, prep, post):
                if post:
                    scatter(i - 1)
                if prep:
                    copy(i + 2, p)

            def epilogue():
                scatter(IMAGES - 1)
                pool.wait_ge(scattered, 16 * TOPK * NTILES * IMAGES)

            run(pool, lambda: (copy(0, 0), copy(1, 1)), body, epilogue)

        @block.scalar
        def _(act):
            act.preload_act_table_set("natural_log_exp_and_others")
            act.wait_ge(mat_step, 3)
            act.activation(mats_hi[:, :, :, :],
                           residual[:, :, :].rearrange("p h (a s) -> p h a s", a=1).to_broadcast([128, HEADS, 2, RANK]),
                           ACT.Copy).then_inc(mat_step, 1)
            act.wait_ge(consts, 5)

            def layernorm_scale(i):
                act.wait_ge(dve_ln, 6 * (i + 1))
                act.activation(logvar[:, :], moments[:, :, 1], ACT.Ln, bias=eps[:, :]).then_inc(act_ln, 1)
                act.wait_ge(act_ln, 2 * i + 1)
                act.activation(rstd[:, :], logvar[:, :], ACT.Exp, scale=-0.5).then_inc(act_ln, 1)

            def transposed(i):
                act.wait_ge(x_turned, i + 1)
                act.activation(xT[:, :, :], ps_m[0:HALF, :, 0:N], ACT.Copy).then_inc(xT_ready, 1)

            def latents(i, p):
                act.wait_ge(lat_mm, i + 1)
                act.activation(lat[:, p, :], ps_q[:, 0:N], ACT.Copy).then_inc(lat_hi, 1)

            def query(i, p, h):
                act.wait_ge(q_mm, HEADS * i + h + 1)
                act.activation(q_hi[:, p, h, :], ps_q[:, 0:N], ACT.Copy).then_inc(q_hi_ready, 1)

            def exponentials(i, h, slot, free):
                if free:
                    act.wait_ge(pv_mm, GROUPS * i + h // GROUP - 1)
                act.wait_ge(t_mm, HEADS * i + h + 1)
                act.activation(probs[:, slot, :], ps_t[0:KEYS, 0:3 * N], ACT.Exp, scale=SCORE_SCALE).then_inc(probs_ready, 1)

            def post_scale(i):
                act.wait_ge(dve_ln2, 6 * (i + 1))
                act.activation(logvar2[:, :], moments2[:, :, 1], ACT.Ln, bias=eps[:, :]).then_inc(act_ln2, 1)
                act.wait_ge(act_ln2, 2 * i + 1)
                act.activation(rstd2[:, :], logvar2[:, :], ACT.Exp, scale=-0.5).then_inc(act_ln2, 1)

            def post_copies(i):
                act.wait_ge(x2_ready, 3 * (i + 1))
                act.activation(routed[:, 1, :, 0:DIM], routed[:, 0, :, 0:DIM], ACT.Copy).then_inc(x2_copied, 1)
                act.wait_ge(x2_turned, i + 1)
                act.activation(x2T[:, :, :], ps_m[0:HALF, :, 0:N], ACT.Copy).then_inc(x2T_ready, 1)

            def post_exponentials(i):
                act.wait_ge(route, ROUTE_STEPS * i + MAX_TAKEN)
                act.activation(expo[:, :, :], expo[:, :, :], ACT.Exp).then_inc(expo_ready, 1)

            def prologue():
                for i in range(2):
                    layernorm_scale(i)
                    transposed(i)
                    latents(i, i)
                for h in range(HEADS):
                    query(0, 0, h)

            def body(i, p, front, prep, post):
                for h in range(HEADS):
                    if front:
                        query(i + 1, 1 - p, h)
                    group = GROUPS * p + h // GROUP
                    exponentials(i, h, (group % 2) * GROUP + h % GROUP, not isinstance(i, int) or GROUPS * i + h // GROUP >= 2)
                    if post and h == POST_SCALE:
                        post_scale(i - 1)
                    if post and h == POST_TURN:
                        post_copies(i - 1)
                    if post and h == POST_ROUTE:
                        post_exponentials(i - 1)
                    if prep and h == LN_AT:
                        layernorm_scale(i + 2)
                    if prep and h == TURN_AT:
                        transposed(i + 2)
                if prep:
                    latents(i + 2, p)

            def epilogue():
                post_scale(IMAGES - 1)
                post_copies(IMAGES - 1)
                post_exponentials(IMAGES - 1)

            run(act, prologue, body, epilogue)

        @block.vector
        def _(dve):
            dve.memset(lat_one[RANK:RANK + 1, :, :].bitcast(F32), -1.0).then_inc(one_row, 1)
            dve.wait_ge(w_in, 16 * 8)
            dve.tensor_reduce(mean_mat[:, :], residual[:, :, :].rearrange("p h s -> p s h"), AX, ALU.add).then_inc(mat_step, 1)
            dve.wait_ge(mat_step, 1)
            dve.tensor_tensor(mean_mat[:, :], core_sb[:, :], mean_mat[:, :], ALU.subtract).then_inc(mat_step, 1)
            dve.wait_ge(mat_step, 2)
            dve.scalar_tensor_tensor(out=residual[:, :, :],
                                     in0=mean_mat[:, :].rearrange("p (a s) -> p a s", a=1).to_broadcast([128, HEADS, RANK]),
                                     scalar=1.0 / HEADS, in1=residual[:, :, :], op0=ALU.mult, op1=ALU.add).then_inc(mat_step, 1)
            dve.wait_ge(mat_step, 4)
            dve.tensor_tensor(mats_lo[:, :, :, :],
                              residual[:, :, :].rearrange("p h (a s) -> p h a s", a=1).to_broadcast([128, HEADS, 2, RANK]),
                              mats_hi[:, :, :, :].bitcast(F32), ALU.subtract).then_inc(mat_step, 1)
            dve.wait_ge(w_turned, 1)
            dve.tensor_copy(basisT[:, :, :, :], ps_m[0:HALF, 0, 0:2 * RANK].rearrange("p (k a r) -> p k a r", k=2, a=1)
                            .to_broadcast([HALF, 2, 2, RANK])).then_inc(w_ready, 1)
            dve.tensor_copy(routerT[:, :, :], ps_m[0:HALF, 0, 256:256 + 2 * EXPERTS].rearrange("p (k e) -> p k e", k=2)).then_inc(w_ready, 1)
            dve.tensor_copy(valueT[:, :, :], ps_m[0:HALF, 1, 0:2 * DIM].rearrange("p (k o) -> p k o", k=2)).then_inc(w_ready, 1)
            dve.wait_ge(consts, 5)

            def layernorm_stats(i, p):
                dve.wait_ge(front_in[p], of_pair(i, p, 32))
                for t in range(NTILES):
                    dve.bn_stats(stats[:, t, :], h_front[:, p, t, :]).then_inc(dve_ln, 1)
                dve.wait_ge(dve_ln, 6 * i + 3)
                dve.nop(nofuse=True)
                for t in range(NTILES):
                    dve.bn_aggr(moments[:, t, :], stats[:, t, :]).then_inc(dve_ln, 1)

            def layernorm(i, p):
                dve.wait_ge(act_ln, 2 * (i + 1))
                if not isinstance(i, int) or i > 0:
                    dve.wait_ge(x_turned, i)
                square, half, scale = (newton[:, k, :] for k in range(3))
                dve.tensor_tensor(square, rstd[:, :], rstd[:, :], ALU.mult).then_inc(refined, 1)
                dve.wait_ge(refined, 4 * i + 1)
                dve.scalar_tensor_tensor(out=half, in0=moments[:, :, 1], scalar=LN_EPS, in1=square,
                                         op0=ALU.add, op1=ALU.mult).then_inc(refined, 1)
                dve.wait_ge(refined, 4 * i + 2)
                dve.tensor_scalar(half, half, -0.5, 1.5, ALU.mult, ALU.add).then_inc(refined, 1)
                dve.wait_ge(refined, 4 * i + 3)
                dve.tensor_tensor(scale, rstd[:, :], half, ALU.mult).then_inc(refined, 1)
                dve.wait_ge(refined, 4 * i + 4)
                for t in range(NTILES):
                    dve.tensor_scalar(xn[:, t, :], h_front[:, p, t, :], moments[:, t, 0:1], newton[:, 2, t:t + 1],
                                      ALU.subtract, ALU.mult).then_inc(xn_ready, 1)

            def latents(i, p):
                dve.wait_ge(lat_hi, i + 1)
                dve.tensor_tensor(lat[RANK:128, p, :], ps_q[RANK:128, 0:N], lat[RANK:128, p, :].bitcast(F32),
                                  ALU.subtract).then_inc(lat_lo, 1)

            def value(i, p):
                dve.wait_ge(v_mm, i + 1)
                for a, b in ((0, 2), (2, 3)):
                    src = ps_m[0:KEYS, a // 2, 0:(b - a) * DIM].rearrange("p (c h d) -> p c h d", c=b - a, h=HEADS)
                    bias = value_bias[:, :].rearrange("p (c h d) -> p c h d", c=1, h=HEADS)
                    if b - a > 1:
                        bias = bias.to_broadcast([KEYS, b - a, HEADS, HEAD_DIM])
                    dve.tensor_tensor(values[:, p, a:b, :, 0:HEAD_DIM], src, bias, ALU.add).then_inc(v_ready, 1)

            def query(i, p, h):
                dve.wait_ge(q_hi_ready, HEADS * i + h + 1)
                dve.tensor_tensor(q_lo[0:RANK, p, h, :], ps_q[0:RANK, 0:N], q_hi[0:RANK, p, h, :].bitcast(F32),
                                  ALU.subtract).then_inc(q_lo_ready, 1)

            def maximum(i, p, h):
                dve.wait_ge(s_mm, HEADS * i + h + 1)
                dve.tensor_reduce(row_max[:, p, :, h], ps_s[0:KEYS, 0:3 * N].rearrange("p (c m) -> p c m", c=3), AX,
                                  ALU.max).then_inc(max_ready, 1)

            def maximum_rows(i, p):
                dve.wait_ge(max_turned, i + 1)
                if not isinstance(i, int) or i > 0:
                    dve.wait_ge(max_in[1 - p], of_pair(i - 1, 1 - p, 16))
                dve.tensor_copy(max_rows[:, :], ps_m[0:HEADS, 1, 0:N]).then_inc(max_rows_ready, 1)

            def products(i, g):
                n = GROUPS * i + g
                dve.wait_ge(pv_mm, n + 1)
                if not isinstance(n, int) or n > 0:
                    dve.wait_ge(ctx_turned, n)
                dve.tensor_copy(ctx_sb[:, :], ps_v[:, 0:N]).then_inc(ctx_ready, 1)

            def residual_add(i, p, g):
                n = GROUPS * i + g
                dve.wait_ge(ctx_turned, n + 1)
                if g == 0:
                    dve.wait_ge(back_in[p], of_pair(i, p, 32))
                src = ps_m[:, 0, 0:NTILES * GROUP * 32].rearrange("p (t b e) -> p t b e", t=NTILES, b=GROUP)
                for a, b, rows in PARTS:
                    dve.reciprocal(recip[0:rows, a:b, :, :], src[0:rows, a:b, :, HEAD_DIM:HEAD_DIM + 1]).then_inc(recip_ready, 1)
                dve.wait_ge(recip_ready, 2 * n + 2)
                for a, b, rows in PARTS:
                    dve.tensor_tensor(scaled[0:rows, a:b, :, :], src[0:rows, a:b, :, 0:HEAD_DIM],
                                      recip[0:rows, a:b, :, :].to_broadcast([rows, b - a, GROUP, HEAD_DIM]),
                                      ALU.mult).then_inc(scaled_ready, 1)
                dve.wait_ge(scaled_ready, 2 * n + 2)
                for a, b, rows in PARTS:
                    at = h_back[0:rows, p, a:b, g * GROUP * HEAD_DIM:(g + 1) * GROUP * HEAD_DIM]
                    dve.tensor_tensor(at, at, scaled[0:rows, a:b, :, :].rearrange("p t b e -> p t (b e)"),
                                      ALU.add).then_inc(h2_ready, 1)

            def post_stats(i, p):
                dve.wait_ge(h2_ready, 2 * GROUPS * (i + 1))
                for t in range(NTILES):
                    dve.bn_stats(stats2[:, t, :], h_back[:, p, t, :]).then_inc(dve_ln2, 1)
                dve.wait_ge(dve_ln2, 6 * i + 3)
                dve.nop(nofuse=True)
                for t in range(NTILES):
                    dve.bn_aggr(moments2[:, t, :], stats2[:, t, :]).then_inc(dve_ln2, 1)

            def post_norm(i, p):
                dve.wait_ge(act_ln2, 2 * (i + 1))
                square, half, scale = (newton2[:, k, :] for k in range(3))
                dve.tensor_tensor(square, rstd2[:, :], rstd2[:, :], ALU.mult).then_inc(refined2, 1)
                dve.wait_ge(refined2, 4 * i + 1)
                dve.scalar_tensor_tensor(out=half, in0=moments2[:, :, 1], scalar=LN_EPS, in1=square,
                                         op0=ALU.add, op1=ALU.mult).then_inc(refined2, 1)
                dve.wait_ge(refined2, 4 * i + 2)
                dve.tensor_scalar(half, half, -0.5, 1.5, ALU.mult, ALU.add).then_inc(refined2, 1)
                dve.wait_ge(refined2, 4 * i + 3)
                dve.tensor_tensor(scale, rstd2[:, :], half, ALU.mult).then_inc(refined2, 1)
                dve.wait_ge(refined2, 4 * i + 4)
                if not isinstance(i, int) or i > 0:
                    dve.wait_ge(scattered, 16 * TOPK * NTILES * i)
                for t in range(NTILES):
                    dve.tensor_scalar(routed[:, 0, t, 0:DIM], h_back[:, p, t, :], moments2[:, t, 0:1], newton2[:, 2, t:t + 1],
                                      ALU.subtract, ALU.mult).then_inc(x2_ready, 1)

            def over_experts(ap):
                return ap.rearrange("p (t e) -> p t e", e=1).to_broadcast([128, NTILES, EXPERTS])

            def over_tiles(ap):
                return ap.rearrange("p (t e) -> p t e", t=1).to_broadcast([128, NTILES, EXPERTS])

            def routing(i):
                n = 0

                def step(instruction, wait=True):
                    nonlocal n
                    n += 1
                    instruction.then_inc(route, 1)
                    if wait:
                        dve.wait_ge(route, ROUTE_STEPS * i + n)

                def first_part():
                    dve.wait_ge(logit_mm, i + 1)
                    step(dve.tensor_copy(logits[:, :, :], ps_m[:, 1, 0:NTILES * EXPERTS].rearrange("p (t e) -> p t e", t=NTILES)))
                    assert n == LOGITS_READ
                    step(dve.tensor_reduce(top[:, :], logits[:, :, :], AX, ALU.max))
                    step(dve.tensor_tensor(expo[:, :, :], logits[:, :, :], over_experts(top[:, :]), ALU.subtract))
                    assert n == MAX_TAKEN
                    for k in range(TOPK):
                        of = logits if k == 0 else rest
                        if k:
                            step(dve.scalar_tensor_tensor(out=rest[:, :, :], in0=pick[:, :, 0, :], scalar=MASKED,
                                                          in1=logits[:, :, :], op0=ALU.mult, op1=ALU.add))
                            step(dve.tensor_reduce(top[:, :], rest[:, :, :], AX, ALU.max))
                        step(dve.tensor_tensor(key[:, :, :], of[:, :, :], over_experts(top[:, :]), ALU.is_equal))
                        step(dve.tensor_tensor(key[:, :, :], key[:, :, :], over_tiles(order[:, :]), ALU.mult))
                        step(dve.tensor_reduce(total[:, :], key[:, :, :], AX, ALU.max))
                        step(dve.tensor_tensor(pick[:, :, k, :], over_tiles(order[:, :]), over_experts(total[:, :]), ALU.is_equal))
                    step(dve.tensor_tensor(key[:, :, :], pick[:, :, 0, :], pick[:, :, 1, :], ALU.add))
                    step(dve.tensor_tensor(picked[:, :, :], key[:, :, :], over_experts(valid[:, :]), ALU.mult))
                    assert n == PICKED

                def second_part():
                    dve.wait_ge(expo_ready, i + 1)
                    step(dve.tensor_reduce(total[:, :], expo[:, :, :], AX, ALU.add))
                    step(dve.reciprocal(total[:, :], total[:, :]))
                    step(dve.tensor_tensor(key[:, :, :], expo[:, :, :], over_experts(total[:, :]), ALU.mult))
                    step(dve.tensor_tensor(importance[:, :, :], importance[:, :, :], key[:, :, :], ALU.add))
                    step(dve.tensor_tensor(of_pick[:, :, :, :], pick[:, :, :, :],
                                           key[:, :, :].rearrange("p t (k e) -> p t k e", k=1).to_broadcast([128, NTILES, TOPK, EXPERTS]),
                                           ALU.mult))
                    step(dve.tensor_reduce(pick_probs[:, bass.ds(i, 1), :, :].rearrange("p i t k -> p (i t) k"),
                                           of_pick[:, :, :, :], AX, ALU.add))
                    step(dve.tensor_copy(picks[:, bass.ds(i, 1), :, :, :].rearrange("p i t k e -> p (i t) k e"), pick[:, :, :, :]))

                def third_part():
                    dve.wait_ge(rank_mm, i + 1)
                    step(dve.tensor_tensor(key[:, :, :], ps_m[:, 1, 0:NTILES * EXPERTS].rearrange("p (t e) -> p t e", t=NTILES),
                                           over_tiles(places[:, :]), ALU.add))
                    step(dve.tensor_tensor(places[:, :], ps_m[:, 1, 32:32 + EXPERTS], places[:, :], ALU.add))
                    step(dve.tensor_tensor(routed[:, :, :, DIM:ROW], goal[:, :, :, :], goal[:, :, :, :], ALU.max))
                    assert n == RANKED
                    step(dve.tensor_tensor(of_pick[:, :, :, :], pick[:, :, :, :],
                                           key[:, :, :].rearrange("p t (k e) -> p t k e", k=1).to_broadcast([128, NTILES, TOPK, EXPERTS]),
                                           ALU.mult))
                    step(dve.tensor_reduce(place[:, :, :], of_pick[:, :, :, :], AX, ALU.add))
                    dve.tensor_scalar(goal[:, :, :, :], goal[:, :, :, :], float(N), None, ALU.add)
                    step(dve.tensor_copy(place_int[:, :, :], place[:, :, :]), wait=False)
                    assert n == ROUTE_STEPS

                return first_part, second_part, third_part

            def prologue():
                dve.wait_ge(order_in, 10)
                dve.tensor_copy(order[:, :], order_int[:, 0:EXPERTS]).then_inc(order_ready, 1)
                dve.tensor_copy(goal[:, :, :, 0], order_int[:, EXPERTS:].rearrange("p (k t) -> p k t", k=TOPK)).then_inc(order_ready, 1)
                dve.memset(importance[:, :, :], 0.0).then_inc(order_ready, 1)
                dve.wait_ge(order_ready, 3)
                dve.tensor_scalar(places[:, :], order[:, :], float(-SPACE), float(EXPERTS * SPACE), ALU.mult, ALU.add).then_inc(order_ready, 1)
                for i in range(2):
                    layernorm_stats(i, i)
                    layernorm(i, i)
                    latents(i, i)
                    value(i, i)
                for h in range(HEADS):
                    query(0, 0, h)
                    maximum(0, 0, h)
                maximum_rows(0, 0)

            def body(i, p, front, prep, post):
                if post:
                    parts = routing(i - 1)
                for h in range(HEADS):
                    if front:
                        query(i + 1, 1 - p, h)
                    if post and h == POST_SCALE:
                        post_stats(i - 1, 1 - p)
                    if post and h in POST_PARTS:
                        parts[POST_PARTS.index(h)]()
                    if prep and h == LN_AT:
                        layernorm_stats(i + 2, p)
                    if h % GROUP == 0 and h > 0:
                        products(i, h // GROUP - 1)
                    if front:
                        maximum(i + 1, 1 - p, h)
                    if post and h == POST_SCALE:
                        post_norm(i - 1, 1 - p)
                    if prep and h == LN_AT:
                        layernorm(i + 2, p)
                    if h % GROUP == 1 and h > 1:
                        residual_add(i, p, h // GROUP - 1)
                if front:
                    maximum_rows(i + 1, 1 - p)
                if prep:
                    latents(i + 2, p)
                products(i, GROUPS - 1)
                residual_add(i, p, GROUPS - 1)
                if prep:
                    value(i + 2, p)

            def epilogue():
                post_stats(IMAGES - 1, 1)
                post_norm(IMAGES - 1, 1)
                for part in routing(IMAGES - 1):
                    part()

            run(dve, prologue, body, epilogue)

        @block.tensor
        def _(pe):
            pe.wait_ge(w_in, 16 * 8)
            pe.wait_ge(consts, 5)
            for k in range(2):
                half = slice(k * HALF, (k + 1) * HALF)
                pe.transpose(ps_m[0:HALF, 0, k * RANK:(k + 1) * RANK], basis_raw[:, half], ident[0:RANK, 0:RANK])
                for o in range(2):
                    pe.transpose(ps_m[0:HALF, 1, k * DIM + o * HALF:k * DIM + (o + 1) * HALF], value_raw[:, o, half],
                                      ident[0:HALF, 0:HALF])
                mm = pe.transpose(ps_m[0:HALF, 0, 256 + k * EXPERTS:256 + (k + 1) * EXPERTS], router_raw[:, half],
                                  ident[0:EXPERTS, 0:EXPERTS])
            mm.then_inc(w_turned, 1)
            pe.wait_ge(w_ready, 3)
            pe.wait_ge(mat_step, 5)

            def transpose_x(i):
                pe.wait_ge(xn_ready, 3 * (i + 1))
                if not isinstance(i, int) or i > 0:
                    pe.wait_ge(xT_ready, i)
                for t, (at, rows) in enumerate(zip(TILE_AT, TILE_ROWS)):
                    for k in range(2):
                        mm = pe.transpose(ps_m[0:HALF, k, at:at + rows], xn[0:rows, t, k * HALF:(k + 1) * HALF],
                                          ident[0:rows, 0:rows])
                mm.then_inc(x_turned, 1)

            def latents(i):
                pe.wait_ge(xT_ready, i + 1)
                for k in range(2):
                    mm = pe.matmul(ps_q[:, 0:N], basisT[:, k, :, :].rearrange("p a r -> p (a r)"), xT[:, k, :],
                                   start=(k == 0), stop=(k == 1))
                mm.then_inc(lat_mm, 1)

            def value(i):
                for c in range(3):
                    for k in range(2):
                        mm = pe.matmul(ps_m[0:KEYS, c // 2, (c % 2) * DIM:(c % 2 + 1) * DIM], xT[:, k, c * KEYS:(c + 1) * KEYS],
                                       valueT[:, k, :], start=(k == 0), stop=(k == 1))
                mm.then_inc(v_mm, 1)

            def query(i, p, h):
                if h == 0:
                    pe.wait_ge(lat_lo, i + 1)
                if not isinstance(i, int) or i > 0 or h > 0:
                    pe.wait_ge(q_lo_ready, HEADS * i + h)
                pe.matmul(ps_q[:, 0:N], mats_lo[:, h, :, :].rearrange("p a s -> p (a s)"), lat[:, p, :], start=True, stop=False)
                pe.matmul(ps_q[:, 0:N], mats_hi[:, h, :, :].rearrange("p a s -> p (a s)"), lat[:, p, :], start=False,
                          stop=True).then_inc(q_mm, 1)

            def scores_by_query(i, p, h):
                pe.wait_ge(q_hi_ready, HEADS * i + h + 1)
                if not isinstance(i, int) or i > 0 or h > 0:
                    pe.wait_ge(max_ready, HEADS * i + h)
                for c, a, b in PIECES:
                    mm = pe.matmul(ps_s[0:KEYS, a:b], q_hi[:, p, h, c * KEYS:(c + 1) * KEYS], lat[:, p, a - c * N:b - c * N],
                                   start=True, stop=True)
                mm.then_inc(s_mm, 1)

            def maximum_rows(i, p):
                pe.wait_ge(max_ready, HEADS * (i + 1))
                for c in range(3):
                    mm = pe.transpose(ps_m[0:HEADS, 1, c * KEYS:(c + 1) * KEYS], row_max[:, p, c, :], ident[0:KEYS, 0:KEYS])
                mm.then_inc(max_turned, 1)

            def scores_by_key(i, p, h):
                if h == 0:
                    pe.wait_ge(one_row, 1)
                    pe.wait_ge(max_in[p], of_pair(i, p, 16))
                    pe.wait_ge(lat_one_ready, i + 1)
                    pe.wait_ge(q_lo_ready, HEADS * (i + 1))
                if not isinstance(i, int) or i > 0 or h > 0:
                    pe.wait_ge(probs_ready, HEADS * i + h)
                for c, a, b in PIECES:
                    keys = slice(c * KEYS, (c + 1) * KEYS)
                    queries = slice(a - c * N, b - c * N)
                    pe.matmul(ps_t[0:KEYS, a:b], lat_one[:, p, keys], q_lo[:, p, h, queries], start=True, stop=False)
                    mm = pe.matmul(ps_t[0:KEYS, a:b], lat[:, p, keys], q_hi[:, p, h, queries], start=False, stop=True)
                mm.then_inc(t_mm, 1)

            def products(i, p, g, slot):
                n = GROUPS * i + g
                if g == 0:
                    pe.wait_ge(v_ready, 2 * (i + 1))
                pe.wait_ge(probs_ready, HEADS * i + (g + 1) * GROUP)
                if not isinstance(n, int) or n > 0:
                    pe.wait_ge(ctx_ready, n)
                for c in range(3):
                    for b in range(GROUP):
                        mm = pe.matmul(ps_v[32 * b:32 * (b + 1), 0:N], values[:, p, c, g * GROUP + b, :],
                                       probs[:, slot * GROUP + b, c * N:(c + 1) * N], start=(c == 0), stop=(c == 2))
                mm.then_inc(pv_mm, 1)

            def turn_products(i, g):
                n = GROUPS * i + g
                pe.wait_ge(ctx_ready, n + 1)
                for t, (at, rows) in enumerate(zip(TILE_AT, TILE_ROWS)):
                    mm = pe.transpose(ps_m[0:rows, 0, t * GROUP * 32:(t + 1) * GROUP * 32], ctx_sb[:, at:at + rows], ident[:, :])
                mm.then_inc(ctx_turned, 1)

            def post_turn(i):
                pe.wait_ge(x2_ready, 3 * (i + 1))
                for t, (at, rows) in enumerate(zip(TILE_AT, TILE_ROWS)):
                    for k in range(2):
                        mm = pe.transpose(ps_m[0:HALF, k, at:at + rows], routed[0:rows, 0, t, k * HALF:(k + 1) * HALF],
                                          ident[0:rows, 0:rows])
                mm.then_inc(x2_turned, 1)

            def post_logits(i):
                pe.wait_ge(x2T_ready, i + 1)
                for t, at in enumerate(TILE_AT):
                    for k in range(2):
                        mm = pe.matmul(ps_m[:, 1, t * EXPERTS:(t + 1) * EXPERTS], x2T[:, k, at:at + 128], routerT[:, k, :],
                                       start=(k == 0), stop=(k == 1))
                mm.then_inc(logit_mm, 1)

            def post_ranks(i):
                pe.wait_ge(route, ROUTE_STEPS * i + PICKED)
                for t in range(NTILES):
                    for of in range(t + 1):
                        pe.matmul(ps_m[:, 1, t * EXPERTS:(t + 1) * EXPERTS], (before if of == t else all_ones)[:, :],
                                  picked[:, of, :], start=(of == 0), stop=(of == t))
                for t in range(NTILES):
                    mm = pe.matmul(ps_m[:, 1, 32:32 + EXPERTS], all_ones[:, :], picked[:, t, :], start=(t == 0), stop=(t == 2))
                mm.then_inc(rank_mm, 1)

            def prologue():
                for i in range(2):
                    if i:
                        pe.wait_ge(v_ready, 2 * i)
                    transpose_x(i)
                    if i:
                        pe.wait_ge(lat_lo, i)
                    latents(i)
                    value(i)
                pe.wait_ge(lat_lo, 2)
                for h in range(HEADS):
                    query(0, 0, h)
                    scores_by_query(0, 0, h)
                pe.wait_ge(v_ready, 4)
                maximum_rows(0, 0)

            def body(i, p, front, prep, post):
                for h in range(HEADS):
                    if front:
                        query(i + 1, 1 - p, h)
                    scores_by_key(i, p, h)
                    if h % GROUP == 0 and h > 0:
                        products(i, p, h // GROUP - 1, (GROUPS * p + h // GROUP - 1) % 2)
                    if front:
                        scores_by_query(i + 1, 1 - p, h)
                    if post and h == POST_TURN:
                        pe.wait_ge(v_ready, 2 * (i + 2) if front else 2 * IMAGES)
                        pe.wait_ge(max_rows_ready, i + 1)
                        pe.wait_ge(scaled_ready, 2 * GROUPS * i)
                        post_turn(i - 1)
                    if post and h == POST_TURN + 1:
                        post_logits(i - 1)
                    if post and h == POST_RANK:
                        if prep:
                            pe.wait_ge(xT_ready, i + 3)
                        post_ranks(i - 1)
                    if h % GROUP == 1 and h > 1:
                        if h // GROUP == 1:
                            pe.wait_ge(v_ready, 2 * (i + 2) if front else 2 * IMAGES)
                        elif prep:
                            pe.wait_ge(xT_ready, i + 3)
                        turn_products(i, h // GROUP - 1)
                    if prep and h == TURN_AT:
                        pe.wait_ge(scaled_ready, 2 * (GROUPS * i + 1))
                        pe.wait_ge(max_rows_ready, i + 1)
                        if post:
                            pe.wait_ge(route, ROUTE_STEPS * (i - 1) + LOGITS_READ)
                        transpose_x(i + 2)
                if front:
                    if prep:
                        pe.wait_ge(xT_ready, i + 3)
                    if post:
                        pe.wait_ge(route, ROUTE_STEPS * (i - 1) + RANKED)
                    maximum_rows(i + 1, 1 - p)
                if prep:
                    pe.wait_ge(q_lo_ready, HEADS * (i + 2))
                    latents(i + 2)
                products(i, p, GROUPS - 1, (GROUPS * p + GROUPS - 1) % 2)
                pe.wait_ge(scaled_ready, 2 * (GROUPS * i + 2))
                turn_products(i, GROUPS - 1)
                if prep:
                    pe.wait_ge(scaled_ready, 2 * (GROUPS * i + 3))
                    pe.wait_ge(max_rows_ready, i + 2)
                    value(i + 2)

            def epilogue():
                pe.wait_ge(scaled_ready, 2 * GROUPS * IMAGES)
                post_turn(IMAGES - 1)
                post_logits(IMAGES - 1)
                post_ranks(IMAGES - 1)

            run(pe, prologue, body, epilogue)


RESULTS = TOPK * TOKENS
INNER = HIDDEN // 128
PAIR = 2
AHEAD = 4
assert BLOCKS % AHEAD == 0


def experts(nc, w1, w2, rows_dram, results_dram, places):
    with ExitStack() as ctx:
        def sb(name, shape, dt=F32):
            return ctx.enter_context(nc.sbuf_tensor(name, shape, dt))

        def psum(name, shape, dt=F32):
            return ctx.enter_context(nc.psum_tensor(name, shape, dt))

        def sem(name):
            return ctx.enter_context(nc.semaphore(name))

        ident = sb("identB", [128, 128])
        w1_hi = sb("w1_hi", [HALF, 2, EXPERTS, HIDDEN], F32R)
        w1_lo = sb("w1_lo", [HALF, 2, EXPERTS, HIDDEN], F32R)
        w2_hi = sb("w2_hi", [128, EXPERTS, INNER, DIM], F32R)
        w2_lo = sb("w2_lo", [128, EXPERTS, INNER, DIM], F32R)
        w1_raw = sb("w1_raw", [128, EXPERTS * INNER, DIM])
        w2_raw = sb("w2_raw", [HALF, 2, EXPERTS, HIDDEN])

        int_consts = sb("int_consts", [128, EXPERTS + 1], I32)
        step_int = sb("step_int", [128, BLOCKS], I32)
        row_no = sb("row_no", [128, 1])
        first_row = sb("first_row", [128, EXPERTS])
        step_no = sb("step_no", [128, BLOCKS])
        empty = sb("empty", [128, ROW])
        pad_place = sb("pad_place", [128, EXPERTS])
        pad_int = sb("pad_int", [128, EXPERTS], I32)
        tiles_int = sb("tiles_int", [128, EXPERTS], I32)
        tiles = sb("tiles", [128, EXPERTS])
        ends = sb("ends", [128, 2, EXPERTS])
        jump = sb("jump", [128, EXPERTS])
        past = sb("past", [128, BLOCKS, EXPERTS])
        table = sb("table", [128, 2, BLOCKS])
        table_int = sb("table_int", [128, 2, BLOCKS], I32)

        rows = sb("rows", [128, AHEAD, ROW])
        goal_int = sb("goal_int", [128, AHEAD, 1], I32)
        x_hi = sb("x_hi", [HALF, 2, 2, 128], F32R)
        x_lo = sb("x_lo", [HALF, 2, 2, 128], F32R)
        hidden = sb("hidden", [128, 2, HIDDEN])
        hT_hi = sb("hT_hi", [128, 2, HIDDEN], F32R)
        hT_lo = sb("hT_lo", [128, 2, HIDDEN], F32R)
        result = sb("result", [128, AHEAD, DIM])

        ps_x = psum("ps_x", [HALF, 2, BANK])
        ps_h = psum("ps_h", [128, 2, BANK])
        ps_t = psum("ps_tB", [128, 2, BANK])
        ps_y = psum("ps_y", [128, 2, BANK])

        consts, const_step = sem("constsB"), sem("const_stepB")
        w1_in = [sem(f"w1_in{i}") for i in range(EXPERTS // PAIR)]
        w2_in = [sem(f"w2_in{i}") for i in range(EXPERTS // PAIR)]
        w_turned = sem("w_turnedB")
        w_hi_ready = sem("w_hi_readyB")
        w_lo_ready = sem("w_lo_readyB")
        table_step = sem("table_step")
        pads_ready = sem("pads_ready")
        table_ready = sem("table_ready")
        padded = sem("padded")
        spare_in = sem("spare_in")
        rows_in = [sem(f"rows_in{i}") for i in range(AHEAD)]
        goal_ready = sem("goal_ready")
        x_turned = sem("x_turnedB")
        x_hi_ready = sem("x_hi_readyB")
        x_lo_ready = sem("x_lo_readyB")
        h_mm = sem("h_mm")
        h_ready = sem("h_ready")
        h_turned = sem("h_turned")
        hT_hi_ready = sem("hT_hi_ready")
        hT_lo_ready = sem("hT_lo_ready")
        y_mm = sem("y_mm")
        y_ready = sem("y_ready")
        stored = [sem(f"stored{i}") for i in range(AHEAD)]

        block = ctx.enter_context(nc.Block())

        GROUPS_W = 4 * EXPERTS

        def group_of(n):
            return n < 2 * EXPERTS, (n % (2 * EXPERTS)) // 2, n % 2

        @block.sync
        def _(sp):
            for e in range(0, EXPERTS, PAIR):
                sp.dma_start(w1_raw[:, e * INNER:(e + PAIR) * INNER, :],
                             w1[e:e + PAIR].rearrange("e (c p) h -> p (e c) h", p=128)).then_inc(w1_in[e // PAIR], 16)
            for e in range(0, EXPERTS, PAIR):
                for k in range(2):
                    sp.dma_start(w2_raw[:, k, e:e + PAIR, :],
                                 w2[e:e + PAIR, k * HALF:(k + 1) * HALF, :].rearrange("e p i -> p e i")).then_inc(w2_in[e // PAIR], 16)
            sp.wait_ge(consts, 4)
            for k in range(SPARE):
                at = EXPERTS * SPACE + k * 128
                sp.dma_start(rows_dram[at:at + 128, :], empty[:, :]).then_inc(spare_in, 16)
            sp.wait_ge(table_ready, 1)
            sp.wait_ge(spare_in, 16 * SPARE)
            sp.wait_ge(padded, 16 * EXPERTS)

            def load(j, u):
                row = sp.value_load(table_int[0:1, 1, bass.ds(j, 1)], min_val=0, max_val=EXPERTS * SPACE + (SPARE - 1) * 128)
                sp.dma_start(rows[:, u, :], rows_dram[bass.ds(row, 128), :]).then_inc(rows_in[u], 16)

            for j in range(AHEAD):
                load(j, j)
            with sp.Fori(0, BLOCKS // AHEAD - 1) as it:
                for u in range(AHEAD):
                    j = it * AHEAD + u
                    sp.wait_ge(x_turned, j + 1)
                    sp.wait_ge(goal_ready, j + 1)
                    load(j + AHEAD, u)

        @block.gpsimd
        def _(pool):
            pool.memset(ident[:, :], 0.0).then_inc(const_step, 1)
            pool.memset(empty[:, 0:DIM], 0.0).then_inc(consts, 1)
            pool.iota(int_consts[:, 0:EXPERTS], [[SPACE // 128, EXPERTS]], base=0, channel_multiplier=0).then_inc(consts, 1)
            pool.iota(int_consts[:, EXPERTS:EXPERTS + 1], [[0, 1]], base=0, channel_multiplier=1).then_inc(consts, 1)
            pool.iota(step_int[:, :], [[1, BLOCKS]], base=0, channel_multiplier=0).then_inc(const_step, 1)
            pool.wait_ge(const_step, 2)
            pool.affine_select(out=ident[:, :], in_=ident[:, :], compare_op=ALU.not_equal, fill=1.0,
                               base=0, pattern=[[-1, 128]], channel_multiplier=1).then_inc(const_step, 1)
            pool.wait_ge(pads_ready, 1)
            for e in range(EXPERTS):
                pool.indirect_dma_start(rows_dram[:, :], bass.IndirectOffsetOnAxis(pad_int[:, e:e + 1], 0),
                                        empty[:, :], None).then_inc(padded, 16)

            def store(j, u):
                pool.wait_ge(goal_ready, j + 1)
                pool.wait_ge(y_ready, j + 1)
                pool.nop(nofuse=True)
                pool.indirect_dma_start(results_dram[:, :], bass.IndirectOffsetOnAxis(goal_int[:, u, :], 0),
                                        result[:, u, :], None, bounds_check=RESULTS - 1,
                                        oob_is_err=False).then_inc(stored[u], 16)

            with pool.Fori(0, BLOCKS // AHEAD) as it:
                for u in range(AHEAD):
                    store(it * AHEAD + u, u)
            for u in range(AHEAD):
                pool.wait_ge(stored[u], 16 * (BLOCKS // AHEAD))

        def split(n):
            is_w1, e, half = group_of(n)
            if is_w1:
                return (w1_hi[:, half, e, :], w1_lo[:, half, e, :], ps_x[:, n % 2, 0:HIDDEN])
            chunks = slice(half * 2, half * 2 + 2)
            return tuple(w[:, e, chunks, :].rearrange("p c d -> p (c d)") for w in (w2_hi, w2_lo)) + (ps_h[:, n % 2, 0:2 * DIM],)

        def of_slot(j, u, each):
            return (j // AHEAD) * each if isinstance(j, int) else (j - u) * (each // AHEAD)

        def pipeline(engine, first, middle, last):
            first()
            for j in range(1, AHEAD + 1):
                middle(j, j % AHEAD)
            with engine.Fori(0, BLOCKS // AHEAD - 2) as it:
                for k in range(1, AHEAD + 1):
                    middle(it * AHEAD + AHEAD + k, k % AHEAD)
            for j in range(BLOCKS - AHEAD + 1, BLOCKS - 1):
                middle(j, j % AHEAD)
            last(BLOCKS - 1, (BLOCKS - 1) % AHEAD)

        @block.scalar
        def _(act):
            act.preload_act_table(ACT.Silu)
            for n in range(GROUPS_W):
                hi, _, src = split(n)
                act.wait_ge(w_turned, n + 1)
                act.activation(hi, src, ACT.Copy).then_inc(w_hi_ready, 1)

            def x_half(j, u):
                act.wait_ge(x_turned, j + 1)
                act.activation(x_hi[:, u % 2, :, :], ps_x[:, u % 2, 0:256].rearrange("p (k t) -> p k t", k=2), ACT.Copy).then_inc(x_hi_ready, 1)

            def silu(j, u):
                act.wait_ge(h_mm, j + 1)
                act.activation(hidden[:, u % 2, :], ps_h[:, u % 2, :], ACT.Silu).then_inc(h_ready, 1)

            def h_half(j, u):
                act.wait_ge(h_turned, j + 1)
                act.activation(hT_hi[:, u % 2, :], ps_t[:, u % 2, :], ACT.Copy).then_inc(hT_hi_ready, 1)

            def first():
                x_half(0, 0)
                silu(0, 0)
                x_half(1, 1)

            def middle(j, u):
                h_half(j - 1, u - 1)
                silu(j, u)
                x_half(j + 1, u + 1)

            def last(j, u):
                h_half(j - 1, u - 1)
                silu(j, u)
                h_half(j, u)

            pipeline(act, first, middle, last)

        @block.vector
        def _(dve):
            dve.wait_ge(consts, 3)
            dve.wait_ge(const_step, 2)
            n = 0

            def step(instruction):
                nonlocal n
                n += 1
                instruction.then_inc(table_step, 1)
                dve.wait_ge(table_step, n)

            dve.tensor_scalar(first_row[:, :], int_consts[:, 0:EXPERTS], 128.0, None, ALU.mult).then_inc(table_step, 1)
            dve.tensor_copy(step_no[:, :], step_int[:, :]).then_inc(table_step, 1)
            n = 2
            step(dve.tensor_copy(row_no[:, :], int_consts[:, EXPERTS:EXPERTS + 1]))
            dve.tensor_scalar(empty[:, DIM:ROW], row_no[:, :], float(RESULTS), None, ALU.add).then_inc(consts, 1)
            step(dve.tensor_scalar(pad_place[:, :], places[:, :], row_no[:, 0:1], None, ALU.add))
            dve.tensor_copy(pad_int[:, :], pad_place[:, :]).then_inc(pads_ready, 1)
            step(dve.tensor_tensor(tiles[:, :], places[:, :], first_row[:, :], ALU.subtract))
            step(dve.tensor_scalar(tiles[:, :], tiles[:, :], 127.0, None, ALU.add))
            step(dve.tensor_copy(tiles_int[:, :], tiles[:, :]))
            step(dve.tensor_single_scalar(tiles_int[:, :], tiles_int[:, :], 7, ALU.arith_shift_right))
            step(dve.tensor_copy(tiles[:, :], tiles_int[:, :]))
            step(dve.tensor_copy(ends[:, 0, :], tiles[:, :]))
            for k, by in enumerate((1, 2, 4)):
                a, b = k % 2, 1 - k % 2
                step(dve.tensor_copy(ends[:, b, 0:by], ends[:, a, 0:by]))
                step(dve.tensor_tensor(ends[:, b, by:EXPERTS], ends[:, a, by:EXPERTS], ends[:, a, 0:EXPERTS - by], ALU.add))
            step(dve.tensor_scalar(jump[:, :], tiles[:, :], -128.0, float(SPACE), ALU.mult, ALU.add))
            step(dve.tensor_tensor(past[:, :, :], step_no[:, :].rearrange("p (j e) -> p j e", e=1).to_broadcast([128, BLOCKS, EXPERTS]),
                                   ends[:, 1, :].rearrange("p (j e) -> p j e", j=1).to_broadcast([128, BLOCKS, EXPERTS]), ALU.is_ge))
            step(dve.tensor_reduce(table[:, 0, :], past[:, :, :], AX, ALU.add))
            step(dve.tensor_scalar(table[:, 0, :], table[:, 0, :], float(EXPERTS - 1), None, ALU.min))
            step(dve.tensor_tensor(past[:, :, :], past[:, :, :],
                                   jump[:, :].rearrange("p (j e) -> p j e", j=1).to_broadcast([128, BLOCKS, EXPERTS]), ALU.mult))
            step(dve.tensor_reduce(table[:, 1, :], past[:, :, :], AX, ALU.add))
            step(dve.scalar_tensor_tensor(out=table[:, 1, :], in0=step_no[:, :], scalar=128.0, in1=table[:, 1, :],
                                          op0=ALU.mult, op1=ALU.add))
            dve.tensor_copy(table_int[:, :, :], table[:, :, :]).then_inc(table_ready, 1)

            for g in range(GROUPS_W):
                hi, lo, src = split(g)
                dve.wait_ge(w_hi_ready, g + 1)
                dve.tensor_tensor(lo, src, hi.bitcast(F32), ALU.subtract).then_inc(w_lo_ready, 1)

            def x_half(j, u):
                dve.wait_ge(x_hi_ready, j + 1)
                dve.tensor_tensor(x_lo[:, u % 2, :, :], ps_x[:, u % 2, 0:256].rearrange("p (k t) -> p k t", k=2),
                                  x_hi[:, u % 2, :, :].bitcast(F32), ALU.subtract).then_inc(x_lo_ready, 1)

            def goal(j, u):
                if not isinstance(j, int) or j >= AHEAD:
                    dve.wait_ge(stored[u], of_slot(j, u, 16))
                dve.wait_ge(rows_in[u], of_slot(j, u, 16) + 16)
                dve.tensor_copy(goal_int[:, u, :], rows[:, u, DIM:ROW]).then_inc(goal_ready, 1)

            def h_half(j, u):
                dve.wait_ge(hT_hi_ready, j + 1)
                dve.tensor_tensor(hT_lo[:, u % 2, :], ps_t[:, u % 2, :], hT_hi[:, u % 2, :].bitcast(F32), ALU.subtract).then_inc(hT_lo_ready, 1)

            def finish(j, u):
                dve.wait_ge(y_mm, j + 1)
                dve.tensor_copy(result[:, u, :], ps_y[:, u % 2, 0:DIM]).then_inc(y_ready, 1)

            def first():
                goal(0, 0)
                x_half(0, 0)
                goal(1, 1)
                x_half(1, 1)

            def middle(j, u):
                h_half(j - 1, u - 1)
                goal(j + 1, (u + 1) % AHEAD)
                x_half(j + 1, u + 1)
                finish(j - 1, (u - 1) % AHEAD)

            def last(j, u):
                h_half(j - 1, u - 1)
                finish(j - 1, u - 1)
                h_half(j, u)
                finish(j, u)

            pipeline(dve, first, middle, last)

        @block.tensor
        def _(pe):
            pe.wait_ge(const_step, 3)
            for n in range(GROUPS_W):
                is_w1, e, half = group_of(n)
                if e % PAIR == 0 and half == 0:
                    pe.wait_ge(w1_in[e // PAIR] if is_w1 else w2_in[e // PAIR], 16 if is_w1 else 32)
                if n >= 2:
                    pe.wait_ge(w_lo_ready, n - 1)
                dst = split(n)[2]
                for c in range(INNER):
                    if is_w1:
                        mm = pe.transpose(dst[:, c * 128:(c + 1) * 128], w1_raw[:, e * INNER + c, half * HALF:(half + 1) * HALF], ident[:, :])
                    else:
                        chunk = half * 2 + c // 2
                        mm = pe.transpose(dst[:, c * HALF:(c + 1) * HALF], w2_raw[:, c % 2, e, chunk * 128:(chunk + 1) * 128],
                                          ident[0:HALF, 0:HALF])
                mm.then_inc(w_turned, 1)
            pe.wait_ge(w_lo_ready, GROUPS_W)
            pe.wait_ge(table_ready, 1)

            def used(j):
                return not isinstance(j, int) or j >= 2

            def turn_x(j, u):
                if used(j):
                    pe.wait_ge(x_lo_ready, j - 1)
                pe.wait_ge(rows_in[u], of_slot(j, u, 16) + 16)
                for k in range(2):
                    mm = pe.transpose(ps_x[:, u % 2, k * 128:(k + 1) * 128], rows[:, u, k * HALF:(k + 1) * HALF], ident[:, :])
                mm.then_inc(x_turned, 1)

            held = [None, None]

            def expert_of(j):
                return pe.value_load(table_int[0:1, 0, bass.ds(j, 1)], min_val=0, max_val=EXPERTS - 1)

            def first_layer(j, u, e):
                if used(j):
                    pe.wait_ge(h_ready, j - 1)
                pe.wait_ge(x_lo_ready, j + 1)
                mm = None
                v = u % 2
                for k in range(2):
                    hi, lo = (w[:, k, bass.ds(e, 1), :].rearrange("p e i -> p (e i)") for w in (w1_hi, w1_lo))
                    pe.matmul(ps_h[:, v, :], x_lo[:, v, k, :], hi, start=(k == 0), stop=False)
                    pe.matmul(ps_h[:, v, :], x_hi[:, v, k, :], lo, start=False, stop=False)
                    mm = pe.matmul(ps_h[:, v, :], x_hi[:, v, k, :], hi, start=False, stop=(k == 1))
                mm.then_inc(h_mm, 1)

            def turn_h(j, u):
                if used(j):
                    pe.wait_ge(hT_lo_ready, j - 1)
                pe.wait_ge(h_ready, j + 1)
                for c in range(INNER):
                    mm = pe.transpose(ps_t[:, u % 2, c * 128:(c + 1) * 128], hidden[:, u % 2, c * 128:(c + 1) * 128], ident[:, :])
                mm.then_inc(h_turned, 1)

            def second_layer(j, u, e):
                if used(j):
                    pe.wait_ge(y_ready, j - 1)
                pe.wait_ge(hT_lo_ready, j + 1)
                v = u % 2
                for c in range(INNER):
                    hi, lo = (w[:, bass.ds(e, 1), c, :].rearrange("p e d -> p (e d)") for w in (w2_hi, w2_lo))
                    at = slice(c * 128, (c + 1) * 128)
                    pe.matmul(ps_y[:, v, 0:DIM], hT_lo[:, v, at], hi, start=(c == 0), stop=False)
                    pe.matmul(ps_y[:, v, 0:DIM], hT_hi[:, v, at], lo, start=False, stop=False)
                    mm = pe.matmul(ps_y[:, v, 0:DIM], hT_hi[:, v, at], hi, start=False, stop=(c == INNER - 1))
                mm.then_inc(y_mm, 1)

            def first():
                turn_x(0, 0)
                first_layer(0, 0, expert_of(0))
                turn_x(1, 1)

            def middle(j, u, more=True):
                if u == 1:
                    held[:] = expert_of(j - 1), expert_of(j)
                e_before, e = held
                turn_h(j - 1, u - 1)
                first_layer(j, u, e)
                if more:
                    turn_x(j + 1, (u + 1) % AHEAD)
                held[:] = e, expert_of(j + 1) if more and u != 0 else None
                second_layer(j - 1, u - 1, e_before)

            def last(j, u):
                middle(j, u, False)
                turn_h(j, u)
                second_layer(j, u, held[0])

            pipeline(pe, first, middle, last)


def combine(nc, h2_dram, results_dram, picks, pick_probs, importance, out):
    with ExitStack() as ctx:
        def sb(name, shape, dt=F32):
            return ctx.enter_context(nc.sbuf_tensor(name, shape, dt))

        def sem(name):
            return ctx.enter_context(nc.semaphore(name))

        ones = sb("onesC", [128, 128])
        running = sb("running", [128, EXPERTS])
        TILES = IMAGES * NTILES * TOPK
        of_pick = sb("of_pickC", [128, TILES, EXPERTS])
        balance = sb("balance", [128, TILES])
        share = sb("share", [128, TILES // TOPK, TOPK])
        whole = sb("whole", [128, TILES // TOPK, 1])
        weight = sb("weight", [128, IMAGES, NTILES, TOPK])
        now = sb("now", [128, 2, NTILES, TOPK])
        base = sb("base", [128, 2, NTILES, DIM])
        part = sb("part", [128, 2, TOPK, NTILES, DIM])
        ps = ctx.enter_context(nc.psum_tensor("ps_c", [128, BANK], F32))

        ones_ready, summed, step = sem("ones_ready"), sem("summedC"), sem("stepC")
        loaded = [sem(f"loaded{i}") for i in range(2)]
        now_ready = sem("now_ready")
        added = sem("added")
        out_stored = [sem(f"out_stored{i}") for i in range(2)]
        PARTS = [(0, 2, PTILE), (2, 3, TEXT)]

        block = ctx.enter_context(nc.Block())

        @block.tensor
        def _(pe):
            pe.wait_ge(ones_ready, 1)
            for t, rows in enumerate(TILE_ROWS):
                mm = pe.matmul(ps[:, 0:EXPERTS], ones[0:rows, :], importance[0:rows, t, :], start=(t == 0), stop=(t == 2))
            mm.then_inc(summed, 1)

        def patch_rows(dram, i, at):
            return dram[bass.ds(at, 2 * PTILE), :].rearrange("(t p) d -> p t d", t=2)

        @block.sync
        def _(sp):
            def load(i, u):
                for dst, dram, at in [(base[:, u], h2_dram, 0), (part[:, u, 0], results_dram, 0), (part[:, u, 1], results_dram, TOKENS)]:
                    sp.dma_start(dst[0:PTILE, 0:2, :], patch_rows(dram, i, at + i * N)).then_inc(loaded[u], 16)
                    sp.dma_start(dst[:, 2, :], dram[bass.ds(at + i * N + 2 * PTILE, TEXT), :]).then_inc(loaded[u], 16)

            load(0, 0)
            load(1, 1)
            with sp.Fori(0, IMAGES // 2 - 1) as it:
                for u in range(2):
                    i = it * 2 + u
                    sp.wait_ge(out_stored[u], 48 * (it + 1))
                    sp.nop(nofuse=True)
                    load(i + 2, u)

        @block.scalar
        def _(act):
            def store(i, u):
                act.wait_ge(added, 4 * (i + 1))
                patches = out[bass.ds(i, 1), 0:2 * PTILE, :].rearrange("a (g w) d -> w (a g) d", w=GRID)
                for t in range(2):
                    act.dma_start(patches[t * TILE_COLS:(t + 1) * TILE_COLS, :, :], base[0:PTILE, u, t, :]).then_inc(out_stored[u], 16)
                act.dma_start(out[bass.ds(i, 1), 2 * PTILE:N, :].rearrange("a p d -> (a p) d"), base[:, u, 2, :]).then_inc(out_stored[u], 16)

            with act.Fori(0, IMAGES // 2) as it:
                for u in range(2):
                    store(it * 2 + u, u)
            for u in range(2):
                act.wait_ge(out_stored[u], 48 * IMAGES // 2)

        @block.vector
        def _(dve):
            n = 0

            def chained(instruction):
                nonlocal n
                n += 1
                instruction.then_inc(step, 1)
                dve.wait_ge(step, n)

            dve.memset(ones[:, :], 1.0).then_inc(ones_ready, 1)
            dve.wait_ge(summed, 1)
            chained(dve.tensor_scalar(running[:, :], ps[:, 0:EXPERTS], 1.0, 1.0 - 0.9, ALU.subtract, ALU.mult))
            chained(dve.tensor_scalar(running[:, :], running[:, :], 1.0, 0.01, ALU.add, ALU.add))
            chained(dve.tensor_tensor(of_pick[:, :, :], picks[:, :, :, :, :].rearrange("p i t k e -> p (i t k) e"),
                                      running[:, :].rearrange("p (t e) -> p t e", t=1).to_broadcast([128, TILES, EXPERTS]), ALU.mult))
            chained(dve.tensor_reduce(balance[:, :], of_pick[:, :, :], AX, ALU.add))
            chained(dve.reciprocal(balance[:, :], balance[:, :]))
            flat = share[:, :, :].rearrange("p n k -> p (n k)")
            chained(dve.tensor_tensor(flat, pick_probs[:, :, :, :].rearrange("p i t k -> p (i t k)"), balance[:, :], ALU.mult))
            chained(dve.tensor_reduce(whole[:, :, 0], share[:, :, :], AX, ALU.add))
            chained(dve.reciprocal(whole[:, :, :], whole[:, :, :]))
            chained(dve.tensor_tensor(weight[:, :, :, :].rearrange("p i t k -> p (i t) k"), share[:, :, :],
                                      whole[:, :, :].to_broadcast([128, TILES // TOPK, TOPK]), ALU.mult))

            def add(i, u, it):
                dve.tensor_copy(now[:, u, :, :], weight[:, bass.ds(i, 1), :, :].rearrange("p i t k -> p (i t) k")).then_inc(now_ready, 1)
                dve.wait_ge(loaded[u], 96 * (it + 1))
                dve.nop(nofuse=True)
                dve.wait_ge(now_ready, i + 1)
                dve.nop(nofuse=True)
                for k in range(TOPK):
                    if k:
                        dve.wait_ge(added, 4 * i + 2)
                    for a, b, rows in PARTS:
                        for t in range(a, b):
                            mm = dve.scalar_tensor_tensor(out=base[0:rows, u, t, :], in0=part[0:rows, u, k, t, :],
                                                          scalar=now[0:rows, u, t, k:k + 1], in1=base[0:rows, u, t, :],
                                                          op0=ALU.mult, op1=ALU.add)
                        mm.then_inc(added, 1)

            with dve.Fori(0, IMAGES // 2) as it:
                for u in range(2):
                    add(it * 2 + u, u, it)


def program(nc, x, txt, gamma, beta, W, b, basis_w, core, head_residual, value_w, value_b, router_w, w1, w2, out):
    h_dram = nc.dram_tensor("h", (IMAGES, N, DIM), F32, kind="Internal").ap()
    h2_dram = nc.dram_tensor("h2", (TOKENS, DIM), F32, kind="Internal").ap()
    rows_dram = nc.dram_tensor("rows_by_expert", (EXPERTS * SPACE + SPARE * 128, ROW), F32, kind="Internal").ap()
    results_dram = nc.dram_tensor("results", (RESULTS, DIM), F32, kind="Internal").ap()
    with ExitStack() as ctx:
        def sb(name, shape):
            return ctx.enter_context(nc.sbuf_tensor(name, shape, F32))

        picks = sb("picks", [128, IMAGES, NTILES, TOPK, EXPERTS])
        pick_probs = sb("pick_probs", [128, IMAGES, NTILES, TOPK])
        places = sb("places", [128, EXPERTS])
        importance = sb("importance", [128, NTILES, EXPERTS])
        tokenize(nc, x, gamma, beta, W, b, h_dram)
        attention(nc, txt, basis_w, core, head_residual, value_w, value_b, router_w, h_dram,
                  h2_dram.rearrange("(i n) d -> i n d", i=IMAGES), rows_dram, (picks, pick_probs, places, importance))
        experts(nc, w1, w2, rows_dram, results_dram, places)
        combine(nc, h2_dram, results_dram, picks, pick_probs, importance, out)


_INS = ["x", "txt", "L0_tok_gamma", "L0_tok_beta", "L0_tok_W", "L0_tok_b", "L0_attn_basis_w", "L0_attn_core",
        "L0_attn_head_residual", "L0_attn_value_w", "L0_attn_value_b", "L0_ffn_router_w", "L0_ffn_w1", "L0_ffn_w2"]


def kernel(**inputs):
    import numpy as _np
    import concourse.bacc as _bacc
    from concourse import mybir as _mybir
    from concourse.bass_utils import run_bass_kernel_spmd as _run

    nc = _bacc.Bacc("TRN2", target_bir_lowering=False, num_devices=1)
    arrays, args = {}, []
    for name in _INS:
        a = _np.ascontiguousarray(inputs[name])
        arrays[f"in_{name}"] = a
        args.append(nc.dram_tensor(f"in_{name}", a.shape, _mybir.dt.from_np(a.dtype), kind="ExternalInput").ap())
    out = nc.dram_tensor("out_dram", (IMAGES, N, DIM), _mybir.dt.float32, kind="ExternalOutput").ap()
    program(nc, *args, out)
    r = _run(nc, [arrays], core_ids=[0])
    return r.results[0]["out_dram"]
```

```python
from contextlib import ExitStack

import concourse.bass as bass
from concourse import mybir

F32 = mybir.dt.float32
F32R = mybir.dt.float32r
I32 = mybir.dt.int32
BF16 = mybir.dt.bfloat16
ALU = mybir.AluOpType
ACT = mybir.ActivationFunctionType
AX = mybir.AxisListType.X

IMAGES, SIDE, CH = 16, 224, 3
TEXT, DIM = 128, 192
PATCH = 16
GRID = SIDE // PATCH
SHIFTS = 5
FEATURES = PATCH * PATCH * SHIFTS * CH
TOK_EPS = 0.001

HALO = PATCH + 2
WIN = HALO * CH
BATCH_IMAGES = 8
BATCHES = IMAGES // BATCH_IMAGES
ROWP = BATCH_IMAGES * GRID
LINE = SIDE * CH
PADLINE = LINE + 2 * CH
CHUNK = 2 * WIN
CHUNKS = HALO // 2
TGROUP = 3

TILE_COLS = GRID // 2
PTILE = TILE_COLS * GRID
N = GRID * GRID + TEXT
SLOTS = 2
STEPS = BATCHES * GRID


def tokenize(nc, x, gamma, beta, W, b, h_dram):
    with ExitStack() as ctx:
        def sb(name, shape, dt=F32):
            return ctx.enter_context(nc.sbuf_tensor(name, shape, dt))

        def psum(name, shape, dt=F32):
            return ctx.enter_context(nc.psum_tensor(name, shape, dt))

        def sem(name):
            return ctx.enter_context(nc.semaphore(name))

        lines = sb("lines", [ROWP, BATCHES, HALO, PADLINE])
        w_shift = lines[0:CHUNK, BATCHES - 1, :, :].rearrange("p r l -> p (r l)")[:, 0:SHIFTS * CHUNKS * DIM] \
            .rearrange("p (s t d) -> p s t d", s=SHIFTS, t=CHUNKS)
        factors_raw = sb("factors_raw", [2 * PATCH, 2, FEATURES // PATCH])
        of_half = sb("of_half", [2 * PATCH, 2])
        spread = sb("spread", [2 * PATCH, 2, SHIFTS, 2, HALO, CH])
        pick_row = sb("pick_row", [2 * PATCH, 3, CHUNKS])
        pick_half = sb("pick_half", [2 * PATCH, 3, CHUNKS])
        factors = sb("factors", [CHUNK, 2, SHIFTS, CHUNKS])
        b_row = sb("b_row", [ROWP, DIM])
        bias = sb("bias", [ROWP, DIM])
        w_sum = sb("w_sum", [CHUNK, CHUNKS, DIM])
        w_hi = sb("w_hi", [CHUNK, CHUNKS, DIM], F32R)
        w_lo = sb("w_lo", [CHUNK, CHUNKS, DIM], F32R)
        count = sb("count", [ROWP, HALO, HALO, CH])
        count_rows = count[:, :, :, :].rearrange("p r q c -> p r (q c)")
        zeros = sb("zeros", [BATCH_IMAGES, LINE])
        ident = sb("ident0", [128, 128])
        eps = sb("eps0", [128, 1])
        win = sb("win", [ROWP, SLOTS, HALO, WIN])
        centred = sb("centred", [ROWP, SLOTS, HALO, WIN])
        square = sb("square", [ROWP, SLOTS, HALO, WIN])
        negmean = sb("negmean", [ROWP, SLOTS])
        var = sb("var", [ROWP, SLOTS])
        logvar = sb("logvar", [ROWP, SLOTS])
        rstd = sb("rstd", [ROWP, SLOTS])
        newton = sb("newton0", [ROWP, SLOTS, 2])
        winT_hi = sb("winT_hi", [CHUNK, SLOTS, CHUNKS, ROWP], F32R)
        winT_lo = sb("winT_lo", [CHUNK, SLOTS, CHUNKS, ROWP], F32R)
        tok = sb("tok", [ROWP, SLOTS, DIM])
        psT = psum("psT", [CHUNK, SLOTS, CHUNKS // TGROUP, 512])
        psO = psum("psO", [ROWP, SLOTS, 512])

        lines_clear = sem("lines_clear")
        shift_clear = sem("shift_clear")
        consts = sem("consts")
        const_step = sem("const_step")
        pick_ready = sem("pick_ready")
        picked = sem("picked0")
        lines_in = [sem(f"lines_in{i}") for i in range(BATCHES)]
        edges_in = sem("edges_in")
        f_in = sem("f_in")
        spread_ready = sem("spread_ready")
        factors_mm = sem("factors_mm")
        factors_ready = sem("factors_ready")
        shift_in = [sem(f"shift_in{i}") for i in range(SHIFTS)]
        w_summed = sem("w_summed")
        w_hi_ready = sem("w_hi_ready")
        w_lo_ready = sem("w_lo_ready")
        bias_mm = sem("bias_mm")
        bias_ready = sem("bias_ready")
        win_ready = sem("win_ready")
        mean_ready = sem("mean_ready")
        centred_ready = sem("centred_ready")
        square_ready = sem("square_ready")
        var_ready = sem("var_ready")
        log_ready = sem("log_ready")
        rstd_ready = sem("rstd_ready")
        refined = sem("refined0")
        turned = sem("turned")
        hi_ready = sem("hi_ready")
        lo_ready = sem("lo_ready")
        projected = sem("projected")
        tok_ready = sem("tok_ready")
        tok_out = [sem(f"tok_out{i}") for i in range(SLOTS)]

        block = ctx.enter_context(nc.Block())

        def late(step, by):
            return not isinstance(step, int) or step >= by

        def of_slot(step, u, each):
            return (step // SLOTS) * each if isinstance(step, int) else (step - u) * (each // SLOTS)

        def run(engine, body):
            for k in range(-2, 2):
                body(k, k % SLOTS, 0, k + 2)
            with engine.Fori(0, (GRID - 4) // SLOTS) as it:
                for u in range(SLOTS):
                    body(it * SLOTS + u + 2, u, 0, it * SLOTS + u + 4)
            with engine.Fori(0, GRID // SLOTS) as it:
                for u in range(SLOTS):
                    body(it * SLOTS + u + GRID - 2, u, 1, it * SLOTS + u)
            for k in range(STEPS - 2, STEPS + 1):
                body(k, k % SLOTS, None, None)

        def valid(step):
            return not isinstance(step, int) or 0 <= step < STEPS

        def load_lines(q, bi, rows=range(0, PATCH, 4)):
            i0 = bi * BATCH_IMAGES
            own = x[i0:i0 + BATCH_IMAGES].rearrange("i (g r) w c -> (i g) r (w c)", r=PATCH)
            for r0 in rows:
                q.dma_start(lines[:, bi, 1 + r0:5 + r0, CH:CH + LINE], own[:, r0:r0 + 4, :]) \
                    .then_inc(lines_in[bi], 16)

        def load_neighbours(q, bi):
            i0 = bi * BATCH_IMAGES
            own = x[i0:i0 + BATCH_IMAGES].rearrange("i (g r) w c -> (i g) r (w c)", r=PATCH)
            q.dma_start(lines[1:ROWP, bi, 0, CH:CH + LINE], own[0:ROWP - 1, PATCH - 1, :]).then_inc(edges_in, 16)
            q.dma_start(lines[0:ROWP - 1, bi, HALO - 1, CH:CH + LINE], own[1:ROWP, 0, :]).then_inc(edges_in, 16)
            q.wait_ge(edges_in, 32 * (bi + 1))
            q.dma_start(lines[0:ROWP:GRID, bi, 0, CH:CH + LINE], zeros[:, :]).then_inc(lines_in[bi], 16)
            q.dma_start(lines[GRID - 1:ROWP:GRID, bi, HALO - 1, CH:CH + LINE], zeros[:, :]).then_inc(lines_in[bi], 16)

        LINES_LANDED = 16 * (4 + 2)

        SOURCE = [(1, 1), (1, 0), (1, 2), (0, 1), (2, 1)]
        w5 = W.rearrange("(h w s c) d -> h w s c d", h=PATCH, w=PATCH, s=SHIFTS)

        def load_shifted(q, s):
            dr, dc = SOURCE[s]
            for odd in range(2):
                t0 = (dr - odd + 1) // 2
                h0 = 2 * t0 + odd - dr
                for c in range(CH):
                    p = (odd * HALO + dc) * CH + c
                    q.dma_start(w_shift[p:p + (PATCH - 1) * CH + 1:CH, s, t0:t0 + PATCH // 2, :],
                                w5[h0:PATCH:2, :, s, c, :].rearrange("t w d -> w t d")) \
                        .then_inc(shift_in[s], 16)

        SHIFTED_LANDED = 16 * 2 * CH

        @block.sync
        def _(sp):
            sp.dma_start(factors_raw[0:PATCH, 0, :], gamma.rearrange("(h f) -> h f", h=PATCH)).then_inc(f_in, 16)
            sp.dma_start(factors_raw[PATCH:2 * PATCH, 0, :], gamma.rearrange("(h f) -> h f", h=PATCH)).then_inc(f_in, 16)
            load_lines(sp, 0)
            for s in range(0, SHIFTS, 2):
                sp.wait_ge(shift_clear, s + 2)
                load_shifted(sp, s)
            sp.wait_ge(w_summed, SHIFTS)
            sp.wait_ge(bias_mm, 1)
            load_lines(sp, 1)
            sp.wait_ge(lines_clear, 4)
            load_neighbours(sp, 1)
            for bi in range(BATCHES):
                with sp.Fori(0, GRID // SLOTS) as i:
                    for u in range(SLOTS):
                        column = i * SLOTS + u
                        out = h_dram[bi * BATCH_IMAGES:(bi + 1) * BATCH_IMAGES, bass.ds(column * GRID, GRID), :]
                        sp.wait_ge(tok_ready, bi * GRID + column + 1)
                        sp.dma_start(out, tok[:, u, :]).then_inc(tok_out[u], 16)
            for u in range(SLOTS):
                sp.wait_ge(tok_out[u], 16 * (STEPS // SLOTS))

        @block.gpsimd
        def _(pool):
            def clear(bi):
                pool.memset(lines[:, bi, 0:HALO:HALO - 1, :], 0.0).then_inc(lines_clear, 1)
                pool.memset(lines[:, bi, 1:HALO - 1, 0:CH], 0.0).then_inc(lines_clear, 1)
                pool.memset(lines[:, bi, 1:HALO - 1, PADLINE - CH:PADLINE], 0.0).then_inc(lines_clear, 1)

            pool.memset(lines[:, 0, 0:HALO:HALO - 1, :], 0.0).then_inc(lines_clear, 1)
            pool.memset(pick_row[:, :, :], 0.0).then_inc(pick_ready, 1)
            pool.memset(pick_half[:, :, :], 0.0).then_inc(pick_ready, 1)
            pool.memset(of_half[:, :], 0.0).then_inc(pick_ready, 1)
            pool.wait_ge(pick_ready, 3)
            for rows, base in ((pick_row, 0), (pick_half, PATCH + 1)):
                pool.affine_select(out=rows[:, :, :], in_=rows[:, :, :], compare_op=ALU.not_equal, fill=1.0,
                                   base=base, pattern=[[-1, 3], [2, CHUNKS]], channel_multiplier=-1).then_inc(pick_ready, 1)
            pool.affine_select(out=of_half[:, 0:1], in_=of_half[:, 0:1], compare_op=ALU.is_ge, fill=1.0,
                               base=-PATCH, pattern=[[0, 1]], channel_multiplier=1).then_inc(pick_ready, 1)
            pool.affine_select(out=of_half[:, 1:2], in_=of_half[:, 1:2], compare_op=ALU.is_ge, fill=1.0,
                               base=PATCH - 1, pattern=[[0, 1]], channel_multiplier=-1).then_inc(pick_ready, 1)
            pool.memset(lines[:, 0, 1:HALO - 1, 0:CH], 0.0).then_inc(consts, 1)
            pool.memset(lines[:, 0, 1:HALO - 1, PADLINE - CH:PADLINE], 0.0).then_inc(consts, 1)
            pool.memset(eps[:, :], TOK_EPS).then_inc(consts, 1)
            pool.memset(ident[:, :], 0.0).then_inc(const_step, 1)
            pool.wait_ge(const_step, 1)
            pool.affine_select(out=ident[:, :], in_=ident[:, :], compare_op=ALU.not_equal, fill=1.0,
                               base=0, pattern=[[-1, 128]], channel_multiplier=1).then_inc(consts, 1)
            end = PATCH + 1
            regions = [((0, HALO), (0, HALO), 0.0), ((1, end), (0, HALO), 1.0), ((0, HALO), (1, end), 1.0),
                       ((1, end), (1, end), 4.0), ((2, end - 1), (2, end - 1), 5.0),
                       ((1, 2), (1, 2), 3.0), ((1, 2), (end - 1, end), 3.0),
                       ((end - 1, end), (1, 2), 3.0), ((end - 1, end), (end - 1, end), 3.0)]
            for n, (r, q, v) in enumerate(regions):
                pool.wait_ge(const_step, 1 + n)
                last = n == len(regions) - 1
                pool.memset(count[:, r[0]:r[1], q[0]:q[1], :], v).then_inc(consts if last else const_step, 1)

            def window(s, u, bi, column):
                if late(s, SLOTS):
                    pool.wait_ge(mean_ready, s - 1)
                pool.nop(nofuse=True)
                pool.tensor_copy(win[:, u, :, :], lines[:, bi, :, bass.ds(column * (PATCH * CH), WIN)]).then_inc(win_ready, 1)

            pool.wait_ge(lines_in[0], LINES_LANDED)
            for s in range(SLOTS):
                window(s, s, 0, s)
            pool.wait_ge(w_summed, SHIFTS)
            pool.wait_ge(bias_mm, 1)
            clear(1)
            with pool.Fori(1, GRID // SLOTS) as it:
                for u in range(SLOTS):
                    window(it * SLOTS + u, u, 0, it * SLOTS + u)
            pool.wait_ge(lines_in[1], LINES_LANDED)
            with pool.Fori(0, GRID // SLOTS) as it:
                for u in range(SLOTS):
                    window(it * SLOTS + u + GRID, u, 1, it * SLOTS + u)

        CONSTS = 5

        @block.scalar
        def _(act):
            act.dma_start(factors_raw[0:PATCH, 1, :], beta.rearrange("(h f) -> h f", h=PATCH)).then_inc(f_in, 16)
            act.dma_start(factors_raw[PATCH:2 * PATCH, 1, :], beta.rearrange("(h f) -> h f", h=PATCH)).then_inc(f_in, 16)
            act.preload_act_table_set("natural_log_exp_and_others")
            act.dma_start(b_row[:, :], b.rearrange("(a d) -> a d", a=1).to_broadcast([ROWP, DIM])).then_inc(f_in, 16)
            act.wait_ge(lines_clear, 1)
            act.wait_ge(shift_clear, 1)
            load_neighbours(act, 0)
            for s in range(1, SHIFTS, 2):
                act.wait_ge(shift_clear, s + 2)
                load_shifted(act, s)
            act.wait_ge(consts, CONSTS)

            def centre(s, u, bi, column):
                act.wait_ge(mean_ready, s + 1)
                if late(s, SLOTS):
                    act.wait_ge(turned, s - 1)
                act.nop(nofuse=True)
                window = lines[:, bi, :, bass.ds(column * (PATCH * CH), WIN)]
                act.activation(centred[:, u, :, :], window, ACT.Identity, bias=negmean[:, u:u + 1]).then_inc(centred_ready, 1)
                act.wait_ge(centred_ready, s + 1)
                act.activation(square[:, u, :, :], centred[:, u, :, :], ACT.Square).then_inc(square_ready, 1)

            def split_hi(s, u):
                act.wait_ge(turned, s + 1)
                if late(s, SLOTS):
                    act.wait_ge(projected, s - 1)
                act.activation(winT_hi[:, u, :, :].rearrange("k (g t) p -> k g (t p)", t=TGROUP),
                               psT[:, u, :, 0:TGROUP * ROWP], ACT.Copy).then_inc(hi_ready, 1)

            def scale(s, u):
                act.wait_ge(var_ready, s + 1)
                act.activation(logvar[:, u:u + 1], var[:, u:u + 1], ACT.Ln, bias=eps[0:ROWP, :]).then_inc(log_ready, 1)
                if late(s, SLOTS):
                    act.wait_ge(refined, 4 * (s - 1))
                act.wait_ge(log_ready, s + 1)
                act.activation(rstd[:, u:u + 1], logvar[:, u:u + 1], ACT.Exp, scale=-0.5).then_inc(rstd_ready, 1)

            def body(k, u, bi, column):
                if isinstance(k, int) and k == 0:
                    act.wait_ge(w_summed, SHIFTS)
                    act.activation(w_hi[:, :, :], w_sum[:, :, :], ACT.Copy).then_inc(w_hi_ready, 1)
                if valid(k):
                    split_hi(k, u)
                if bi is not None:
                    centre(k + 2, u, bi, column)
                if valid(k):
                    scale(k, u)

            run(act, body)

        @block.vector
        def _(dve):
            dve.memset(zeros[:, :], 0.0).then_inc(shift_clear, 1)
            dve.memset(w_shift[:, 0, :, :], 0.0).then_inc(shift_clear, 1)
            dve.memset(w_shift[:, 1, :, :], 0.0).then_inc(shift_clear, 1)
            dve.memset(spread[:, :, :, :, :, :], 0.0).then_inc(picked, 1)
            for s in range(2, SHIFTS):
                dve.memset(w_shift[:, s, :, :], 0.0).then_inc(shift_clear, 1)
            dve.wait_ge(f_in, 80)
            dve.wait_ge(pick_ready, 7)
            dve.wait_ge(picked, 1)
            for s, (_, dc) in enumerate(SOURCE):
                for half in range(2):
                    for k in range(2):
                        dve.tensor_scalar(spread[:, k, s, half, dc:dc + PATCH, :],
                                          factors_raw[:, k, :].rearrange("h (w s c) -> h w s c", w=PATCH, s=SHIFTS)[:, :, s, :],
                                          of_half[:, half:half + 1], None, ALU.mult)
            dve.tensor_scalar(pick_row[:, :, :], pick_row[:, :, :], of_half[:, 0:1], None, ALU.mult).then_inc(picked, 1)
            dve.wait_ge(picked, 2)
            dve.scalar_tensor_tensor(out=pick_row[:, :, :], in0=pick_half[:, :, :], scalar=of_half[:, 1:2], in1=pick_row[:, :, :],
                                     op0=ALU.mult, op1=ALU.add).then_inc(spread_ready, 1)
            dve.wait_ge(factors_mm, 1)
            dve.tensor_copy(factors[:, :, :, :].rearrange("p k s t -> p (k s t)"), psO[0:CHUNK, 1, 0:2 * SHIFTS * CHUNKS]).then_inc(factors_ready, 1)
            dve.wait_ge(factors_ready, 1)
            for s in range(SHIFTS):
                dve.wait_ge(shift_in[s], SHIFTED_LANDED)
                if s:
                    dve.wait_ge(w_summed, s)
                for t in range(CHUNKS):
                    if s == 0:
                        mm = dve.tensor_scalar(w_sum[:, t, :], w_shift[:, s, t, :], factors[:, 0, s, t:t + 1], None, ALU.mult)
                    else:
                        mm = dve.scalar_tensor_tensor(out=w_sum[:, t, :], in0=w_shift[:, s, t, :], scalar=factors[:, 0, s, t:t + 1],
                                                      in1=w_sum[:, t, :], op0=ALU.mult, op1=ALU.add)
                mm.then_inc(w_summed, 1)
            dve.wait_ge(consts, CONSTS)

            def mean(s, u):
                if late(s, SLOTS):
                    dve.wait_ge(var_ready, s - 1)
                    dve.wait_ge(square_ready, s - 1)
                dve.wait_ge(win_ready, s + 1)
                dve.tensor_tensor_reduce(square[:, u, :, :], win[:, u, :, :], count_rows, -1.0 / FEATURES, 0.0,
                                         ALU.mult, ALU.add, negmean[:, u:u + 1]).then_inc(mean_ready, 1)

            def split_lo(s, u):
                dve.wait_ge(hi_ready, s + 1)
                dve.tensor_tensor(winT_lo[:, u, :, :].rearrange("k (g t) p -> k g (t p)", t=TGROUP),
                                  psT[:, u, :, 0:TGROUP * ROWP],
                                  winT_hi[:, u, :, :].rearrange("k (g t) p -> k g (t p)", t=TGROUP).bitcast(F32),
                                  ALU.subtract).then_inc(lo_ready, 1)

            def variance(s, u):
                dve.wait_ge(square_ready, s + 1)
                dve.tensor_tensor_reduce(square[:, u, :, :], square[:, u, :, :], count_rows, 1.0 / FEATURES, 0.0,
                                         ALU.mult, ALU.add, var[:, u:u + 1]).then_inc(var_ready, 1)

            def refine(s, u, part):
                y, a, scale = rstd[:, u:u + 1], newton[:, u, 0:1], newton[:, u, 1:2]
                if part == 0:
                    dve.wait_ge(rstd_ready, s + 1)
                    step = dve.tensor_tensor(a, y, y, ALU.mult)
                else:
                    dve.wait_ge(refined, 4 * s + part)
                if part == 1:
                    step = dve.scalar_tensor_tensor(out=a, in0=var[:, u:u + 1], scalar=TOK_EPS, in1=a, op0=ALU.add, op1=ALU.mult)
                if part == 2:
                    step = dve.tensor_scalar(a, a, -0.5, 1.5, ALU.mult, ALU.add)
                if part == 3:
                    step = dve.tensor_tensor(scale, y, a, ALU.mult)
                step.then_inc(refined, 1)

            def finish(s, u):
                if late(s, SLOTS):
                    dve.wait_ge(tok_out[u], of_slot(s, u, 16))
                dve.wait_ge(refined, 4 * s + 4)
                dve.wait_ge(projected, s + 1)
                dve.scalar_tensor_tensor(out=tok[:, u, :], in0=psO[:, u, 0:DIM], scalar=newton[:, u, 1:2], in1=bias[:, :],
                                         op0=ALU.mult, op1=ALU.add).then_inc(tok_ready, 1)

            def body(k, u, bi, column):
                if isinstance(k, int) and k == 0:
                    dve.wait_ge(w_hi_ready, 1)
                    dve.tensor_tensor(w_lo[:, :, :], w_sum[:, :, :], w_hi[:, :, :].bitcast(F32), ALU.subtract).then_inc(w_lo_ready, 1)
                    dve.wait_ge(bias_mm, 1)
                    dve.tensor_tensor(bias[:, :], psO[:, 0, 0:DIM], b_row[:, :], ALU.add).then_inc(bias_ready, 1)
                last = valid(k - 1)
                if bi is not None:
                    mean(k + 2, u)
                if last:
                    refine(k - 1, 1 - u, 0)
                if valid(k):
                    split_lo(k, u)
                if last:
                    refine(k - 1, 1 - u, 1)
                    refine(k - 1, 1 - u, 2)
                if valid(k + 1):
                    variance(k + 1, 1 - u)
                if last:
                    refine(k - 1, 1 - u, 3)
                    finish(k - 1, 1 - u)

            run(dve, body)

        @block.tensor
        def _(pe):
            pe.wait_ge(spread_ready, 1)
            for k in range(2):
                for s, (dr, _) in enumerate(SOURCE):
                    at = (k * SHIFTS + s) * CHUNKS
                    mm = pe.matmul(psO[0:CHUNK, 1, at:at + CHUNKS], spread[:, k, s, :, :, :].rearrange("h a q c -> h (a q c)"),
                                   pick_row[:, dr, :], start=True, stop=True)
            mm.then_inc(factors_mm, 1)
            pe.wait_ge(factors_ready, 1)
            for s in range(SHIFTS):
                pe.wait_ge(shift_in[s], SHIFTED_LANDED)
                for t in range(CHUNKS):
                    mm = pe.matmul(psO[:, 0, 0:DIM], factors[:, 1, s, t:t + 1].to_broadcast([CHUNK, ROWP]), w_shift[:, s, t, :],
                                   start=(s == 0 and t == 0), stop=(s == SHIFTS - 1 and t == CHUNKS - 1))
            mm.then_inc(bias_mm, 1)
            pe.wait_ge(consts, CONSTS)

            def turn(s, u):
                if late(s, SLOTS):
                    pe.wait_ge(lo_ready, s - 1)
                pe.wait_ge(centred_ready, s + 1)
                flat = centred[:, u, :, :].rearrange("p r w -> p (r w)")
                for t in range(CHUNKS):
                    g, k = t // TGROUP, t % TGROUP
                    mm = pe.transpose(psT[:, u, g, k * ROWP:(k + 1) * ROWP], flat[:, t * CHUNK:(t + 1) * CHUNK], ident[0:ROWP, 0:ROWP])
                mm.then_inc(turned, 1)

            def project(s, u):
                if late(s, SLOTS):
                    pe.wait_ge(tok_ready, s - 1)
                pe.wait_ge(lo_ready, s + 1)
                for t in range(CHUNKS):
                    hi, lo = winT_hi[:, u, t, :], winT_lo[:, u, t, :]
                    pe.matmul(psO[:, u, 0:DIM], lo, w_hi[:, t, :], start=(t == 0), stop=False)
                    pe.matmul(psO[:, u, 0:DIM], hi, w_lo[:, t, :], start=False, stop=False)
                    mm = pe.matmul(psO[:, u, 0:DIM], hi, w_hi[:, t, :], start=False, stop=(t == CHUNKS - 1))
                mm.then_inc(projected, 1)

            def body(k, u, bi, column):
                if valid(k + 1):
                    turn(k + 1, 1 - u)
                if isinstance(k, int) and k == 0:
                    pe.wait_ge(w_lo_ready, 1)
                    pe.wait_ge(bias_ready, 1)
                if valid(k):
                    project(k, u)

            run(pe, body)


HEADS, RANK = 12, 64
HEAD_DIM = DIM // HEADS
LN_EPS = 1e-5
HALF = DIM // 2
NTILES = 3
TILE_ROWS = [PTILE, PTILE, TEXT]
TILE_AT = [0, PTILE, 2 * PTILE]
KEYS = N // 3
GROUP = 4
GROUPS = HEADS // GROUP
SCORE_SCALE = RANK ** -0.5
BANK = 512
POST_SCALE = 8
POST_TURN, POST_LOGITS, POST_EXP, POST_RANKS = 1, 2, 4, 7
LN_SCALE, TURN_AT, LATENTS_AT, VALUES_AT = 2, 5, 6, 6
POST_SECOND = 9
PICKS_AT = 3
RANK_COL, LOGIT_COL = 400, 448
EXPERTS, HIDDEN, TOPK = 8, 512, 2
TOKENS = IMAGES * N
ROW = DIM + 1
SPACE = -(-(TOKENS + 127) // 128) * 128
BLOCKS = (TOPK * TOKENS + EXPERTS * 127) // 128
SPARE = BLOCKS - -(-TOPK * TOKENS // 128)
MASKED = -3e38
PIECES = [(c, max(a, c * N), min(a + BANK, (c + 1) * N))
          for a in (0, BANK) for c in range(3) if max(a, c * N) < min(a + BANK, (c + 1) * N)]


def attention(nc, txt, basis_w, core, head_residual, value_w, value_b, router_w, h_dram, h2_dram, rows_dram, kept,
              w1, w1_raw, w1_in):
    picks, pick_probs, places, importance = kept
    with ExitStack() as ctx:
        def sb(name, shape, dt=F32):
            return ctx.enter_context(nc.sbuf_tensor(name, shape, dt))

        def psum(name, shape, dt=F32):
            return ctx.enter_context(nc.psum_tensor(name, shape, dt))

        def sem(name):
            return ctx.enter_context(nc.semaphore(name))

        ident = sb("identA", [128, 128])
        eps = sb("epsA", [128, 1])
        basis_raw = sb("basis_raw", [RANK, DIM])
        basisT = sb("basisT", [HALF, 2, 2, RANK])
        value_raw = sb("value_raw", [HALF, 2, DIM])
        valueT = sb("valueT", [HALF, 2, DIM])
        value_bias = sb("value_bias", [KEYS, DIM])
        residual = sb("residual", [128, HEADS, RANK])
        core_sb = sb("core_sb", [128, RANK])
        mean_mat = sb("mean_mat", [128, RANK])
        mats_hi = sb("mats_hi", [128, HEADS, 2, RANK], F32R)
        mats_lo = sb("mats_lo", [128, HEADS, 2, RANK], F32R)

        h_front = sb("h_front", [128, 2, NTILES, DIM])
        h_back = sb("h_back", [128, 2, NTILES, DIM])
        stats = sb("stats", [128, NTILES, 6])
        moments = sb("moments", [128, NTILES, 2])
        logvar = sb("logvarA", [128, NTILES])
        rstd = sb("rstdA", [128, NTILES])
        newton = sb("newton", [128, 3, NTILES])
        xn = sb("xn", [128, NTILES, DIM])
        xT = sb("xT", [HALF, 2, N])
        lat_next = sb("lat_next", [128, N])
        values_next = sb("values_next", [KEYS, 3, DIM])
        lat = sb("lat", [128, 2, N], F32R)
        lat_one = sb("lat_one", [RANK + 1, 2, N], F32R)
        values = sb("values", [KEYS, 2, 3, HEADS, 32])
        q_hi = sb("q_hi", [128, 2, HEADS, N], F32R)
        q_lo = sb("q_lo", [RANK + 1, 2, HEADS, N], F32R)
        row_max = sb("row_max", [KEYS, 2, 3, HEADS])
        max_rows = sb("max_rows", [HEADS, N], F32R)
        probs = sb("probs", [KEYS, 2 * GROUP, 3 * N])
        ctx_sb = sb("ctx_sb", [128, N])
        recip = sb("recip", [128, NTILES, GROUP, 1])
        scaled = sb("scaled", [128, 2, NTILES, GROUP, HEAD_DIM])

        router_raw = sb("router_raw", [EXPERTS, DIM])
        routerT = sb("routerT", [HALF, 2, EXPERTS])
        before = sb("before", [128, 128], BF16)
        all_ones = sb("all_ones", [128, 128], BF16)
        valid = sb("valid", [128, NTILES])
        order_int = sb("order_int", [128, EXPERTS + TOPK * NTILES], I32)
        order = sb("order", [128, EXPERTS])
        goal = sb("goal", [128, TOPK, NTILES, 1])
        newton2 = sb("newton2", [128, 3, NTILES])
        stats2 = sb("stats2", [128, NTILES, 6])
        moments2 = sb("moments2", [128, NTILES, 2])
        logvar2 = sb("logvar2", [128, NTILES])
        rstd2 = sb("rstd2", [128, NTILES])
        routed = sb("routed", [128, 2, TOPK, NTILES, ROW])
        x2T = sb("x2T", [HALF, 2, N])
        logits = sb("logits", [128, NTILES, EXPERTS])
        rest = sb("rest", [128, NTILES, EXPERTS])
        key = sb("key", [128, NTILES, EXPERTS])
        top = sb("top", [128, NTILES])
        expo = sb("expo", [128, NTILES, EXPERTS])
        total = sb("total", [128, NTILES])
        sums = sb("sums", [128, NTILES])
        summed = sb("summed", [128, NTILES, 1])
        share = sb("shareA", [128, NTILES, EXPERTS])
        halves = sb("halves", [128, NTILES * TOPK, 4])
        pick = sb("pick", [128, NTILES, TOPK, EXPERTS])
        picked = sb("picked", [128, NTILES, EXPERTS], BF16)
        of_pick = sb("of_pick", [128, NTILES, TOPK, EXPERTS])
        probs_now = sb("probs_now", [128, NTILES * TOPK, 1])
        rank_sb = sb("rank_sb", [128, NTILES + 1, EXPERTS])
        place = sb("place", [128, NTILES, TOPK])
        place_int = sb("place_int", [128, 2, NTILES, TOPK], I32)

        ps_s = psum("ps_s", [128, 2 * BANK])
        ps_t = psum("ps_t", [128, 2 * BANK])
        ps_q = psum("ps_q", [128, BANK])
        ps_v = psum("ps_v", [128, BANK])
        ps_m = psum("ps_m", [128, 2, BANK])

        one_row = sem("one_row")
        w_in, const_step, consts = sem("w_inA"), sem("const_stepA"), sem("constsA")
        w_turned, w_ready, mat_step = sem("w_turned"), sem("w_readyA"), sem("mat_step")
        front_in = [sem(f"front_in{i}") for i in range(2)]
        back_in = [sem(f"back_in{i}") for i in range(2)]
        max_in = [sem(f"max_in{i}") for i in range(2)]
        h2_out = [sem(f"h2_out{i}") for i in range(2)]
        dve_ln = sem("dve_ln")
        act_ln = sem("act_ln")
        refined = sem("refined")
        xn_ready = sem("xn_ready")
        x_turned = sem("x_turned")
        xT_ready = sem("xT_ready")
        lat_mm = sem("lat_mm")
        lat_hi = sem("lat_hi")
        lat_lo = sem("lat_lo")
        lat_one_ready = sem("lat_one_ready")
        v_mm = sem("v_mm")
        lat_staged = sem("lat_staged")
        v_ready = sem("v_ready")
        values_ready = sem("values_ready")
        q_mm = sem("q_mm")
        q_hi_ready = sem("q_hi_ready")
        q_lo_ready = sem("q_lo_ready")
        s_mm = sem("s_mm")
        max_ready = sem("max_ready")
        max_turned = sem("max_turned")
        max_rows_ready = sem("max_rows_ready")
        t_mm = sem("t_mm")
        probs_ready = sem("probs_ready")
        pv_mm = sem("pv_mm")
        ctx_ready = sem("ctx_ready")
        ctx_turned = sem("ctx_turned")
        recip_ready = sem("recip_ready")
        scaled_ready = sem("scaled_ready")
        h2_ready = sem("h2_ready")

        dve_ln2 = sem("dve_ln2")
        act_ln2 = sem("act_ln2")
        refined2 = sem("refined2")
        x2_ready = sem("x2_ready")
        x2_copied = sem("x2_copied")
        x2_turned = sem("x2_turned")
        x2T_ready = sem("x2T_ready")
        logit_mm = sem("logit_mm")
        route = sem("route")
        placed = sem("placed")
        expo_ready = sem("expo_ready")
        sums_ready = sem("sums_ready")
        inverse_ready = sem("inverse_ready")
        rank_mm = sem("rank_mm")
        ranks_ready = sem("ranks_ready")
        scattered = [sem(f"scattered{i}") for i in range(2)]
        order_in = sem("order_in")
        order_ready = sem("order_ready")

        block = ctx.enter_context(nc.Block())

        FIRST_BANKS = [ps_s, ps_t]

        PARTS = [(0, 2, PTILE), (2, 3, TEXT)]

        def run(engine, prologue, body, epilogue):
            prologue()
            body(0, 0, True, True, False, False, False)
            body(1, 1, True, True, True, False, False)
            body(2, 0, True, True, True, True, False)
            body(3, 1, True, True, True, True, True)
            with engine.Fori(2, (IMAGES - 2) // 2) as it:
                for p in range(2):
                    body(it * 2 + p, p, True, True, True, True, True)
            body(IMAGES - 2, 0, True, False, True, True, True)
            body(IMAGES - 1, 1, False, False, True, True, True)
            epilogue()

        LOGITS_READ, MAX_TAKEN, PICKED = 1, 3, 15
        PLACED = 16

        def of_pair(i, p, each):
            return (i // 2 + 1) * each if isinstance(i, int) else (i - p) * (each // 2) + each

        @block.sync
        def _(sp):
            def load(dst, i, p, landed):
                sp.dma_start(dst[0:PTILE, p, 0:2, :],
                             h_dram[bass.ds(i, 1), 0:2 * PTILE, :].rearrange("a (t p) d -> p (a t) d", t=2)).then_inc(landed[p], 16)
                sp.dma_start(dst[:, p, 2, :], txt[bass.ds(i, 1), :, :].rearrange("a p d -> (a p) d")).then_inc(landed[p], 16)

            def prologue():
                sp.wait_ge(consts, 1)
                load(h_front, 0, 0, front_in)
                sp.dma_start(basis_raw[:, :], basis_w).then_inc(w_in, 16)
                for d in range(2):
                    sp.dma_start(residual[d * RANK:(d + 1) * RANK, :, :], head_residual.rearrange("h r s -> r h s")).then_inc(w_in, 16)
                    sp.dma_start(core_sb[d * RANK:(d + 1) * RANK, :], core).then_inc(w_in, 16)
                sp.dma_start(value_raw[:, :, :], value_w.rearrange("(k p) h -> p k h", k=2)).then_inc(w_in, 16)
                sp.dma_start(value_bias[:, :], value_b.rearrange("(a d) -> a d", a=1).to_broadcast([KEYS, DIM])).then_inc(w_in, 16)
                sp.dma_start(router_raw[:, :], router_w).then_inc(w_in, 16)
                load(h_front, 1, 1, front_in)
                sp.wait_ge(consts, 2)
                for i in range(2):
                    load(h_back, i, i, back_in)

            def body(i, p, front, prep, post, place, send):
                if prep:
                    sp.wait_ge(xn_ready, 3 * (i + 1))
                    load(h_front, i + 2, p, front_in)
                if post:
                    store(i - 1, 1 - p)
                if post and front:
                    sp.wait_ge(x2_ready, 3 * i)
                    sp.wait_ge(h2_out[1 - p], of_pair(i - 1, 1 - p, 32))
                    load(h_back, i + 1, 1 - p, back_in)

            def store(i, p):
                sp.wait_ge(h2_ready, 2 * GROUPS * (i + 1))
                sp.dma_start(h2_dram[bass.ds(i, 1), 0:2 * PTILE, :].rearrange("a (t p) d -> p (a t) d", t=2),
                             h_back[0:PTILE, p, 0:2, :]).then_inc(h2_out[p], 16)
                sp.dma_start(h2_dram[bass.ds(i, 1), 2 * PTILE:N, :].rearrange("a p d -> (a p) d"), h_back[:, p, 2, :]).then_inc(h2_out[p], 16)

            def prologue2():
                prologue()
                sp.dma_start(w1_raw[:, :, :], w1.rearrange("e (c p) h -> p (e c) h", p=128)).then_inc(w1_in, 16)

            def epilogue():
                store(IMAGES - 1, 1)
                for p in range(2):
                    sp.wait_ge(h2_out[p], 32 * IMAGES // 2)

            run(sp, prologue2, body, epilogue)

        @block.gpsimd
        def _(pool):
            pool.memset(h_front[:, :, :, :], 0.0).then_inc(consts, 1)
            pool.memset(h_back[:, :, :, :], 0.0).then_inc(consts, 1)
            pool.memset(ident[:, :], 0.0).then_inc(const_step, 1)
            pool.memset(eps[:, :], LN_EPS).then_inc(consts, 1)
            pool.wait_ge(const_step, 1)
            pool.affine_select(out=ident[:, :], in_=ident[:, :], compare_op=ALU.not_equal, fill=1.0,
                               base=0, pattern=[[-1, 128]], channel_multiplier=1).then_inc(consts, 1)
            pool.memset(values[:, :, :, :, :], 0.0).then_inc(const_step, 1)
            pool.wait_ge(const_step, 2)
            pool.memset(values[:, :, :, :, HEAD_DIM:HEAD_DIM + 1], 1.0).then_inc(consts, 1)

            for k in range(TOPK):
                for t in range(NTILES):
                    at = EXPERTS + k * NTILES + t
                    pool.iota(order_int[:, at:at + 1], [[0, 1]], base=k * TOKENS + TILE_AT[t], channel_multiplier=1).then_inc(order_in, 1)
            pool.iota(order_int[:, 0:EXPERTS], [[-1, EXPERTS]], base=EXPERTS, channel_multiplier=0).then_inc(order_in, 1)
            pool.memset(all_ones[:, :], 1.0).then_inc(order_in, 1)
            pool.memset(valid[:, :], 1.0).then_inc(const_step, 1)
            pool.wait_ge(const_step, 3)
            pool.wait_ge(order_in, 8)
            pool.affine_select(out=before[:, :], in_=all_ones[:, :], compare_op=ALU.is_gt, fill=0.0, base=0,
                               pattern=[[1, 128]], channel_multiplier=-1).then_inc(order_in, 1)
            pool.affine_select(out=valid[:, 0:2], in_=valid[:, 0:2], compare_op=ALU.is_gt, fill=0.0, base=PTILE,
                               pattern=[[0, 2]], channel_multiplier=-1).then_inc(order_in, 1)

            def over_tiles(ap):
                return ap.rearrange("p (t e) -> p t e", t=1).to_broadcast([128, NTILES, EXPERTS])

            def over_picks(ap):
                return ap.rearrange("p t (k e) -> p t k e", k=1).to_broadcast([128, NTILES, TOPK, EXPERTS])

            def places_of(i, p):
                n = 0

                def step(instruction, wait=True):
                    nonlocal n
                    n += 1
                    instruction.then_inc(placed, 1)
                    if wait:
                        pool.wait_ge(placed, PLACED * i + n)

                def sum_last(out, ap):
                    rows = ap.shape[1]
                    half = halves[:, 0:rows, :]
                    step(pool.tensor_tensor(half, ap[:, :, 0:4], ap[:, :, 4:8], ALU.add))
                    step(pool.tensor_tensor(half[:, :, 0:2], half[:, :, 0:2], half[:, :, 2:4], ALU.add))
                    step(pool.tensor_tensor(out, half[:, :, 0:1], half[:, :, 1:2], ALU.add))

                pool.wait_ge(route, PICKED * (i + 1))
                pool.wait_ge(inverse_ready, i + 1)
                step(pool.tensor_tensor(share[:, :, :], expo[:, :, :], summed[:, :, :].to_broadcast([128, NTILES, EXPERTS]), ALU.mult))
                step(pool.tensor_tensor(importance[:, :, :], importance[:, :, :], share[:, :, :], ALU.add), wait=False)
                step(pool.tensor_tensor(of_pick[:, :, :, :], pick[:, :, :, :], over_picks(share[:, :, :]), ALU.mult))
                sum_last(probs_now[:, :, :], of_pick[:, :, :, :].rearrange("p t k e -> p (t k) e"))
                pool.nop(nofuse=True)
                step(pool.tensor_copy(pick_probs[:, bass.ds(i, 1), :, :].rearrange("p i t k -> p (i t k)"), probs_now[:, :, 0]), wait=False)
                step(pool.tensor_copy(picks[:, bass.ds(i, 1), :, :, :].rearrange("p i t k e -> p (i t) k e"), pick[:, :, :, :]), wait=False)
                pool.wait_ge(ranks_ready, i + 1)
                step(pool.tensor_tensor(share[:, :, :], rank_sb[:, 0:NTILES, :], over_tiles(places[:, :]), ALU.add))
                step(pool.tensor_tensor(places[:, :], rank_sb[:, NTILES, :], places[:, :], ALU.add))
                pool.nop(nofuse=True)
                step(pool.tensor_copy(routed[:, p, :, :, DIM:ROW], goal[:, :, :, :]))
                step(pool.tensor_tensor(of_pick[:, :, :, :], pick[:, :, :, :], over_picks(share[:, :, :]), ALU.mult))
                sum_last(place[:, :, :].rearrange("p t (k o) -> p (t k) o", o=1), of_pick[:, :, :, :].rearrange("p t k e -> p (t k) e"))
                pool.nop(nofuse=True)
                pool.tensor_scalar(goal[:, :, :, :], goal[:, :, :, :], float(N), None, ALU.add)
                step(pool.tensor_copy(place_int[:, p, :, :], place[:, :, :]))
                assert n == PLACED

            def scatter(i, p):
                pool.wait_ge(x2_copied, i + 1)
                pool.nop(nofuse=True)
                for t, rows in enumerate(TILE_ROWS):
                    for k in range(TOPK):
                        pool.indirect_dma_start(rows_dram[:, :], bass.IndirectOffsetOnAxis(place_int[0:rows, p, t, k:k + 1], 0),
                                                routed[0:rows, p, k, t, :], None).then_inc(scattered[p], 16)

            def copy(i, p):
                if not isinstance(i, int) or i >= 2:
                    pool.wait_ge(t_mm, HEADS * (i - 1))
                pool.wait_ge(lat_lo, i + 1)
                pool.nop(nofuse=True)
                pool.tensor_copy(lat_one[0:RANK, p, :], lat[0:RANK, p, :].bitcast(F32)).then_inc(lat_one_ready, 1)
                if not isinstance(i, int) or i >= 2:
                    pool.wait_ge(pv_mm, GROUPS * (i - 1))
                pool.wait_ge(v_ready, 2 * (i + 1))
                pool.nop(nofuse=True)
                pool.tensor_copy(values[:, p, :, :, 0:HEAD_DIM],
                                 values_next[:, :, :].rearrange("p c (h d) -> p c h d", h=HEADS)).then_inc(values_ready, 1)

            def residual_add(i, p, g):
                if g == 0:
                    pool.wait_ge(back_in[p], of_pair(i, p, 32))
                pool.wait_ge(scaled_ready, 2 * (GROUPS * i + g + 1))
                pool.nop(nofuse=True)
                for a, b, rows in PARTS:
                    at = h_back[0:rows, p, a:b, g * GROUP * HEAD_DIM:(g + 1) * GROUP * HEAD_DIM]
                    pool.tensor_tensor(at, at, scaled[0:rows, (GROUPS * p + g) % 2, a:b, :, :].rearrange("p t b e -> p t (b e)"),
                                       ALU.add).then_inc(h2_ready, 1)

            def prologue():
                copy(0, 0)
                copy(1, 1)
                pool.wait_ge(order_ready, 4)

            def body(i, p, front, prep, post, place, send):
                if post:
                    residual_add(i - 1, 1 - p, 1)
                if send:
                    scatter(i - 3, 1 - p)
                if post:
                    residual_add(i - 1, 1 - p, 2)
                if front and post:
                    copy(i + 1, 1 - p)
                residual_add(i, p, 0)
                if place:
                    places_of(i - 2, p)

            def epilogue():
                residual_add(IMAGES - 1, 1, 1)
                residual_add(IMAGES - 1, 1, 2)
                scatter(IMAGES - 3, 1)
                places_of(IMAGES - 2, 0)
                scatter(IMAGES - 2, 0)
                places_of(IMAGES - 1, 1)
                scatter(IMAGES - 1, 1)
                for p in range(2):
                    pool.wait_ge(scattered[p], 16 * TOPK * NTILES * IMAGES // 2)

            run(pool, prologue, body, epilogue)

        @block.scalar
        def _(act):
            act.preload_act_table_set("natural_log_exp_and_others")
            act.wait_ge(consts, 5)

            def layernorm_scale(i):
                act.wait_ge(dve_ln, 6 * (i + 1))
                act.activation(logvar[:, :], moments[:, :, 1], ACT.Ln, bias=eps[:, :]).then_inc(act_ln, 1)
                act.wait_ge(act_ln, 2 * i + 1)
                act.activation(rstd[:, :], logvar[:, :], ACT.Exp, scale=-0.5).then_inc(act_ln, 1)

            def transposed(i):
                act.wait_ge(x_turned, i + 1)
                act.activation(xT[:, :, :], ps_m[0:HALF, :, 0:N], ACT.Copy).then_inc(xT_ready, 1)

            def latents_out(i):
                act.wait_ge(lat_mm, i + 1)
                if not isinstance(i, int) or i > 0:
                    act.wait_ge(lat_lo, i)
                act.activation(lat_next[:, :], ps_q[:, 0:N], ACT.Copy).then_inc(lat_staged, 1)

            def latents(i, p):
                if not isinstance(i, int) or i >= 2:
                    act.wait_ge(t_mm, HEADS * (i - 1))
                act.wait_ge(lat_staged, i + 1)
                act.activation(lat[:, p, :], lat_next[:, :], ACT.Copy).then_inc(lat_hi, 1)

            def products(i, g):
                n = GROUPS * i + g
                act.wait_ge(pv_mm, n + 1)
                if not isinstance(n, int) or n > 0:
                    act.wait_ge(ctx_turned, n)
                act.activation(ctx_sb[:, :], ps_v[:, 0:N], ACT.Copy).then_inc(ctx_ready, 1)

            def maximum_rows(i, p):
                act.wait_ge(max_turned, i + 1)
                if not isinstance(i, int) or i > 0:
                    act.wait_ge(max_in[1 - p], of_pair(i - 1, 1 - p, 16))
                act.activation(max_rows[:, :], ps_m[0:HEADS, 1, 0:N], ACT.Copy).then_inc(max_rows_ready, 1)

            def send_maxima(i, p):
                act.wait_ge(max_rows_ready, i + 1)
                act.dma_start(q_lo[RANK:RANK + 1, p, :, :].bitcast(F32), max_rows[:, :].bitcast(F32)).then_inc(max_in[p], 16)

            def query(i, p, h):
                act.wait_ge(q_mm, HEADS * i + h + 1)
                act.activation(q_hi[:, p, h, :], ps_q[:, 0:N], ACT.Copy).then_inc(q_hi_ready, 1)

            def exponentials(i, h, slot, free):
                if free:
                    act.wait_ge(pv_mm, GROUPS * i + h // GROUP - 1)
                act.wait_ge(t_mm, HEADS * i + h + 1)
                act.activation(probs[:, slot, :], ps_t[0:KEYS, 0:3 * N], ACT.Exp, scale=SCORE_SCALE).then_inc(probs_ready, 1)

            def post_scale(i):
                act.wait_ge(dve_ln2, 6 * (i + 1))
                act.activation(logvar2[:, :], moments2[:, :, 1], ACT.Ln, bias=eps[:, :]).then_inc(act_ln2, 1)
                act.wait_ge(act_ln2, 2 * i + 1)
                act.activation(rstd2[:, :], logvar2[:, :], ACT.Exp, scale=-0.5).then_inc(act_ln2, 1)

            def post_second(i, p):
                act.wait_ge(x2_ready, 3 * (i + 1))
                act.activation(routed[:, p, 1, :, 0:DIM], routed[:, p, 0, :, 0:DIM], ACT.Copy).then_inc(x2_copied, 1)

            def post_transposed(i):
                act.wait_ge(x2_turned, i + 1)
                act.activation(x2T[:, :, :], ps_m[0:HALF, :, 0:N], ACT.Copy).then_inc(x2T_ready, 1)

            def post_exponentials(i):
                act.wait_ge(route, PICKED * i + MAX_TAKEN)
                act.activation(expo[:, :, :], expo[:, :, :], ACT.Exp).then_inc(expo_ready, 1)

            def post_ranks(i):
                act.wait_ge(rank_mm, i + 1)
                if not isinstance(i, int) or i > 0:
                    act.wait_ge(placed, PLACED * i)
                act.activation(rank_sb[:, :, :], ps_v[:, RANK_COL:RANK_COL + (NTILES + 1) * EXPERTS]
                               .rearrange("p (t e) -> p t e", t=NTILES + 1), ACT.Copy).then_inc(ranks_ready, 1)

            def prologue():
                layernorm_scale(0)
                act.wait_ge(mat_step, 3)
                act.activation(mats_hi[:, :, :, :],
                               residual[:, :, :].rearrange("p h (a s) -> p h a s", a=1).to_broadcast([128, HEADS, 2, RANK]),
                               ACT.Copy).then_inc(mat_step, 1)
                layernorm_scale(1)
                for i in range(2):
                    transposed(i)
                    latents_out(i)
                    latents(i, i)
                for h in range(HEADS):
                    query(0, 0, h)
                maximum_rows(0, 0)
                send_maxima(0, 0)

            def body(i, p, front, prep, post, place, send):
                for h in range(HEADS):
                    if post and h == 0:
                        maximum_rows(i, p)
                    if front:
                        query(i + 1, 1 - p, h)
                    if post and h == 0:
                        send_maxima(i, p)
                    group = GROUPS * p + h // GROUP
                    exponentials(i, h, (group % 2) * GROUP + h % GROUP, not isinstance(i, int) or GROUPS * i + h // GROUP >= 2)
                    if h == 1 and post:
                        products(i - 1, 2)
                    if h in (6, 10):
                        products(i, h // GROUP - 1)
                    if post and h == POST_SCALE:
                        post_scale(i - 1)
                    if place and h == POST_TURN:
                        post_transposed(i - 2)
                    if place and h == POST_SECOND:
                        post_second(i - 2, p)
                    if place and h == POST_EXP:
                        post_exponentials(i - 2)
                    if place and h == POST_RANKS:
                        post_ranks(i - 2)
                    if prep and h == LN_SCALE:
                        layernorm_scale(i + 2)
                    if prep and h == TURN_AT:
                        transposed(i + 2)
                    if prep and h == LATENTS_AT:
                        latents_out(i + 2)
                if prep:
                    latents(i + 2, p)

            def epilogue():
                products(IMAGES - 1, GROUPS - 1)
                post_second(IMAGES - 2, 0)
                post_transposed(IMAGES - 2)
                post_scale(IMAGES - 1)
                post_exponentials(IMAGES - 2)
                post_ranks(IMAGES - 2)
                post_second(IMAGES - 1, 1)
                post_transposed(IMAGES - 1)
                post_exponentials(IMAGES - 1)
                post_ranks(IMAGES - 1)

            run(act, prologue, body, epilogue)

        @block.vector
        def _(dve):
            dve.memset(lat_one[RANK:RANK + 1, :, :].bitcast(F32), -1.0).then_inc(one_row, 1)
            def layernorm_stats(i, p):
                dve.wait_ge(front_in[p], of_pair(i, p, 32))
                for t in range(NTILES):
                    dve.bn_stats(stats[:, t, :], h_front[:, p, t, :]).then_inc(dve_ln, 1)

            def layernorm_moments(i):
                dve.wait_ge(dve_ln, 6 * i + 3)
                dve.nop(nofuse=True)
                for t in range(NTILES):
                    dve.bn_aggr(moments[:, t, :], stats[:, t, :]).then_inc(dve_ln, 1)

            def refine(part, i, work, y, variance, counted, scale_ready):
                square, half, scale = (work[:, k, :] for k in range(3))
                if part == 0:
                    dve.wait_ge(scale_ready, 2 * (i + 1))
                    step = dve.tensor_tensor(square, y, y, ALU.mult)
                else:
                    dve.wait_ge(counted, 4 * i + part)
                if part == 1:
                    step = dve.scalar_tensor_tensor(out=half, in0=variance, scalar=LN_EPS, in1=square, op0=ALU.add, op1=ALU.mult)
                if part == 2:
                    step = dve.tensor_scalar(half, half, -0.5, 1.5, ALU.mult, ALU.add)
                if part == 3:
                    step = dve.tensor_tensor(scale, y, half, ALU.mult)
                step.then_inc(counted, 1)

            def layernorm_refine(i, part):
                refine(part, i, newton, rstd[:, :], moments[:, :, 1], refined, act_ln)

            def post_refine(i, part):
                refine(part, i, newton2, rstd2[:, :], moments2[:, :, 1], refined2, act_ln2)

            def layernorm(i, p):
                if not isinstance(i, int) or i > 0:
                    dve.wait_ge(x_turned, i)
                dve.wait_ge(refined, 4 * i + 4)
                for t in range(NTILES):
                    dve.tensor_scalar(xn[:, t, :], h_front[:, p, t, :], moments[:, t, 0:1], newton[:, 2, t:t + 1],
                                      ALU.subtract, ALU.mult).then_inc(xn_ready, 1)

            def latents(i, p):
                dve.wait_ge(lat_hi, i + 1)
                dve.tensor_tensor(lat[RANK:128, p, :], lat_next[RANK:128, :], lat[RANK:128, p, :].bitcast(F32),
                                  ALU.subtract).then_inc(lat_lo, 1)

            def value(i):
                dve.wait_ge(v_mm, i + 1)
                if not isinstance(i, int) or i > 0:
                    dve.wait_ge(values_ready, i)
                for a, b in ((0, 2), (2, 3)):
                    src = ps_m[0:KEYS, a // 2, 0:(b - a) * DIM].rearrange("p (c d) -> p c d", c=b - a)
                    bias = value_bias[:, :].rearrange("p (c d) -> p c d", c=1)
                    if b - a > 1:
                        bias = bias.to_broadcast([KEYS, b - a, DIM])
                    dve.tensor_tensor(values_next[:, a:b, :], src, bias, ALU.add).then_inc(v_ready, 1)

            def query(i, p, h):
                dve.wait_ge(q_hi_ready, HEADS * i + h + 1)
                dve.tensor_tensor(q_lo[0:RANK, p, h, :], ps_q[0:RANK, 0:N], q_hi[0:RANK, p, h, :].bitcast(F32),
                                  ALU.subtract).then_inc(q_lo_ready, 1)

            def maximum(i, p, h, src=ps_s):
                dve.wait_ge(s_mm, HEADS * i + h + 1)
                dve.tensor_reduce(row_max[:, p, :, h], src[0:KEYS, 0:3 * N].rearrange("p (c m) -> p c m", c=3), AX,
                                  ALU.max).then_inc(max_ready, 1)

            def sums_inverse(i, g):
                n = GROUPS * i + g
                dve.wait_ge(ctx_turned, n + 1)
                src = ps_m[:, 0, 0:NTILES * GROUP * 32].rearrange("p (t b e) -> p t b e", t=NTILES, b=GROUP)
                for a, b, rows in PARTS:
                    dve.reciprocal(recip[0:rows, a:b, :, :], src[0:rows, a:b, :, HEAD_DIM:HEAD_DIM + 1]).then_inc(recip_ready, 1)

            def scale_products(i, p, g):
                n = GROUPS * i + g
                if not isinstance(n, int) or n >= 2:
                    dve.wait_ge(h2_ready, 2 * n - 2)
                dve.wait_ge(recip_ready, 2 * n + 2)
                src = ps_m[:, 0, 0:NTILES * GROUP * 32].rearrange("p (t b e) -> p t b e", t=NTILES, b=GROUP)
                for a, b, rows in PARTS:
                    dve.tensor_tensor(scaled[0:rows, (GROUPS * p + g) % 2, a:b, :, :], src[0:rows, a:b, :, 0:HEAD_DIM],
                                      recip[0:rows, a:b, :, :].to_broadcast([rows, b - a, GROUP, HEAD_DIM]),
                                      ALU.mult).then_inc(scaled_ready, 1)

            def post_stats(i, p):
                dve.wait_ge(h2_ready, 2 * GROUPS * (i + 1))
                for t in range(NTILES):
                    dve.bn_stats(stats2[:, t, :], h_back[:, p, t, :]).then_inc(dve_ln2, 1)

            def post_moments(i):
                dve.wait_ge(dve_ln2, 6 * i + 3)
                dve.nop(nofuse=True)
                for t in range(NTILES):
                    dve.bn_aggr(moments2[:, t, :], stats2[:, t, :]).then_inc(dve_ln2, 1)

            def post_norm(i, p):
                dve.wait_ge(refined2, 4 * i + 4)
                if not isinstance(i, int) or i >= 2:
                    dve.wait_ge(scattered[p], of_pair(i - 2, p, 16 * TOPK * NTILES))
                for t in range(NTILES):
                    dve.tensor_scalar(routed[:, p, 0, t, 0:DIM], h_back[:, p, t, :], moments2[:, t, 0:1], newton2[:, 2, t:t + 1],
                                      ALU.subtract, ALU.mult).then_inc(x2_ready, 1)

            def over_experts(ap):
                return ap.rearrange("p (t e) -> p t e", e=1).to_broadcast([128, NTILES, EXPERTS])

            def over_tiles(ap):
                return ap.rearrange("p (t e) -> p t e", t=1).to_broadcast([128, NTILES, EXPERTS])

            def picks_step(i, n):
                if n == 0:
                    dve.wait_ge(logit_mm, i + 1)
                    if not isinstance(i, int) or i > 0:
                        dve.wait_ge(placed, PLACED * i)
                    step = dve.tensor_copy(logits[:, :, :], ps_v[:, LOGIT_COL:LOGIT_COL + NTILES * EXPERTS]
                                           .rearrange("p (t e) -> p t e", t=NTILES))
                else:
                    dve.wait_ge(route, PICKED * i + n)
                k, of = (0, logits) if n < 7 else (1, rest)
                if n == 1:
                    step = dve.tensor_reduce(top[:, :], logits[:, :, :], AX, ALU.max)
                if n == 2:
                    step = dve.tensor_tensor(expo[:, :, :], logits[:, :, :], over_experts(top[:, :]), ALU.subtract)
                if n == 7:
                    step = dve.scalar_tensor_tensor(out=rest[:, :, :], in0=pick[:, :, 0, :], scalar=MASKED,
                                                    in1=logits[:, :, :], op0=ALU.mult, op1=ALU.add)
                if n == 8:
                    step = dve.tensor_reduce(top[:, :], rest[:, :, :], AX, ALU.max)
                if n in (3, 9):
                    step = dve.tensor_tensor(key[:, :, :], of[:, :, :], over_experts(top[:, :]), ALU.is_equal)
                if n in (4, 10):
                    step = dve.tensor_tensor(key[:, :, :], key[:, :, :], over_tiles(order[:, :]), ALU.mult)
                if n in (5, 11):
                    step = dve.tensor_reduce(total[:, :], key[:, :, :], AX, ALU.max)
                if n in (6, 12):
                    step = dve.tensor_tensor(pick[:, :, k, :], over_tiles(order[:, :]), over_experts(total[:, :]), ALU.is_equal)
                if n == 13:
                    step = dve.tensor_tensor(key[:, :, :], pick[:, :, 0, :], pick[:, :, 1, :], ALU.add)
                if n == 14:
                    step = dve.tensor_tensor(picked[:, :, :], key[:, :, :], over_experts(valid[:, :]), ALU.mult)
                step.then_inc(route, 1)

            def sum_inverse(i):
                dve.wait_ge(expo_ready, i + 1)
                dve.tensor_reduce(sums[:, :], expo[:, :, :], AX, ALU.add).then_inc(sums_ready, 1)
                dve.wait_ge(sums_ready, i + 1)
                dve.reciprocal(summed[:, :, 0], sums[:, :]).then_inc(inverse_ready, 1)

            def prologue():
                layernorm_stats(0, 0)
                layernorm_moments(0)
                dve.wait_ge(w_in, 16 * 8)
                dve.tensor_reduce(mean_mat[:, :], residual[:, :, :].rearrange("p h s -> p s h"), AX, ALU.add).then_inc(mat_step, 1)
                dve.wait_ge(mat_step, 1)
                dve.tensor_tensor(mean_mat[:, :], core_sb[:, :], mean_mat[:, :], ALU.subtract).then_inc(mat_step, 1)
                dve.wait_ge(mat_step, 2)
                dve.scalar_tensor_tensor(out=residual[:, :, :],
                                         in0=mean_mat[:, :].rearrange("p (a s) -> p a s", a=1).to_broadcast([128, HEADS, RANK]),
                                         scalar=1.0 / HEADS, in1=residual[:, :, :], op0=ALU.mult, op1=ALU.add).then_inc(mat_step, 1)
                for part in range(4):
                    layernorm_refine(0, part)
                layernorm(0, 0)
                dve.wait_ge(w_turned, 1)
                dve.tensor_copy(basisT[:, :, :, :], ps_m[0:HALF, 0, 0:2 * RANK].rearrange("p (k a r) -> p k a r", k=2, a=1)
                                .to_broadcast([HALF, 2, 2, RANK])).then_inc(w_ready, 1)
                dve.tensor_copy(routerT[:, :, :], ps_m[0:HALF, 0, 256:256 + 2 * EXPERTS].rearrange("p (k e) -> p k e", k=2)).then_inc(w_ready, 1)
                dve.tensor_copy(valueT[:, :, :], ps_m[0:HALF, 1, 0:2 * DIM].rearrange("p (k o) -> p k o", k=2)).then_inc(w_ready, 1)
                layernorm_stats(1, 1)
                layernorm_moments(1)
                dve.wait_ge(mat_step, 4)
                dve.tensor_tensor(mats_lo[:, :, :, :],
                                  residual[:, :, :].rearrange("p h (a s) -> p h a s", a=1).to_broadcast([128, HEADS, 2, RANK]),
                                  mats_hi[:, :, :, :].bitcast(F32), ALU.subtract).then_inc(mat_step, 1)
                for part in range(4):
                    layernorm_refine(1, part)
                layernorm(1, 1)
                for i in range(2):
                    latents(i, i)
                    value(i)
                dve.wait_ge(order_in, 10)
                dve.tensor_copy(order[:, :], order_int[:, 0:EXPERTS]).then_inc(order_ready, 1)
                dve.tensor_copy(goal[:, :, :, 0], order_int[:, EXPERTS:].rearrange("p (k t) -> p k t", k=TOPK)).then_inc(order_ready, 1)
                dve.memset(importance[:, :, :], 0.0).then_inc(order_ready, 1)
                dve.wait_ge(order_ready, 3)
                dve.tensor_scalar(places[:, :], order[:, :], float(-SPACE), float(EXPERTS * SPACE), ALU.mult, ALU.add).then_inc(order_ready, 1)
                query(0, 0, 0)
                for h in range(HEADS):
                    if h + 1 < HEADS:
                        query(0, 0, h + 1)
                    maximum(0, 0, h, FIRST_BANKS[h % 2])

            def body(i, p, front, prep, post, place, send):
                for h in range(HEADS):
                    if front:
                        query(i + 1, 1 - p, h)
                    if prep and h == 1:
                        layernorm_stats(i + 2, p)
                    if post and h in (0, 4):
                        sums_inverse(i - 1, 1 + h // GROUP)
                    if h == 9:
                        sums_inverse(i, 0)
                    if prep and h in (3, 4):
                        layernorm_refine(i + 2, 2 * (h - 3))
                    if post and h in (9, 10):
                        post_refine(i - 1, 2 * (h - 9))
                    if place and PICKS_AT <= h < PICKS_AT + 4:
                        picks_step(i - 2, 4 * (h - PICKS_AT))
                    if front:
                        maximum(i + 1, 1 - p, h)
                    if prep and h == 1:
                        layernorm_moments(i + 2)
                    if post and h in (0, 4):
                        scale_products(i - 1, 1 - p, 1 + h // GROUP)
                    if h == 9:
                        scale_products(i, p, 0)
                    if prep and h in (3, 4):
                        layernorm_refine(i + 2, 2 * (h - 3) + 1)
                    if place and PICKS_AT <= h < PICKS_AT + 4:
                        picks_step(i - 2, 4 * (h - PICKS_AT) + 1)
                    if prep and h == 4:
                        layernorm(i + 2, p)
                    if prep and h == VALUES_AT + 1:
                        value(i + 2)
                    if post and h == 6:
                        post_stats(i - 1, 1 - p)
                    if post and h == 7:
                        post_moments(i - 1)
                    if post and h in (9, 10):
                        post_refine(i - 1, 2 * (h - 9) + 1)
                    if prep and h == 11:
                        latents(i + 2, p)
                    if post and h == 11:
                        post_norm(i - 1, 1 - p)
                    if place and PICKS_AT <= h < PICKS_AT + 4:
                        picks_step(i - 2, 4 * (h - PICKS_AT) + 2)
                        if h < PICKS_AT + 3:
                            picks_step(i - 2, 4 * (h - PICKS_AT) + 3)
                    if place and h == 8:
                        sum_inverse(i - 2)

            def epilogue():
                for g in (1, 2):
                    sums_inverse(IMAGES - 1, g)
                    scale_products(IMAGES - 1, 1, g)
                post_stats(IMAGES - 1, 1)
                post_moments(IMAGES - 1)
                for part in range(4):
                    post_refine(IMAGES - 1, part)
                for n in range(PICKED):
                    picks_step(IMAGES - 2, n)
                sum_inverse(IMAGES - 2)
                post_norm(IMAGES - 1, 1)
                for n in range(PICKED):
                    picks_step(IMAGES - 1, n)
                sum_inverse(IMAGES - 1)

            run(dve, prologue, body, epilogue)

        @block.tensor
        def _(pe):
            pe.wait_ge(w_in, 16 * 8)
            pe.wait_ge(consts, 5)
            for k in range(2):
                half = slice(k * HALF, (k + 1) * HALF)
                pe.transpose(ps_m[0:HALF, 0, k * RANK:(k + 1) * RANK], basis_raw[:, half], ident[0:RANK, 0:RANK])
                for o in range(2):
                    pe.transpose(ps_m[0:HALF, 1, k * DIM + o * HALF:k * DIM + (o + 1) * HALF], value_raw[:, o, half],
                                      ident[0:HALF, 0:HALF])
                mm = pe.transpose(ps_m[0:HALF, 0, 256 + k * EXPERTS:256 + (k + 1) * EXPERTS], router_raw[:, half],
                                  ident[0:EXPERTS, 0:EXPERTS])
            mm.then_inc(w_turned, 1)
            pe.wait_ge(w_ready, 3)

            def transpose_x(i):
                pe.wait_ge(xn_ready, 3 * (i + 1))
                if not isinstance(i, int) or i > 0:
                    pe.wait_ge(xT_ready, i)
                for t, (at, rows) in enumerate(zip(TILE_AT, TILE_ROWS)):
                    for k in range(2):
                        mm = pe.transpose(ps_m[0:HALF, k, at:at + rows], xn[0:rows, t, k * HALF:(k + 1) * HALF],
                                          ident[0:rows, 0:rows])
                mm.then_inc(x_turned, 1)

            def latents(i):
                pe.wait_ge(xT_ready, i + 1)
                for k in range(2):
                    mm = pe.matmul(ps_q[:, 0:N], basisT[:, k, :, :].rearrange("p a r -> p (a r)"), xT[:, k, :],
                                   start=(k == 0), stop=(k == 1))
                mm.then_inc(lat_mm, 1)

            def value(i):
                for c in range(3):
                    for k in range(2):
                        mm = pe.matmul(ps_m[0:KEYS, c // 2, (c % 2) * DIM:(c % 2 + 1) * DIM], xT[:, k, c * KEYS:(c + 1) * KEYS],
                                       valueT[:, k, :], start=(k == 0), stop=(k == 1))
                mm.then_inc(v_mm, 1)

            def query(i, p, h):
                if h == 0:
                    pe.wait_ge(lat_lo, i + 1)
                    pe.wait_ge(lat_staged, i + 1)
                if not isinstance(i, int) or i > 0 or h > 0:
                    pe.wait_ge(q_lo_ready, HEADS * i + h)
                pe.matmul(ps_q[:, 0:N], mats_lo[:, h, :, :].rearrange("p a s -> p (a s)"), lat[:, p, :], start=True, stop=False)
                pe.matmul(ps_q[:, 0:N], mats_hi[:, h, :, :].rearrange("p a s -> p (a s)"), lat[:, p, :], start=False,
                          stop=True).then_inc(q_mm, 1)

            def scores_by_query(i, p, h, dst=None):
                pe.wait_ge(q_hi_ready, HEADS * i + h + 1)
                if dst is None:
                    pe.wait_ge(max_ready, HEADS * i + h)
                elif h >= 2:
                    pe.wait_ge(max_ready, h - 1)
                dst = ps_s if dst is None else dst
                for c, a, b in PIECES:
                    mm = pe.matmul(dst[0:KEYS, a:b], q_hi[:, p, h, c * KEYS:(c + 1) * KEYS], lat[:, p, a - c * N:b - c * N],
                                   start=True, stop=True)
                mm.then_inc(s_mm, 1)

            def maximum_rows(i, p):
                pe.wait_ge(max_ready, HEADS * (i + 1))
                for c in range(3):
                    mm = pe.transpose(ps_m[0:HEADS, 1, c * KEYS:(c + 1) * KEYS], row_max[:, p, c, :], ident[0:KEYS, 0:KEYS])
                mm.then_inc(max_turned, 1)

            def scores_by_key(i, p, h):
                if h == 0:
                    pe.wait_ge(one_row, 1)
                    pe.wait_ge(max_in[p], of_pair(i, p, 16))
                    pe.wait_ge(lat_one_ready, i + 1)
                    pe.wait_ge(q_lo_ready, HEADS * (i + 1))
                if not isinstance(i, int) or i > 0 or h > 0:
                    pe.wait_ge(probs_ready, HEADS * i + h)
                for c, a, b in PIECES:
                    keys = slice(c * KEYS, (c + 1) * KEYS)
                    queries = slice(a - c * N, b - c * N)
                    pe.matmul(ps_t[0:KEYS, a:b], lat_one[:, p, keys], q_lo[:, p, h, queries], start=True, stop=False)
                    mm = pe.matmul(ps_t[0:KEYS, a:b], lat[:, p, keys], q_hi[:, p, h, queries], start=False, stop=True)
                mm.then_inc(t_mm, 1)

            def products(i, p, g, place, chunks=range(3)):
                n = GROUPS * i + g
                if 0 in chunks:
                    if g == 0:
                        pe.wait_ge(values_ready, i + 1)
                    pe.wait_ge(probs_ready, HEADS * i + (g + 1) * GROUP)
                    if not isinstance(n, int) or n > 0:
                        pe.wait_ge(ctx_ready, n)
                    if place and g == 0:
                        pe.wait_ge(route, PICKED * (i - 2) + LOGITS_READ)
                    if place and g == 1:
                        pe.wait_ge(ranks_ready, i - 1)
                slot = (GROUPS * p + g) % 2
                for c in chunks:
                    for b in range(GROUP):
                        mm = pe.matmul(ps_v[32 * b:32 * (b + 1), 0:N], values[:, p, c, g * GROUP + b, :],
                                       probs[:, slot * GROUP + b, c * N:(c + 1) * N], start=(c == 0), stop=(c == 2))
                if 2 in chunks:
                    mm.then_inc(pv_mm, 1)

            def turn_products(i, g):
                n = GROUPS * i + g
                pe.wait_ge(ctx_ready, n + 1)
                for t, (at, rows) in enumerate(zip(TILE_AT, TILE_ROWS)):
                    mm = pe.transpose(ps_m[0:rows, 0, t * GROUP * 32:(t + 1) * GROUP * 32], ctx_sb[:, at:at + rows], ident[:, :])
                mm.then_inc(ctx_turned, 1)

            def post_turn(i, p):
                pe.wait_ge(x2_ready, 3 * (i + 1))
                for t, (at, rows) in enumerate(zip(TILE_AT, TILE_ROWS)):
                    for k in range(2):
                        mm = pe.transpose(ps_m[0:HALF, k, at:at + rows], routed[0:rows, p, 0, t, k * HALF:(k + 1) * HALF],
                                          ident[0:rows, 0:rows])
                mm.then_inc(x2_turned, 1)

            def post_logits(i):
                pe.wait_ge(x2T_ready, i + 1)
                for t, at in enumerate(TILE_AT):
                    for k in range(2):
                        mm = pe.matmul(ps_v[:, LOGIT_COL + t * EXPERTS:LOGIT_COL + (t + 1) * EXPERTS], x2T[:, k, at:at + 128], routerT[:, k, :],
                                       start=(k == 0), stop=(k == 1))
                mm.then_inc(logit_mm, 1)

            def post_ranks(i):
                pe.wait_ge(route, PICKED * (i + 1))
                for t in range(NTILES):
                    for of in range(t + 1):
                        pe.matmul(ps_v[:, RANK_COL + t * EXPERTS:RANK_COL + (t + 1) * EXPERTS], (before if of == t else all_ones)[:, :],
                                  picked[:, of, :], start=(of == 0), stop=(of == t))
                for t in range(NTILES):
                    mm = pe.matmul(ps_v[:, RANK_COL + NTILES * EXPERTS:RANK_COL + (NTILES + 1) * EXPERTS], all_ones[:, :], picked[:, t, :], start=(t == 0), stop=(t == 2))
                mm.then_inc(rank_mm, 1)

            def prologue():
                for i in range(2):
                    if i:
                        pe.wait_ge(v_ready, 2 * i)
                    transpose_x(i)
                    if i:
                        pe.wait_ge(lat_staged, i)
                    latents(i)
                    value(i)
                pe.wait_ge(lat_lo, 2)
                pe.wait_ge(mat_step, 5)
                query(0, 0, 0)
                for h in range(HEADS):
                    if h + 1 < HEADS:
                        query(0, 0, h + 1)
                    scores_by_query(0, 0, h, FIRST_BANKS[h % 2])
                pe.wait_ge(v_ready, 4)
                maximum_rows(0, 0)

            def body(i, p, front, prep, post, place, send):
                for h in range(HEADS):
                    if post and h == 0:
                        pe.wait_ge(v_ready, 2 * (i + 2) if front else 2 * IMAGES)
                        maximum_rows(i, p)
                    if front:
                        if prep and h == LATENTS_AT + 1:
                            pe.wait_ge(lat_staged, i + 3)
                        query(i + 1, 1 - p, h)
                    if post and h == 0:
                        if front:
                            scores_by_query(i + 1, 1 - p, 0)
                        products(i - 1, 1 - p, 2, False, [1, 2])
                    scores_by_key(i, p, h)
                    if h % GROUP < 3 and h >= GROUP:
                        products(i, p, h // GROUP - 1, place, [h % GROUP])
                    if front and not (post and h == 0):
                        scores_by_query(i + 1, 1 - p, h)
                    if place and h == POST_TURN:
                        pe.wait_ge(scaled_ready, 2 * (GROUPS * i - 1))
                        pe.wait_ge(max_rows_ready, i + 1)
                        post_turn(i - 2, p)
                    if place and h == POST_LOGITS:
                        pe.wait_ge(ctx_ready, GROUPS * i)
                        post_logits(i - 2)
                    if post and h == 3:
                        if place:
                            pe.wait_ge(x2T_ready, i - 1)
                        pe.wait_ge(scaled_ready, 2 * (GROUPS * i - 1))
                        pe.wait_ge(max_rows_ready, i + 1)
                        turn_products(i - 1, 2)
                    if prep and h == TURN_AT:
                        if post:
                            pe.wait_ge(scaled_ready, 2 * GROUPS * i)
                        pe.wait_ge(max_rows_ready, i + 1)
                        transpose_x(i + 2)
                    if prep and h == LATENTS_AT:
                        pe.wait_ge(q_lo_ready, HEADS * (i + 1) + h + 1)
                        latents(i + 2)
                    if prep and h == VALUES_AT:
                        pe.wait_ge(xT_ready, i + 3)
                        value(i + 2)
                    if h == 8:
                        if prep:
                            pe.wait_ge(v_ready, 2 * (i + 3))
                        if post:
                            pe.wait_ge(scaled_ready, 2 * GROUPS * i)
                        pe.wait_ge(max_rows_ready, i + 1)
                        turn_products(i, 0)
                    if h == 11:
                        pe.wait_ge(scaled_ready, 2 * (GROUPS * i + 1))
                        turn_products(i, 1)
                    if place and h == POST_RANKS:
                        pe.wait_ge(ctx_ready, GROUPS * i + 1)
                        post_ranks(i - 2)
                products(i, p, 2, False, [0])

            def epilogue():
                products(IMAGES - 1, 1, 2, False, [1, 2])
                pe.wait_ge(scaled_ready, 2 * (GROUPS * IMAGES - 1))
                turn_products(IMAGES - 1, 2)
                for i in range(IMAGES - 2, IMAGES):
                    pe.wait_ge(scaled_ready, 2 * GROUPS * IMAGES)
                    pe.wait_ge(x2T_ready, i)
                    post_turn(i, i % 2)
                    pe.wait_ge(ctx_ready, GROUPS * IMAGES)
                    pe.wait_ge(ranks_ready, i)
                    post_logits(i)
                    post_ranks(i)

            run(pe, prologue, body, epilogue)


RESULTS = TOPK * TOKENS
INNER = HIDDEN // 128
PAIR = 8
DEPTH = 4
AHEAD = 8
assert BLOCKS % AHEAD == 0


def experts(nc, w1, w2, rows_dram, results_dram, places, w1_raw, w1_in):
    with ExitStack() as ctx:
        def sb(name, shape, dt=F32):
            return ctx.enter_context(nc.sbuf_tensor(name, shape, dt))

        def psum(name, shape, dt=F32):
            return ctx.enter_context(nc.psum_tensor(name, shape, dt))

        def sem(name):
            return ctx.enter_context(nc.semaphore(name))

        ident = sb("identB", [128, 128])
        w1_hi = sb("w1_hi", [HALF, 2, EXPERTS, HIDDEN], F32R)
        w1_lo = sb("w1_lo", [HALF, 2, EXPERTS, HIDDEN], F32R)
        w2_both = sb("w2_both", [128, EXPERTS, INNER, 2, DIM], F32R)
        w2_raw = sb("w2_raw", [HALF, 2, EXPERTS, HIDDEN])

        int_consts = sb("int_consts", [128, EXPERTS + 1], I32)
        step_int = sb("step_int", [128, BLOCKS], I32)
        row_no = sb("row_no", [128, 1])
        first_row = sb("first_row", [128, EXPERTS])
        step_no = sb("step_no", [128, BLOCKS])
        empty = sb("empty", [128, ROW])
        pad_place = sb("pad_place", [128, EXPERTS])
        pad_int = sb("pad_int", [128, EXPERTS], I32)
        tiles_int = sb("tiles_int", [128, EXPERTS], I32)
        tiles = sb("tiles", [128, EXPERTS])
        ends = sb("ends", [128, 2, EXPERTS])
        jump = sb("jump", [128, EXPERTS])
        past = sb("past", [128, BLOCKS, EXPERTS])
        table = sb("table", [128, 2, BLOCKS])
        table_int = sb("table_int", [128, 2, BLOCKS], I32)

        rows = sb("rows", [128, AHEAD, ROW])
        goal_int = sb("goal_int", [128, AHEAD, 1], I32)
        x_hi = sb("x_hi", [HALF, 2, 2, 128], F32R)
        x_lo = sb("x_lo", [HALF, 2, 2, 128], F32R)
        hidden = sb("hidden", [128, 2, HIDDEN])
        hT_hi = sb("hT_hi", [128, 2, HIDDEN], F32R)
        hT_lo = sb("hT_lo", [128, 2, HIDDEN], F32R)
        result = sb("result", [128, AHEAD, DIM])

        ps_x = psum("ps_x", [HALF, 2, BANK])
        ps_h = psum("ps_h", [128, 2, BANK])
        ps_t = psum("ps_tB", [128, 2, BANK])
        ps_y = psum("ps_y", [128, 2, BANK])

        consts, const_step = sem("constsB"), sem("const_stepB")
        w2_in = [sem(f"w2_in{i}") for i in range(EXPERTS // PAIR)]
        w_turned = sem("w_turnedB")
        w_hi_ready = sem("w_hi_readyB")
        w_lo_ready = sem("w_lo_readyB")
        table_step = sem("table_step")
        pads_ready = sem("pads_ready")
        table_ready = sem("table_ready")
        padded = sem("padded")
        spare_in = sem("spare_in")
        rows_in = [sem(f"rows_in{i}") for i in range(AHEAD)]
        goal_ready = sem("goal_ready")
        x_turned = sem("x_turnedB")
        x_hi_ready = sem("x_hi_readyB")
        x_lo_ready = sem("x_lo_readyB")
        h_mm = sem("h_mm")
        h_ready = sem("h_ready")
        h_turned = sem("h_turned")
        hT_hi_ready = sem("hT_hi_ready")
        hT_lo_ready = sem("hT_lo_ready")
        y_mm = sem("y_mm")
        y_ready = sem("y_ready")
        stored = [sem(f"stored{i}") for i in range(AHEAD)]

        block = ctx.enter_context(nc.Block())

        GROUPS_W = 4 * EXPERTS

        def group_of(n):
            return n < 2 * EXPERTS, (n % (2 * EXPERTS)) // 2, n % 2

        @block.sync
        def _(sp):
            for e in range(0, EXPERTS, PAIR):
                for k in range(2):
                    sp.dma_start(w2_raw[:, k, e:e + PAIR, :],
                                 w2[e:e + PAIR, k * HALF:(k + 1) * HALF, :].rearrange("e p i -> p e i")).then_inc(w2_in[e // PAIR], 16)
            sp.wait_ge(consts, 4)
            for k in range(SPARE):
                at = EXPERTS * SPACE + k * 128
                sp.dma_start(rows_dram[at:at + 128, :], empty[:, :]).then_inc(spare_in, 16)
            sp.wait_ge(table_ready, 1)
            sp.wait_ge(spare_in, 16 * SPARE)
            sp.wait_ge(padded, 16 * EXPERTS)

            def load(j, u):
                row = sp.value_load(table_int[0:1, 1, bass.ds(j, 1)], min_val=0, max_val=EXPERTS * SPACE + (SPARE - 1) * 128)
                sp.dma_start(rows[:, u, :], rows_dram[bass.ds(row, 128), :]).then_inc(rows_in[u], 16)

            for j in range(AHEAD):
                load(j, j)
            with sp.Fori(0, BLOCKS // AHEAD - 1) as it:
                for u in range(AHEAD):
                    j = it * AHEAD + u
                    sp.wait_ge(x_turned, j + 1)
                    sp.wait_ge(goal_ready, j + 1)
                    load(j + AHEAD, u)

        @block.gpsimd
        def _(pool):
            pool.memset(ident[:, :], 0.0).then_inc(const_step, 1)
            pool.memset(empty[:, 0:DIM], 0.0).then_inc(consts, 1)
            pool.iota(int_consts[:, 0:EXPERTS], [[SPACE // 128, EXPERTS]], base=0, channel_multiplier=0).then_inc(consts, 1)
            pool.iota(int_consts[:, EXPERTS:EXPERTS + 1], [[0, 1]], base=0, channel_multiplier=1).then_inc(consts, 1)
            pool.iota(step_int[:, :], [[1, BLOCKS]], base=0, channel_multiplier=0).then_inc(const_step, 1)
            pool.wait_ge(const_step, 2)
            pool.affine_select(out=ident[:, :], in_=ident[:, :], compare_op=ALU.not_equal, fill=1.0,
                               base=0, pattern=[[-1, 128]], channel_multiplier=1).then_inc(const_step, 1)
            pool.wait_ge(pads_ready, 1)
            for e in range(EXPERTS):
                pool.indirect_dma_start(rows_dram[:, :], bass.IndirectOffsetOnAxis(pad_int[:, e:e + 1], 0),
                                        empty[:, :], None).then_inc(padded, 16)

            def store(j, u):
                pool.wait_ge(goal_ready, j + 1)
                pool.wait_ge(y_ready, j + 1)
                pool.nop(nofuse=True)
                pool.indirect_dma_start(results_dram[:, :], bass.IndirectOffsetOnAxis(goal_int[:, u, :], 0),
                                        result[:, u, :], None, bounds_check=RESULTS - 1,
                                        oob_is_err=False).then_inc(stored[u], 16)

            with pool.Fori(0, BLOCKS // AHEAD) as it:
                for u in range(AHEAD):
                    store(it * AHEAD + u, u)
            for u in range(AHEAD):
                pool.wait_ge(stored[u], 16 * (BLOCKS // AHEAD))

        def split(n):
            is_w1, e, half = group_of(n)
            if is_w1:
                bank = (ps_x, ps_t[0:HALF])[n // 2 % 2]
                return (w1_hi[:, half, e, :], w1_lo[:, half, e, :], bank[:, n % 2, 0:HIDDEN])
            chunks = slice(half * 2, half * 2 + 2)
            bank = (ps_h, ps_y)[n // 2 % 2][:, n % 2, 0:2 * DIM].rearrange("p (c d) -> p c d", c=2)
            return w2_both[:, e, chunks, 0, :], w2_both[:, e, chunks, 1, :], bank

        def of_slot(j, u, each):
            return (j // AHEAD) * each if isinstance(j, int) else (j - u) * (each // AHEAD)

        def pipeline(engine, first, middle, last):
            first()
            for j in range(1, AHEAD + 1):
                middle(j, j % AHEAD)
            with engine.Fori(0, BLOCKS // AHEAD - 2) as it:
                for k in range(1, AHEAD + 1):
                    middle(it * AHEAD + AHEAD + k, k % AHEAD)
            for j in range(BLOCKS - AHEAD + 1, BLOCKS - 1):
                middle(j, j % AHEAD)
            last(BLOCKS - 1, (BLOCKS - 1) % AHEAD)

        @block.scalar
        def _(act):
            act.preload_act_table(ACT.Silu)
            for n in range(GROUPS_W):
                hi, _, src = split(n)
                act.wait_ge(w_turned, n + 1)
                act.activation(hi, src, ACT.Copy).then_inc(w_hi_ready, 1)

            def x_half(j, u):
                act.wait_ge(x_turned, j + 1)
                act.activation(x_hi[:, u % 2, :, :], ps_x[:, u % 2, 0:256].rearrange("p (k t) -> p k t", k=2), ACT.Copy).then_inc(x_hi_ready, 1)

            def silu(j, u):
                act.wait_ge(h_mm, j + 1)
                act.activation(hidden[:, u % 2, :], ps_h[:, u % 2, :], ACT.Silu).then_inc(h_ready, 1)

            def h_half(j, u):
                act.wait_ge(h_turned, j + 1)
                act.activation(hT_hi[:, u % 2, :], ps_t[:, u % 2, :], ACT.Copy).then_inc(hT_hi_ready, 1)

            def first():
                x_half(0, 0)
                silu(0, 0)
                x_half(1, 1)

            def middle(j, u):
                h_half(j - 1, u - 1)
                silu(j, u)
                x_half(j + 1, u + 1)

            def last(j, u):
                h_half(j - 1, u - 1)
                silu(j, u)
                h_half(j, u)

            pipeline(act, first, middle, last)

        @block.vector
        def _(dve):
            dve.wait_ge(consts, 3)
            dve.wait_ge(const_step, 2)
            n = 0

            def step(instruction):
                nonlocal n
                n += 1
                instruction.then_inc(table_step, 1)
                dve.wait_ge(table_step, n)

            dve.tensor_scalar(first_row[:, :], int_consts[:, 0:EXPERTS], 128.0, None, ALU.mult).then_inc(table_step, 1)
            dve.tensor_copy(step_no[:, :], step_int[:, :]).then_inc(table_step, 1)
            n = 2
            step(dve.tensor_copy(row_no[:, :], int_consts[:, EXPERTS:EXPERTS + 1]))
            dve.tensor_scalar(empty[:, DIM:ROW], row_no[:, :], float(RESULTS), None, ALU.add).then_inc(consts, 1)
            step(dve.tensor_scalar(pad_place[:, :], places[:, :], row_no[:, 0:1], None, ALU.add))
            dve.tensor_copy(pad_int[:, :], pad_place[:, :]).then_inc(pads_ready, 1)
            step(dve.tensor_tensor(tiles[:, :], places[:, :], first_row[:, :], ALU.subtract))
            step(dve.tensor_scalar(tiles[:, :], tiles[:, :], 127.0, None, ALU.add))
            step(dve.tensor_copy(tiles_int[:, :], tiles[:, :]))
            step(dve.tensor_single_scalar(tiles_int[:, :], tiles_int[:, :], 7, ALU.arith_shift_right))
            step(dve.tensor_copy(tiles[:, :], tiles_int[:, :]))
            step(dve.tensor_copy(ends[:, 0, :], tiles[:, :]))
            for k, by in enumerate((1, 2, 4)):
                a, b = k % 2, 1 - k % 2
                step(dve.tensor_copy(ends[:, b, 0:by], ends[:, a, 0:by]))
                step(dve.tensor_tensor(ends[:, b, by:EXPERTS], ends[:, a, by:EXPERTS], ends[:, a, 0:EXPERTS - by], ALU.add))
            step(dve.tensor_scalar(jump[:, :], tiles[:, :], -128.0, float(SPACE), ALU.mult, ALU.add))
            step(dve.tensor_tensor(past[:, :, :], step_no[:, :].rearrange("p (j e) -> p j e", e=1).to_broadcast([128, BLOCKS, EXPERTS]),
                                   ends[:, 1, :].rearrange("p (j e) -> p j e", j=1).to_broadcast([128, BLOCKS, EXPERTS]), ALU.is_ge))
            step(dve.tensor_reduce(table[:, 0, :], past[:, :, :], AX, ALU.add))
            step(dve.tensor_scalar(table[:, 0, :], table[:, 0, :], float(EXPERTS - 1), None, ALU.min))
            step(dve.tensor_tensor(past[:, :, :], past[:, :, :],
                                   jump[:, :].rearrange("p (j e) -> p j e", j=1).to_broadcast([128, BLOCKS, EXPERTS]), ALU.mult))
            step(dve.tensor_reduce(table[:, 1, :], past[:, :, :], AX, ALU.add))
            step(dve.scalar_tensor_tensor(out=table[:, 1, :], in0=step_no[:, :], scalar=128.0, in1=table[:, 1, :],
                                          op0=ALU.mult, op1=ALU.add))
            dve.tensor_copy(table_int[:, :, :], table[:, :, :]).then_inc(table_ready, 1)

            for g in range(GROUPS_W):
                hi, lo, src = split(g)
                dve.wait_ge(w_hi_ready, g + 1)
                dve.tensor_tensor(lo, src, hi.bitcast(F32), ALU.subtract).then_inc(w_lo_ready, 1)

            def x_half(j, u):
                dve.wait_ge(x_hi_ready, j + 1)
                dve.tensor_tensor(x_lo[:, u % 2, :, :], ps_x[:, u % 2, 0:256].rearrange("p (k t) -> p k t", k=2),
                                  x_hi[:, u % 2, :, :].bitcast(F32), ALU.subtract).then_inc(x_lo_ready, 1)

            def goal(j, u):
                if not isinstance(j, int) or j >= AHEAD:
                    dve.wait_ge(stored[u], of_slot(j, u, 16))
                dve.wait_ge(rows_in[u], of_slot(j, u, 16) + 16)
                dve.tensor_copy(goal_int[:, u, :], rows[:, u, DIM:ROW]).then_inc(goal_ready, 1)

            def h_half(j, u):
                dve.wait_ge(hT_hi_ready, j + 1)
                dve.tensor_tensor(hT_lo[:, u % 2, :], ps_t[:, u % 2, :], hT_hi[:, u % 2, :].bitcast(F32), ALU.subtract).then_inc(hT_lo_ready, 1)

            def finish(j, u):
                dve.wait_ge(y_mm, j + 1)
                dve.tensor_reduce(result[:, u, :], ps_y[:, u % 2, 0:2 * DIM].rearrange("p (k d) -> p d k", k=2), AX, ALU.add).then_inc(y_ready, 1)

            def first():
                goal(0, 0)
                x_half(0, 0)
                goal(1, 1)
                x_half(1, 1)

            def middle(j, u):
                h_half(j - 1, u - 1)
                goal(j + 1, (u + 1) % AHEAD)
                x_half(j + 1, u + 1)
                finish(j - 1, (u - 1) % AHEAD)

            def last(j, u):
                h_half(j - 1, u - 1)
                finish(j - 1, u - 1)
                h_half(j, u)
                finish(j, u)

            pipeline(dve, first, middle, last)

        @block.tensor
        def _(pe):
            pe.wait_ge(const_step, 3)
            for n in range(GROUPS_W):
                is_w1, e, half = group_of(n)
                if n == 0:
                    pe.wait_ge(w1_in, 16)
                if not is_w1 and e % PAIR == 0 and half == 0:
                    pe.wait_ge(w2_in[e // PAIR], 32)
                if n >= 4:
                    pe.wait_ge(w_lo_ready, n - 3)
                dst = split(n)[2]
                for c in range(INNER):
                    if is_w1:
                        mm = pe.transpose(dst[:, c * 128:(c + 1) * 128], w1_raw[:, e * INNER + c, half * HALF:(half + 1) * HALF], ident[:, :])
                    else:
                        chunk = half * 2 + c // 2
                        mm = pe.transpose(dst[:, c // 2, c % 2 * HALF:(c % 2 + 1) * HALF], w2_raw[:, c % 2, e, chunk * 128:(chunk + 1) * 128],
                                          ident[0:HALF, 0:HALF])
                mm.then_inc(w_turned, 1)
            pe.wait_ge(w_lo_ready, GROUPS_W)
            pe.wait_ge(table_ready, 1)

            def used(j):
                return not isinstance(j, int) or j >= 2

            def turn_x(j, u):
                if used(j):
                    pe.wait_ge(x_lo_ready, j - 1)
                pe.wait_ge(rows_in[u], of_slot(j, u, 16) + 16)
                for k in range(2):
                    mm = pe.transpose(ps_x[:, u % 2, k * 128:(k + 1) * 128], rows[:, u, k * HALF:(k + 1) * HALF], ident[:, :])
                mm.then_inc(x_turned, 1)

            held = [None, None]

            def expert_of(j):
                return pe.value_load(table_int[0:1, 0, bass.ds(j, 1)], min_val=0, max_val=EXPERTS - 1)

            def first_layer(j, u, e):
                if used(j):
                    pe.wait_ge(h_ready, j - 1)
                pe.wait_ge(x_lo_ready, j + 1)
                mm = None
                v = u % 2
                for k in range(2):
                    hi, lo = (w[:, k, bass.ds(e, 1), :].rearrange("p e i -> p (e i)") for w in (w1_hi, w1_lo))
                    pe.matmul(ps_h[:, v, :], x_lo[:, v, k, :], hi, start=(k == 0), stop=False)
                    pe.matmul(ps_h[:, v, :], x_hi[:, v, k, :], lo, start=False, stop=False)
                    mm = pe.matmul(ps_h[:, v, :], x_hi[:, v, k, :], hi, start=False, stop=(k == 1))
                mm.then_inc(h_mm, 1)

            def turn_h(j, u):
                if used(j):
                    pe.wait_ge(hT_lo_ready, j - 1)
                pe.wait_ge(h_ready, j + 1)
                for c in range(INNER):
                    mm = pe.transpose(ps_t[:, u % 2, c * 128:(c + 1) * 128], hidden[:, u % 2, c * 128:(c + 1) * 128], ident[:, :])
                mm.then_inc(h_turned, 1)

            def second_layer(j, u, e):
                if used(j):
                    pe.wait_ge(y_ready, j - 1)
                pe.wait_ge(hT_lo_ready, j + 1)
                v = u % 2
                for c in range(INNER):
                    both = w2_both[:, bass.ds(e, 1), c, :, :].rearrange("p e k d -> p (e k d)")
                    hi = w2_both[:, bass.ds(e, 1), c, 0, :].rearrange("p e d -> p (e d)")
                    at = slice(c * 128, (c + 1) * 128)
                    pe.matmul(ps_y[:, v, 0:2 * DIM], hT_hi[:, v, at], both, start=(c == 0), stop=False)
                    mm = pe.matmul(ps_y[:, v, 0:DIM], hT_lo[:, v, at], hi, start=False, stop=(c == INNER - 1))
                mm.then_inc(y_mm, 1)

            def first():
                turn_x(0, 0)
                first_layer(0, 0, expert_of(0))
                turn_x(1, 1)

            def middle(j, u, more=True):
                turn_h(j - 1, u - 1)
                if u == 1:
                    held[1] = expert_of(j)
                e_before, e = held
                first_layer(j, u, e)
                if more:
                    turn_x(j + 1, (u + 1) % AHEAD)
                if u == 1:
                    e_before = expert_of(j - 1)
                held[:] = e, expert_of(j + 1) if more and u != 0 else None
                second_layer(j - 1, u - 1, e_before)

            def last(j, u):
                middle(j, u, False)
                turn_h(j, u)
                second_layer(j, u, held[0])

            pipeline(pe, first, middle, last)


def combine(nc, h2_dram, results_dram, picks, pick_probs, importance, out):
    with ExitStack() as ctx:
        def sb(name, shape, dt=F32):
            return ctx.enter_context(nc.sbuf_tensor(name, shape, dt))

        def sem(name):
            return ctx.enter_context(nc.semaphore(name))

        ones = sb("onesC", [128, 128])
        running = sb("running", [128, EXPERTS])
        TILES = IMAGES * NTILES * TOPK
        of_pick = sb("of_pickC", [128, TILES, EXPERTS])
        balance = sb("balance", [128, TILES])
        share = sb("share", [128, TILES // TOPK, TOPK])
        whole = sb("whole", [128, TILES // TOPK, 1])
        weight = sb("weight", [128, IMAGES, NTILES, TOPK])
        now = sb("now", [128, DEPTH, NTILES, TOPK])
        base = sb("base", [128, DEPTH, NTILES, DIM])
        part = sb("part", [128, DEPTH, TOPK, NTILES, DIM])
        ps = ctx.enter_context(nc.psum_tensor("ps_c", [128, BANK], F32))

        ones_ready, summed, step = sem("ones_ready"), sem("summedC"), sem("stepC")
        loaded = [sem(f"loaded{i}") for i in range(DEPTH)]
        base_in = [sem(f"base_in{i}") for i in range(DEPTH)]
        now_ready = sem("now_ready")
        added = sem("added")
        out_stored = [sem(f"out_stored{i}") for i in range(DEPTH)]
        PARTS = [(0, 2, PTILE), (2, 3, TEXT)]

        block = ctx.enter_context(nc.Block())

        @block.tensor
        def _(pe):
            pe.wait_ge(ones_ready, 1)
            for t, rows in enumerate(TILE_ROWS):
                mm = pe.matmul(ps[:, 0:EXPERTS], ones[0:rows, :], importance[0:rows, t, :], start=(t == 0), stop=(t == 2))
            mm.then_inc(summed, 1)

        of_picks = results_dram.rearrange("(k n) d -> n k d", k=TOPK)

        @block.sync
        def _(sp):
            def load(i, u):
                at = i * N
                for t, rows in enumerate(TILE_ROWS):
                    sp.dma_start(part[0:rows, u, :, t, :], of_picks[bass.ds(at + TILE_AT[t], rows), :, :]).then_inc(loaded[u], 16)

            for i in range(DEPTH):
                load(i, i)
            with sp.Fori(0, IMAGES // DEPTH - 1) as it:
                for u in range(DEPTH):
                    i = it * DEPTH + u
                    sp.wait_ge(out_stored[u], 48 * (it + 1))
                    sp.nop(nofuse=True)
                    load(i + DEPTH, u)

        @block.gpsimd
        def _(pool):
            def load(i, u):
                at = i * N
                pool.dma_start(base[0:PTILE, u, 0:2, :], h2_dram[bass.ds(at, 2 * PTILE), :].rearrange("(t p) d -> p t d", t=2)).then_inc(base_in[u], 16)
                pool.dma_start(base[:, u, 2, :], h2_dram[bass.ds(at + 2 * PTILE, TEXT), :]).then_inc(base_in[u], 16)

            for i in range(DEPTH):
                load(i, i)
            with pool.Fori(0, IMAGES // DEPTH - 1) as it:
                for u in range(DEPTH):
                    pool.wait_ge(out_stored[u], 48 * (it + 1))
                    pool.nop(nofuse=True)
                    load(it * DEPTH + u + DEPTH, u)

        @block.scalar
        def _(act):
            def store(i, u):
                act.wait_ge(added, 4 * (i + 1))
                patches = out[bass.ds(i, 1), 0:2 * PTILE, :].rearrange("a (g w) d -> w (a g) d", w=GRID)
                for t in range(2):
                    act.dma_start(patches[t * TILE_COLS:(t + 1) * TILE_COLS, :, :], base[0:PTILE, u, t, :]).then_inc(out_stored[u], 16)
                act.dma_start(out[bass.ds(i, 1), 2 * PTILE:N, :].rearrange("a p d -> (a p) d"), base[:, u, 2, :]).then_inc(out_stored[u], 16)

            with act.Fori(0, IMAGES // DEPTH) as it:
                for u in range(DEPTH):
                    store(it * DEPTH + u, u)
            for u in range(DEPTH):
                act.wait_ge(out_stored[u], 48 * IMAGES // DEPTH)

        @block.vector
        def _(dve):
            n = 0

            def chained(instruction):
                nonlocal n
                n += 1
                instruction.then_inc(step, 1)
                dve.wait_ge(step, n)

            dve.memset(ones[:, :], 1.0).then_inc(ones_ready, 1)
            dve.wait_ge(summed, 1)
            chained(dve.tensor_scalar(running[:, :], ps[:, 0:EXPERTS], 1.0, 1.0 - 0.9, ALU.subtract, ALU.mult))
            chained(dve.tensor_scalar(running[:, :], running[:, :], 1.0, 0.01, ALU.add, ALU.add))
            chained(dve.tensor_tensor(of_pick[:, :, :], picks[:, :, :, :, :].rearrange("p i t k e -> p (i t k) e"),
                                      running[:, :].rearrange("p (t e) -> p t e", t=1).to_broadcast([128, TILES, EXPERTS]), ALU.mult))
            chained(dve.tensor_reduce(balance[:, :], of_pick[:, :, :], AX, ALU.add))
            chained(dve.reciprocal(balance[:, :], balance[:, :]))
            flat = share[:, :, :].rearrange("p n k -> p (n k)")
            chained(dve.tensor_tensor(flat, pick_probs[:, :, :, :].rearrange("p i t k -> p (i t k)"), balance[:, :], ALU.mult))
            chained(dve.tensor_reduce(whole[:, :, 0], share[:, :, :], AX, ALU.add))
            chained(dve.reciprocal(whole[:, :, :], whole[:, :, :]))
            chained(dve.tensor_tensor(weight[:, :, :, :].rearrange("p i t k -> p (i t) k"), share[:, :, :],
                                      whole[:, :, :].to_broadcast([128, TILES // TOPK, TOPK]), ALU.mult))

            def add(i, u, it):
                dve.tensor_copy(now[:, u, :, :], weight[:, bass.ds(i, 1), :, :].rearrange("p i t k -> p (i t) k")).then_inc(now_ready, 1)
                dve.wait_ge(loaded[u], 48 * (it + 1))
                dve.wait_ge(base_in[u], 32 * (it + 1))
                dve.nop(nofuse=True)
                dve.wait_ge(now_ready, i + 1)
                dve.nop(nofuse=True)
                for k in range(TOPK):
                    if k:
                        dve.wait_ge(added, 4 * i + 2)
                    for a, b, rows in PARTS:
                        for t in range(a, b):
                            mm = dve.scalar_tensor_tensor(out=base[0:rows, u, t, :], in0=part[0:rows, u, k, t, :],
                                                          scalar=now[0:rows, u, t, k:k + 1], in1=base[0:rows, u, t, :],
                                                          op0=ALU.mult, op1=ALU.add)
                        mm.then_inc(added, 1)

            with dve.Fori(0, IMAGES // DEPTH) as it:
                for u in range(DEPTH):
                    add(it * DEPTH + u, u, it)


def program(nc, x, txt, gamma, beta, W, b, basis_w, core, head_residual, value_w, value_b, router_w, w1, w2, out):
    h_dram = nc.dram_tensor("h", (IMAGES, N, DIM), F32, kind="Internal").ap()
    h2_dram = nc.dram_tensor("h2", (TOKENS, DIM), F32, kind="Internal").ap()
    rows_dram = nc.dram_tensor("rows_by_expert", (EXPERTS * SPACE + SPARE * 128, ROW), F32, kind="Internal").ap()
    results_dram = nc.dram_tensor("results", (RESULTS, DIM), F32, kind="Internal").ap()
    with ExitStack() as ctx:
        def sb(name, shape):
            return ctx.enter_context(nc.sbuf_tensor(name, shape, F32))

        picks = sb("picks", [128, IMAGES, NTILES, TOPK, EXPERTS])
        pick_probs = sb("pick_probs", [128, IMAGES, NTILES, TOPK])
        places = sb("places", [128, EXPERTS])
        importance = sb("importance", [128, NTILES, EXPERTS])
        w1_raw = sb("w1_raw", [128, EXPERTS * INNER, DIM])
        w1_in = ctx.enter_context(nc.semaphore("w1_in"))
        tokenize(nc, x, gamma, beta, W, b, h_dram)
        attention(nc, txt, basis_w, core, head_residual, value_w, value_b, router_w, h_dram,
                  h2_dram.rearrange("(i n) d -> i n d", i=IMAGES), rows_dram, (picks, pick_probs, places, importance), w1, w1_raw, w1_in)
        experts(nc, w1, w2, rows_dram, results_dram, places, w1_raw, w1_in)
        combine(nc, h2_dram, results_dram, picks, pick_probs, importance, out)


_INS = ["x", "txt", "L0_tok_gamma", "L0_tok_beta", "L0_tok_W", "L0_tok_b", "L0_attn_basis_w", "L0_attn_core",
        "L0_attn_head_residual", "L0_attn_value_w", "L0_attn_value_b", "L0_ffn_router_w", "L0_ffn_w1", "L0_ffn_w2"]


def kernel(**inputs):
    import numpy as _np
    import concourse.bacc as _bacc
    from concourse import mybir as _mybir
    from concourse.bass_utils import run_bass_kernel_spmd as _run

    nc = _bacc.Bacc("TRN2", target_bir_lowering=False, num_devices=1)
    arrays, args = {}, []
    for name in _INS:
        a = _np.ascontiguousarray(inputs[name])
        arrays[f"in_{name}"] = a
        args.append(nc.dram_tensor(f"in_{name}", a.shape, _mybir.dt.from_np(a.dtype), kind="ExternalInput").ap())
    out = nc.dram_tensor("out_dram", (IMAGES, N, DIM), _mybir.dt.float32, kind="ExternalOutput").ap()
    program(nc, *args, out)
    r = _run(nc, [arrays], core_ids=[0])
    return r.results[0]["out_dram"]
```
